# Optimizing a Trainium2 kernel written in Bass

```python
import numpy as np
import jax
import jax.numpy as jnp

def _softmax(x, axis=-1):
    return jax.nn.softmax(x, axis=axis)

def _gelu(x):
    return jax.nn.gelu(x, approximate=True)

def _silu(x):
    return jax.nn.silu(x)

def _sigmoid(x):
    return jax.nn.sigmoid(x)

def _layernorm(x, axis=-1, eps=1e-05):
    m = jnp.mean(x, axis=axis, keepdims=True)
    v = jnp.var(x, axis=axis, keepdims=True)
    return (x - m) / jnp.sqrt(v + eps)

def _scatter_add(tgt, idx, src, axis=0):
    return tgt.at[idx].add(src)

def _segment_sum(src, seg, n):
    return jax.ops.segment_sum(src, seg, n)
kernel_name = 'mk_gnn_ffn_d1_gnn_r8_6036a8'

def setup_inputs(seed: int=0):
    np.random.seed(seed)
    _w = jnp.asarray

    def _rec_inputs():
        import jax
        import jax.numpy as jnp
        _gk = jax.random.key(seed)
        x = -0.0003713 + 1 * jax.random.normal(jax.random.fold_in(_gk, 1), (6250, 256), jnp.float32)
        src = jax.random.randint(jax.random.fold_in(_gk, 2), (100000,), 0, 6250, jnp.int32)
        dst = jnp.minimum((6250 * jax.random.uniform(jax.random.fold_in(_gk, 3), (100000,)) ** 2.0).astype(jnp.int32), 49999)
        _o = jnp.argsort(dst, stable=True)
        src = src[_o]
        dst = dst[_o]
        return (x, src, dst)
    x, src, dst = _rec_inputs()

    def _L0_gnn_setup():
        import jax, jax.numpy as jnp
        import numpy as np
        N_NODES = 6250
        N_EDGES = 40000
        IN_DIM = 256
        HID = 256
        N_LAYERS = 4
        EPS = 1e-05
        key = jax.random.key(seed)
        ks = jax.random.split(key, 12)
        s = 0.05
        x = jax.random.normal(ks[0], (N_NODES, IN_DIM), jnp.float32)
        rows = jax.random.randint(ks[1], (N_EDGES,), 0, N_NODES, dtype=jnp.int32)
        cols = jax.random.randint(ks[2], (N_EDGES,), 0, N_NODES, dtype=jnp.int32)
        W_in = jax.random.normal(ks[3], (IN_DIM, HID), jnp.float32) * s
        b_in = jnp.zeros((HID,), jnp.float32)
        Wl = jax.random.normal(ks[4], (N_LAYERS, HID, HID), jnp.float32) * s
        bl = jnp.zeros((N_LAYERS, HID), jnp.float32)
        Wg = jax.random.normal(ks[5], (N_LAYERS, HID, HID), jnp.float32) * s
        bg = jnp.zeros((N_LAYERS, HID), jnp.float32)
        gamma = jnp.ones((N_LAYERS, HID), jnp.float32)
        beta = jnp.zeros((N_LAYERS, HID), jnp.float32)
        return {'x': x, 'rows': rows, 'cols': cols, 'W_in': W_in, 'b_in': b_in, 'Wl': Wl, 'bl': bl, 'Wg': Wg, 'bg': bg, 'gamma': gamma, 'beta': beta}
    _L0_gnn_all = _L0_gnn_setup()
    _L0_gnn_in = {k: v for k, v in _L0_gnn_all.items() if k in ('W_in', 'b_in', 'Wl', 'bl', 'Wg', 'bg', 'gamma', 'beta')}
    del _L0_gnn_all

    def _L0_ffn_setup():
        import jax, jax.numpy as jnp
        import numpy as np
        B, N, D = (16, 512, 256)
        NUM_EXPERTS, TOP_K, HEADS = (4, 2, 4)
        N_EDGES = 131072
        LN_EPS = 1e-05

        def _layernorm(x, g, b):
            mu = x.mean(-1, keepdims=True)
            var = ((x - mu) ** 2).mean(-1, keepdims=True)
            return (x - mu) * jax.lax.rsqrt(var + LN_EPS) * g + b

        def _forward(x, edge_index, W_gat, att_src, att_dst, b_gat, ln_gamma, ln_beta, W1, b1, W2, b2):
            Bc, Nc, Dc = x.shape
            M = Bc * Nc
            x_flat = x.reshape(M, Dc)
            h = (x_flat @ W_gat).reshape(M, HEADS, NUM_EXPERTS)
            loops = jnp.arange(M, dtype=edge_index.dtype)
            src = jnp.concatenate([edge_index[0], loops])
            dst = jnp.concatenate([edge_index[1], loops])
            a_src = (h * att_src).sum(-1)
            a_dst = (h * att_dst).sum(-1)
            e = jax.nn.leaky_relu(a_src[src] + a_dst[dst], negative_slope=0.2)
            e_max = jax.ops.segment_max(e, dst, num_segments=M)
            ee = jnp.exp(e - e_max[dst])
            denom = jax.ops.segment_sum(ee, dst, num_segments=M)
            alpha = ee / (denom[dst] + 1e-16)
            msg = h[src] * alpha[:, :, None]
            agg = jax.ops.segment_sum(msg, dst, num_segments=M).reshape(M, HEADS * NUM_EXPERTS) + b_gat
            scores = _layernorm(agg, ln_gamma, ln_beta).reshape(M, HEADS, NUM_EXPERTS).mean(1)
            scores = scores.reshape(Bc, Nc, NUM_EXPERTS)
            topk_s, topk_i = jax.lax.top_k(scores, TOP_K)
            w = jax.nn.softmax(topk_s, axis=-1)
            out = jnp.zeros_like(x)
            for ei in range(NUM_EXPERTS):
                g = jnp.where(topk_i == ei, w, 0.0).sum(-1)
                hh = jax.nn.gelu(x @ W1[ei] + b1[ei], approximate=False)
                out = out + g[..., None] * (hh @ W2[ei] + b2[ei])
            return out
        key = jax.random.key(seed)
        ks = jax.random.split(key, 8)
        s = 0.05
        return {'x': jax.random.normal(ks[0], (B, N, D), jnp.float32), 'W_gat': jax.random.normal(ks[1], (D, HEADS * NUM_EXPERTS), jnp.float32) * s, 'att_src': jax.random.normal(ks[2], (HEADS, NUM_EXPERTS), jnp.float32) * s, 'att_dst': jax.random.normal(ks[3], (HEADS, NUM_EXPERTS), jnp.float32) * s, 'b_gat': jnp.zeros((HEADS * NUM_EXPERTS,), jnp.float32), 'ln_gamma': jnp.ones((HEADS * NUM_EXPERTS,), jnp.float32), 'ln_beta': jnp.zeros((HEADS * NUM_EXPERTS,), jnp.float32), 'W1': jax.random.normal(ks[4], (NUM_EXPERTS, D, 2 * D), jnp.float32) * s, 'b1': jnp.zeros((NUM_EXPERTS, 2 * D), jnp.float32), 'W2': jax.random.normal(ks[5], (NUM_EXPERTS, 2 * D, D), jnp.float32) * s, 'b2': jnp.zeros((NUM_EXPERTS, D), jnp.float32), 'edge_index': jax.random.randint(ks[6], (2, N_EDGES), 0, B * N, jnp.int32)}
    _L0_ffn_all = _L0_ffn_setup()
    _L0_ffn_in = {k: v for k, v in _L0_ffn_all.items() if k in ('W_gat', 'att_src', 'att_dst', 'b_gat', 'ln_gamma', 'ln_beta', 'W1', 'b1', 'W2', 'b2', 'edge_index')}
    del _L0_ffn_all
    return {'x': x, 'src': src, 'dst': dst, 'L0_gnn_W_in': _L0_gnn_in['W_in'], 'L0_gnn_b_in': _L0_gnn_in['b_in'], 'L0_gnn_Wl': _L0_gnn_in['Wl'], 'L0_gnn_bl': _L0_gnn_in['bl'], 'L0_gnn_Wg': _L0_gnn_in['Wg'], 'L0_gnn_bg': _L0_gnn_in['bg'], 'L0_gnn_gamma': _L0_gnn_in['gamma'], 'L0_gnn_beta': _L0_gnn_in['beta'], 'L0_ffn_W_gat': _L0_ffn_in['W_gat'], 'L0_ffn_att_src': _L0_ffn_in['att_src'], 'L0_ffn_att_dst': _L0_ffn_in['att_dst'], 'L0_ffn_b_gat': _L0_ffn_in['b_gat'], 'L0_ffn_ln_gamma': _L0_ffn_in['ln_gamma'], 'L0_ffn_ln_beta': _L0_ffn_in['ln_beta'], 'L0_ffn_W1': _L0_ffn_in['W1'], 'L0_ffn_b1': _L0_ffn_in['b1'], 'L0_ffn_W2': _L0_ffn_in['W2'], 'L0_ffn_b2': _L0_ffn_in['b2'], 'L0_ffn_edge_index': _L0_ffn_in['edge_index']}

def reference(x, src, dst, L0_gnn_W_in, L0_gnn_b_in, L0_gnn_Wl, L0_gnn_bl, L0_gnn_Wg, L0_gnn_bg, L0_gnn_gamma, L0_gnn_beta, L0_ffn_W_gat, L0_ffn_att_src, L0_ffn_att_dst, L0_ffn_b_gat, L0_ffn_ln_gamma, L0_ffn_ln_beta, L0_ffn_W1, L0_ffn_b1, L0_ffn_W2, L0_ffn_b2, L0_ffn_edge_index):
    import jax
    import jax.numpy as jnp

    def _L0_gnn_ref(x, rows, cols, W_in, b_in, Wl, bl, Wg, bg, gamma, beta):
        import jax, jax.numpy as jnp
        import numpy as np
        N_NODES = 6250
        N_EDGES = 40000
        IN_DIM = 256
        HID = 256
        N_LAYERS = 4
        EPS = 1e-05
        n = x.shape[0]
        deg = jax.ops.segment_sum(jnp.ones(rows.shape, x.dtype), rows, num_segments=n) + 1.0
        dinv = jax.lax.rsqrt(deg)[:, None]
        h = x @ W_in + b_in
        for l in range(Wl.shape[0]):
            h_scaled = h * dinv
            msg = jax.ops.segment_sum(h_scaled[cols], rows, num_segments=n) * dinv
            global_ctx = jnp.mean(h, axis=0) @ Wg[l] + bg[l]
            z = jax.nn.relu((h + msg) @ Wl[l] + bl[l] + global_ctx)
            mu = jnp.mean(z, axis=-1, keepdims=True)
            var = jnp.var(z, axis=-1, keepdims=True)
            h = (z - mu) * jax.lax.rsqrt(var + EPS) * gamma[l] + beta[l]
        return h

    def _L0_ffn_ref(x, W_gat, att_src, att_dst, b_gat, ln_gamma, ln_beta, W1, b1, W2, b2, edge_index):
        import jax, jax.numpy as jnp
        import numpy as np
        B, N, D = (16, 512, 256)
        NUM_EXPERTS, TOP_K, HEADS = (4, 2, 4)
        N_EDGES = 131072
        LN_EPS = 1e-05

        def _layernorm(x, g, b):
            mu = x.mean(-1, keepdims=True)
            var = ((x - mu) ** 2).mean(-1, keepdims=True)
            return (x - mu) * jax.lax.rsqrt(var + LN_EPS) * g + b

        def _forward(x, edge_index, W_gat, att_src, att_dst, b_gat, ln_gamma, ln_beta, W1, b1, W2, b2):
            Bc, Nc, Dc = x.shape
            M = Bc * Nc
            x_flat = x.reshape(M, Dc)
            h = (x_flat @ W_gat).reshape(M, HEADS, NUM_EXPERTS)
            loops = jnp.arange(M, dtype=edge_index.dtype)
            src = jnp.concatenate([edge_index[0], loops])
            dst = jnp.concatenate([edge_index[1], loops])
            a_src = (h * att_src).sum(-1)
            a_dst = (h * att_dst).sum(-1)
            e = jax.nn.leaky_relu(a_src[src] + a_dst[dst], negative_slope=0.2)
            e_max = jax.ops.segment_max(e, dst, num_segments=M)
            ee = jnp.exp(e - e_max[dst])
            denom = jax.ops.segment_sum(ee, dst, num_segments=M)
            alpha = ee / (denom[dst] + 1e-16)
            msg = h[src] * alpha[:, :, None]
            agg = jax.ops.segment_sum(msg, dst, num_segments=M).reshape(M, HEADS * NUM_EXPERTS) + b_gat
            scores = _layernorm(agg, ln_gamma, ln_beta).reshape(M, HEADS, NUM_EXPERTS).mean(1)
            scores = scores.reshape(Bc, Nc, NUM_EXPERTS)
            topk_s, topk_i = jax.lax.top_k(scores, TOP_K)
            w = jax.nn.softmax(topk_s, axis=-1)
            out = jnp.zeros_like(x)
            for ei in range(NUM_EXPERTS):
                g = jnp.where(topk_i == ei, w, 0.0).sum(-1)
                hh = jax.nn.gelu(x @ W1[ei] + b1[ei], approximate=False)
                out = out + g[..., None] * (hh @ W2[ei] + b2[ei])
            return out
        return _forward(x, edge_index, W_gat, att_src, att_dst, b_gat, ln_gamma, ln_beta, W1, b1, W2, b2)
    x = x + _L0_gnn_ref(_layernorm(x, axis=-1), src, dst, L0_gnn_W_in, L0_gnn_b_in, L0_gnn_Wl, L0_gnn_bl, L0_gnn_Wg, L0_gnn_bg, L0_gnn_gamma, L0_gnn_beta)
    x = x + _L0_ffn_ref(_layernorm(x, axis=-1)[None], L0_ffn_W_gat, L0_ffn_att_src, L0_ffn_att_dst, L0_ffn_b_gat, L0_ffn_ln_gamma, L0_ffn_ln_beta, L0_ffn_W1, L0_ffn_b1, L0_ffn_W2, L0_ffn_b2, L0_ffn_edge_index)[0]
    return x

_drawn_inputs = setup_inputs


def setup_inputs(seed=0):
    import zlib

    import numpy as np

    out = dict(_drawn_inputs(seed))
    spreads = {'L0_gnn_b_in': (0.0, 0.1),
     'L0_gnn_bl': (0.0, 0.1),
     'L0_gnn_bg': (0.0, 0.1),
     'L0_gnn_gamma': (1.0, 0.2),
     'L0_gnn_beta': (0.0, 0.1),
     'L0_ffn_b_gat': (0.0, 0.1),
     'L0_ffn_ln_gamma': (1.0, 0.2),
     'L0_ffn_ln_beta': (0.0, 0.1),
     'L0_ffn_b1': (0.0, 0.1),
     'L0_ffn_b2': (0.0, 0.1)}
    factors = {'L0_ffn_att_src': 3.112, 'L0_ffn_att_dst': 5.708}
    for name, (base, spread) in spreads.items():
        noise = np.random.default_rng([zlib.crc32(name.encode()), seed]).standard_normal(out[name].shape)
        drawn = base * np.exp(spread * noise) if base else spread * noise
        out[name] = jnp.asarray(drawn.astype(out[name].dtype))
    for name, factor in factors.items():
        out[name] = (out[name] * factor).astype(out[name].dtype)
    return out
```

```python
import concourse.bass as bass
from concourse import mybir
from contextlib import ExitStack

F32 = mybir.dt.float32
BF16 = mybir.dt.bfloat16
I32 = mybir.dt.int32
ALU = mybir.AluOpType
ACT = mybir.ActivationFunctionType
AX = mybir.AxisListType

P = 128
N = 6250
NB = (N + P - 1) // P
NP = NB * P
LAST = N - (NB - 1) * P
D = 256
DC = D // P
LAYERS = 4
GRP = 7
NG = NB // GRP
EXPERTS, HEADS, TOPK = 4, 4, 2
HE = HEADS * EXPERTS
HID = 512
HM = HID // P
ROW = HE + HEADS
EPS = 1e-5
NEG = -1e30
E_GNN = 100000
E_GAT = 131072
T_GNN = 784
T_GAT = E_GAT // P
CH = 8
LO_SHIFT = 13
NO_NODE = P
OUTSIDE = 8191
FAR = float(1 << 20)


def tiles_bound(edges, multiple):
    n = edges // P + NB
    return -(-n // multiple) * multiple


M_GNN = tiles_bound(E_GNN, 2 * CH)
M_GAT = tiles_bound(E_GAT, 2 * CH)


class Chain:

    def __init__(self, eng, sem):
        self.eng, self.sem, self.base, self.n = eng, sem, 0, 0

    def link(self, ins):
        ins.then_inc(self.sem, 1)
        self.n += 1
        self.eng.wait_ge(self.sem, self.base + self.n)

    def enter(self, it, per):
        self.start, self.per, self.first = self.base + self.n, per, True
        self.base, self.n = self.start + it * per, 0

    def leave(self, count):
        assert self.n == self.per, (self.n, self.per)
        self.base, self.n = self.start + count * self.per, 0


def semaphores(nc, c, tag):
    used = []

    def make(name):
        used.append(nc.alloc_semaphore(tag + name))
        return used[-1]

    def clear():
        nc.clear_and_free_semaphores(used)
        nc.all_engine_barrier()

    c.callback(clear)
    return make


def settle(ve, t):
    ve.memset(t.spare[0:1, 3:4], 0.0)


def settle_gpsimd(gp, t, settled, before):
    gp.wait_ge(settled, before)
    gp.tensor_tensor(t.spare[0:1, 0:1], t.spare[0:1, 1:2], t.spare[0:1, 2:3], ALU.add).then_inc(settled, 1)


class Tensors:
    pass


def build_constants(nc, t):
    with ExitStack() as c:
        const_step = semaphores(nc, c, "const_")("step")
        block = c.enter_context(nc.Block())

        @block.gpsimd
        def _(gp):
            c = Chain(gp, const_step)
            gp.iota(t.iota_f[:, :], pattern=[[1, P]], base=0, channel_multiplier=0,
                    allow_small_or_imprecise_dtypes=True)
            gp.iota(t.iota_b[:, :], pattern=[[1, P]], base=0, channel_multiplier=0,
                    allow_small_or_imprecise_dtypes=True)
            gp.memset(t.ident_f[:, :], 0.0)
            gp.memset(t.neg_ident_b[:, :], 0.0)
            gp.memset(t.ones_f[:, :], 1.0)
            gp.memset(t.spare[:, :], 0.0)
            gp.memset(t.ones_b[:, :], 1.0)
            gp.memset(t.lower_b[:, :], 1.0)
            c.link(gp.memset(t.valid[:, :], 1.0))
            gp.affine_select(out=t.ident_f[:, :], in_=t.ident_f[:, :], compare_op=ALU.not_equal, fill=1.0,
                             base=0, pattern=[[-1, P]], channel_multiplier=1)
            gp.affine_select(out=t.neg_ident_b[:, :], in_=t.neg_ident_b[:, :], compare_op=ALU.not_equal,
                             fill=NEG, base=0, pattern=[[-1, P]], channel_multiplier=1)
            gp.affine_select(out=t.lower_b[:, :], in_=t.lower_b[:, :], compare_op=ALU.is_gt, fill=0.0,
                             base=0, pattern=[[1, P]], channel_multiplier=-1)
            c.link(gp.affine_select(out=t.valid[:, 1:2], in_=t.valid[:, 1:2], compare_op=ALU.is_gt, fill=0.0,
                                    base=LAST, pattern=[[0, 1]], channel_multiplier=-1))
            c.link(gp.memset(t.zero_b[:, :], 0.0))


def sort_edges(nc, t, tag, load_edges, loads, T, M, slots_dram, gather_idx, node_of_slot, block_of_tile, dinv):
    NCH = T // CH
    with ExitStack() as c:
        sb = lambda n, s, d=F32: c.enter_context(nc.sbuf_tensor(tag + n, s, d))
        pb = lambda n, s, d=F32: c.enter_context(nc.psum_tensor(tag + n, s, d))
        sem = semaphores(nc, c, tag)
        key = sb("key", [P, T], I32)
        val = sb("val", [P, T], I32)
        tmp_i = sb("tmp_i", [P, T], I32)
        lo_b = sb("lo_b", [P, T], BF16)
        hi_b = sb("hi_b", [P, T], BF16)
        packed = sb("packed", [P, T])
        dropped = sb("dropped", [P, T])
        in_block = sb("in_block", [P, T, NB], BF16)
        at_lane = sb("at_lane", [P, 2, CH, P], BF16)
        fill = sb("fill", [P, M])
        counts = sb("counts", [P, NB])
        counts_i = sb("counts_i", [P, NB], I32)
        ntiles = sb("ntiles", [P, NB])
        zeros = sb("zeros", [P, NB])
        end_tile = sb("end_tile", [P, NB])
        end_col = sb("end_col", [NB, 1])
        ended = sb("ended", [NB, M])
        tile_iota = sb("tile_iota", [NB, M])
        run = sb("run", [P, NB])
        ranked = sb("ranked", [P, CH, NB])
        picked = sb("picked", [P, CH, NB])
        pos = sb("pos", [P, CH])
        pos_ring = sb("pos_ring", [P, 2, CH], I32)
        pay_ring = sb("pay_ring", [P, 2, CH])
        G = next(g for g in range(-(-M // P), M + 1) if M % g == 0)
        RT = M // G
        BANK = 512 // RT
        rows = sb("rows", [RT, G, P])
        slot_i = sb("slot_i", [P, M], I32)
        rank_ps = pb("rank_ps", [P, 2, 512])
        total_ps = pb("total_ps", [P, 2, 512])
        hist_ps = pb("hist_ps", [P, 512])
        misc_ps = pb("misc_ps", [P, 3, 512])

        keys_clear = sem("keys_clear")
        edges_in = sem("edges_in")
        dv = sem("dv")
        hi_ready = sem("hi_ready")
        fill_ready = sem("fill_ready")
        filled = sem("filled")
        iota_ready = sem("iota_ready")
        blocks_ready = sem("blocks_ready")
        lane_ready = [sem(f"lane_ready{k}") for k in range(2)]
        lane_used = [sem(f"lane_used{k}") for k in range(2)]
        counted = sem("counted")
        hist_done = sem("hist_done")
        counts_ready = sem("counts_ready")
        end_row_ready = sem("end_row_ready")
        end_col_done = sem("end_col_done")
        ended_ready = sem("ended_ready")
        ended_done = sem("ended_done")
        rank_done = [sem(f"rank_done{k}") for k in range(2)]
        rank_used = [sem(f"rank_used{k}") for k in range(2)]
        pos_ready = [sem(f"pos_ready{k}") for k in range(2)]
        pay_ready = [sem(f"pay_ready{k}") for k in range(2)]
        packed_ready = sem("packed_ready")
        scattered = [sem(f"scattered{k}") for k in range(2)]
        rows_in = sem("rows_in")
        settled = sem("settled")
        turned = sem("turned")
        sqrt_in = sem("sqrt_in")
        sqrt_out = sem("sqrt_out")
        turned_ps = lambda g: [rank_ps, total_ps][g // BANK // 2][:, g // BANK % 2, g % BANK * RT:(g % BANK + 1) * RT]
        block = c.enter_context(nc.Block())

        @block.sync
        def _(sp):
            sp.wait_ge(keys_clear, 2)
            load_edges(sp, key, val, edges_in)
            sp.wait_ge(fill_ready, 1)
            sp.dma_start(slots_dram.rearrange("(p m) o -> p (m o)", p=P), fill[:, :]).then_inc(filled, 16)
            for k in range(2):
                sp.wait_ge(scattered[k], 16 * CH * NCH // 2)
            sp.dma_start(rows[:, :, :], slots_dram.rearrange("(g r s) o -> r g (s o)", g=G, s=P)).then_inc(rows_in, 16)

        @block.gpsimd
        def _(gp):
            gp.iota(tile_iota[:, :], pattern=[[1, M]], base=0, channel_multiplier=0,
                    allow_small_or_imprecise_dtypes=True).then_inc(iota_ready, 1)
            gp.wait_ge(filled, 16)
            with gp.Fori(0, NCH // 2) as i:
                for k in range(2):
                    gp.wait_ge(pos_ready[k], i + 1)
                    gp.wait_ge(pay_ready[k], i + 1)
                    settle_gpsimd(gp, t, settled, i * 2 + k)
                    for j in range(CH):
                        gp.indirect_dma_start(
                            out=slots_dram, out_offset=bass.IndirectOffsetOnAxis(ap=pos_ring[:, k, j:j + 1], axis=0),
                            in_=pay_ring[:, k, j:j + 1], in_offset=None,
                            bounds_check=M * P - 1, oob_is_err=False).then_inc(scattered[k], 16)

        @block.scalar
        def _(act):
            if dinv is not None:
                act.wait_ge(sqrt_in, 1)
                nc.scalar.activation(dinv[:, :], dinv[:, :], ACT.Sqrt).then_inc(sqrt_out, 1)
            act.wait_ge(packed_ready, 1)
            with act.Fori(0, NCH // 2) as i:
                for k in range(2):
                    act.wait_ge(scattered[k], i * (16 * CH))
                    nc.scalar.activation(pay_ring[:, k, :], packed[:, bass.ds(i * (2 * CH) + k * CH, CH)],
                                         ACT.Copy).then_inc(pay_ready[k], 1)

        @block.tensor
        def _(pe):
            pe.wait_ge(hi_ready, 1)
            if dinv is not None:
                nc.tensor.matmul(hist_ps[:, 0:NB], t.zero_b[:, :], in_block[:, 0, :], start=True, stop=False)
                with pe.Fori(0, NCH // 2) as i:
                    for k in range(2):
                        pe.wait_ge(lane_ready[k], i + 1)
                        for j in range(CH):
                            last = nc.tensor.matmul(hist_ps[:, 0:NB], at_lane[:, k, j, :],
                                                    in_block[:, bass.ds(i * (2 * CH) + (k * CH + j), 1), :].rearrange("p a b -> p (a b)"),
                                                    start=False, stop=False)
                        last.then_inc(lane_used[k], 1)
                nc.tensor.matmul(hist_ps[:, 0:NB], t.zero_b[:, :], in_block[:, 0, :], start=False, stop=True).then_inc(counted, 1)
            else:
                pe.wait_ge(blocks_ready, NCH)
                nc.tensor.matmul(hist_ps[:, 0:NB], t.zero_b[:, :], in_block[:, 0, :], start=True, stop=False)
                with pe.Fori(0, NCH) as i:
                    for j in range(CH):
                        nc.tensor.matmul(hist_ps[:, 0:NB], t.ones_b[:, :],
                                                in_block[:, bass.ds(i * CH + j, 1), :].rearrange("p a b -> p (a b)"),
                                                start=False, stop=False)
                nc.tensor.matmul(hist_ps[:, 0:NB], t.zero_b[:, :], in_block[:, 0, :], start=False, stop=True).then_inc(counted, 1)
            if dinv is not None:
                pe.wait_ge(counts_ready, 1)
                nc.tensor.matmul(misc_ps[:, 0, 0:NB], t.ones_f[:, :], counts[:, :], start=True, stop=True).then_inc(hist_done, 1)
            pe.wait_ge(end_row_ready, 1)
            nc.tensor.matmul(misc_ps[0:NB, 1, 0:1], end_tile[0:1, :], t.ones_f[0:1, 0:1], start=True, stop=True).then_inc(end_col_done, 1)
            pe.wait_ge(ended_ready, 1)
            for h in range(0, M, 512):
                w = min(512, M - h)
                last = nc.tensor.matmul(misc_ps[0:1, h // 512, 0:w], t.ones_f[0:NB, 0:1], ended[:, h:h + w], start=True, stop=True)
            last.then_inc(ended_done, 1)
            with pe.Fori(0, NCH // 2) as i:
                for k in range(2):
                    pe.wait_ge(rank_used[k], i)
                    c0 = i * (2 * CH) + k * CH
                    one = lambda j: in_block[:, bass.ds(c0 + j, 1), :]
                    nc.tensor.matmul(rank_ps[:, k, 0:CH * NB].rearrange("p (a b) -> p a b", b=NB), t.lower_b[:, :],
                                     in_block[:, bass.ds(c0, CH), :], start=True, stop=False)
                    for j in range(CH - 1):
                        nc.tensor.matmul(rank_ps[:, k, (j + 1) * NB:CH * NB].rearrange("p (a b) -> p a b", b=NB),
                                         t.ones_b[:, :], one(j).to_broadcast([P, CH - 1 - j, NB]),
                                         start=False, stop=(j == CH - 2))
                    for j in range(CH):
                        last = nc.tensor.matmul(total_ps[:, k, 0:NB], t.ones_b[:, :], one(j).rearrange("p a b -> p (a b)"),
                                                start=(j == 0), stop=(j == CH - 1))
                    last.then_inc(rank_done[k], 1)
            pe.wait_ge(rows_in, 16)
            for g in range(G):
                last = nc.tensor.transpose(turned_ps(g), rows[:, g, :], t.ident_f[0:RT, 0:RT])
            last.then_inc(turned, 1)

        @block.vector
        def _(ve):
            v = nc.vector
            ch = Chain(ve, dv)
            v.memset(key[:, :], OUTSIDE).then_inc(keys_clear, 1)
            v.memset(val[:, :], 0).then_inc(keys_clear, 1)
            ch.link(v.memset(zeros[:, :], 0.0))
            v.memset(gather_idx[:, :], 0)
            v.memset(node_of_slot[:, :], float(NO_NODE))
            v.memset(fill[:, :], float(NO_NODE << LO_SHIFT)).then_inc(fill_ready, 1)
            ve.wait_ge(edges_in, 16 * loads)
            ch.link(v.tensor_scalar(val[:, :], val[:, :], float(N - 1), None, ALU.min))
            ch.link(v.tensor_scalar(tmp_i[:, :], key[:, :], 7, None, ALU.arith_shift_right))
            ch.link(v.tensor_copy(hi_b[:, :], tmp_i[:, :]))
            ch.link(v.tensor_scalar(tmp_i[:, :], key[:, :], P - 1, None, ALU.bitwise_and))
            ch.link(v.tensor_copy(lo_b[:, :], tmp_i[:, :]))
            v.scalar_tensor_tensor(packed[:, :], tmp_i[:, :], float(1 << LO_SHIFT), val[:, :],
                                   ALU.mult, ALU.add).then_inc(packed_ready, 1)
            ch.link(v.tensor_scalar(dropped[:, :], key[:, :], float(NP), FAR, ALU.is_ge, ALU.mult))
            with ve.Fori(0, NCH) as i:
                v.tensor_tensor(in_block[:, bass.ds(i * CH, CH), :],
                                hi_b[:, bass.ds(i * CH, CH)].unsqueeze(2).to_broadcast([P, CH, NB]),
                                t.iota_b[:, 0:NB].unsqueeze(1).to_broadcast([P, CH, NB]), ALU.is_equal).then_inc(blocks_ready, 1)
            ve.wait_ge(blocks_ready, NCH)
            v.memset(ranked[:, 0, 0:1], 0.0).then_inc(hi_ready, 1)
            if dinv is not None:
                with ve.Fori(0, NCH // 2) as i:
                    for k in range(2):
                        ve.wait_ge(lane_used[k], i)
                        v.tensor_tensor(at_lane[:, k, :, :],
                                        lo_b[:, bass.ds(i * (2 * CH) + k * CH, CH)].unsqueeze(2).to_broadcast([P, CH, P]),
                                        t.iota_b[:, :].unsqueeze(1).to_broadcast([P, CH, P]), ALU.is_equal).then_inc(lane_ready[k], 1)
                ve.wait_ge(counted, 1)
                v.tensor_copy(counts[:, :], hist_ps[:, 0:NB]).then_inc(counts_ready, 1)
                ve.wait_ge(counts_ready, 1)
                v.tensor_scalar(dinv[:, :], counts[:, :], 1.0, None, ALU.add).then_inc(sqrt_in, 1)
                ve.wait_ge(hist_done, 1)
                ch.link(v.tensor_copy(counts_i[:, :], misc_ps[:, 0, 0:NB]))
                ve.wait_ge(sqrt_out, 1)
                ch.link(v.reciprocal(dinv[:, :], dinv[:, :]))
                ch.link(v.tensor_scalar(counts[:, :], counts[:, :], 1.0, -0.5, ALU.add, ALU.mult))
                ch.link(v.tensor_tensor(counts[:, :], counts[:, :], dinv[:, :], ALU.mult))
                ch.link(v.tensor_tensor(counts[:, :], counts[:, :], dinv[:, :], ALU.mult))
                ch.link(v.scalar_tensor_tensor(dinv[:, :], counts[:, :], 1.5, dinv[:, :], ALU.add, ALU.mult))
            else:
                ve.wait_ge(counted, 1)
                ch.link(v.tensor_copy(counts_i[:, :], hist_ps[:, 0:NB]))
            ch.link(v.tensor_scalar(counts_i[:, :], counts_i[:, :], float(P - 1), None, ALU.add))
            ch.link(v.tensor_scalar(counts_i[:, :], counts_i[:, :], 7, None, ALU.arith_shift_right))
            ch.link(v.tensor_copy(ntiles[:, :], counts_i[:, :]))
            v.tensor_tensor_scan(end_tile[:, :], ntiles[:, :], zeros[:, :], 0.0, ALU.add, ALU.add).then_inc(end_row_ready, 1)
            ve.wait_ge(end_row_ready, 1)
            ch.link(v.tensor_tensor(run[:, :], end_tile[:, :], ntiles[:, :], ALU.subtract))
            ch.link(v.tensor_scalar(run[:, :], run[:, :], float(P), None, ALU.mult))
            ve.wait_ge(end_col_done, 1)
            ch.link(v.tensor_copy(end_col[:, :], misc_ps[0:NB, 1, 0:1]))
            ve.wait_ge(iota_ready, 1)
            v.tensor_scalar(ended[:, :], tile_iota[:, :], end_col[:, 0:1], None, ALU.is_ge).then_inc(ended_ready, 1)
            ve.wait_ge(ended_done, 1)
            for h in range(0, M, 512):
                w = min(512, M - h)
                last = v.tensor_scalar(block_of_tile[:, h:h + w], misc_ps[0:1, h // 512, 0:w], float(NB - 1), None, ALU.min)
            ch.link(last)
            with ve.Fori(0, NCH // 2) as i:
                ch.enter(i, 6)
                for k in range(2):
                    c0 = i * (2 * CH) + k * CH
                    ve.wait_ge(rank_done[k], i + 1)
                    ch.link(v.tensor_tensor(ranked[:, :, :], rank_ps[:, k, 0:CH * NB].rearrange("p (a b) -> p a b", b=NB),
                                            run[:, :].unsqueeze(1).to_broadcast([P, CH, NB]), ALU.add))
                    v.tensor_tensor(run[:, :], run[:, :], total_ps[:, k, 0:NB], ALU.add).then_inc(rank_used[k], 1)
                    ve.wait_ge(rank_used[k], i + 1)
                    ch.link(v.tensor_tensor(picked[:, :, :], ranked[:, :, :], in_block[:, bass.ds(c0, CH), :], ALU.mult))
                    ch.link(v.tensor_reduce(pos[:, :], picked[:, :, :], AX.X, ALU.add))
                    ve.wait_ge(scattered[k], i * (16 * CH))
                    v.tensor_tensor(pos_ring[:, k, :], pos[:, :], dropped[:, bass.ds(c0, CH)], ALU.add).then_inc(pos_ready[k], 1)
            ch.leave(NCH // 2)
            ve.wait_ge(turned, 1)
            for g in range(G):
                last = v.tensor_copy(slot_i[:, g * RT:(g + 1) * RT], turned_ps(g))
            ch.link(last)
            v.tensor_scalar(gather_idx[:, 0:M], slot_i[:, 0:M], (1 << LO_SHIFT) - 1, None, ALU.bitwise_and)
            ch.link(v.tensor_scalar(slot_i[:, 0:M], slot_i[:, 0:M], LO_SHIFT, None, ALU.arith_shift_right))
            ch.link(v.tensor_copy(node_of_slot[:, 0:M], slot_i[:, 0:M]))


def group_statistics(ve, v, t, ch, src, s, var_ready, std_ready, groups_before):
    settle(ve, t)
    for j in range(GRP):
        last = v.bn_stats(s.st[:, j, :], src[:, j, :])
    ch.link(last)
    settle(ve, t)
    for j in range(GRP):
        last = v.bn_aggr(s.mv[:, j, :], s.st[:, j, :])
    ch.link(last)
    v.tensor_scalar(s.var[:, :], s.mv[:, :, 1], EPS, None, ALU.add).then_inc(var_ready, 1)
    ve.wait_ge(std_ready, groups_before + 1)
    ch.link(v.reciprocal(s.rstd[:, :], s.std[:, :]))
    ch.link(v.scalar_tensor_tensor(s.var[:, :], s.var[:, :], -0.5, s.rstd[:, :], ALU.mult, ALU.mult))
    ch.link(v.tensor_tensor(s.var[:, :], s.var[:, :], s.rstd[:, :], ALU.mult))
    ch.link(v.scalar_tensor_tensor(s.rstd[:, :], s.var[:, :], 1.5, s.rstd[:, :], ALU.add, ALU.mult))


STAT_LINKS = 6


def statistics_tensors(nc, c, tag):
    s = Tensors()
    s.st = c.enter_context(nc.sbuf_tensor(tag + "st", [P, GRP, 6], F32))
    s.mv = c.enter_context(nc.sbuf_tensor(tag + "mv", [P, GRP, 2], F32))
    s.var = c.enter_context(nc.sbuf_tensor(tag + "var", [P, GRP], F32))
    s.std = c.enter_context(nc.sbuf_tensor(tag + "std", [P, GRP], F32))
    s.rstd = c.enter_context(nc.sbuf_tensor(tag + "rstd", [P, GRP], F32))
    return s


def project_input(nc, t, x, W_in, b_in):
    with ExitStack() as c:
        sb = lambda n, s, d=F32: c.enter_context(nc.sbuf_tensor("in_" + n, s, d))
        sem = semaphores(nc, c, "in_")
        w = sb("w", [P, DC, D])
        b = sb("b", [1, D])
        norm = sb("norm", [P, GRP, D])
        normT = sb("normT", [P, GRP, DC, P])
        s = statistics_tensors(nc, c, "in_")
        ps = c.enter_context(nc.psum_tensor("in_ps", [P, 8, 512], F32))
        loaded, dv, var_ready, std_ready, norm_ready, turned, turned_sb, made, stored = (
            sem(n) for n in ("loaded", "dv", "var_ready", "std_ready", "norm_ready", "turned", "turned_sb", "made", "stored"))
        half = lambda lo, j: ps[:, lo + j // 2, (j % 2) * D:(j % 2 + 1) * D]
        both = lambda lo: ps[:, lo:lo + 4, :].rearrange("p a b -> p (a b)")[:, 0:GRP * D]
        block = c.enter_context(nc.Block())

        @block.sync
        def _(sp):
            sp.dma_start(t.h[:, :, :], x.rearrange("(b p) d -> p b d", p=P)).then_inc(loaded, 16)
            sp.dma_start(w[:, :, :], W_in.rearrange("(c p) d -> p c d", p=P)).then_inc(loaded, 16)
            sp.dma_start(b[:, :], b_in.rearrange("(o d) -> o d", o=1)).then_inc(loaded, 16)

        @block.vector
        def _(ve):
            v = nc.vector
            ch = Chain(ve, dv)
            ve.wait_ge(loaded, 48)
            with ve.Fori(0, NG) as i:
                ch.enter(i, STAT_LINKS)
                xg = t.h[:, bass.ds(i * GRP, GRP), :]
                group_statistics(ve, v, t, ch, xg, s, var_ready, std_ready, i)
                ve.wait_ge(turned, i)
                for j in range(GRP):
                    last = v.tensor_scalar(norm[:, j, :], xg[:, j, :], s.mv[:, j, 0:1], s.rstd[:, j:j + 1],
                                           ALU.subtract, ALU.mult)
                last.then_inc(norm_ready, 1)
            ch.leave(NG)

        @block.scalar
        def _(act):
            with act.Fori(0, NG) as i:
                act.wait_ge(var_ready, i + 1)
                nc.scalar.activation(s.std[:, :], s.var[:, :], ACT.Sqrt).then_inc(std_ready, 1)
                act.wait_ge(turned, i + 1)
                nc.scalar.activation(normT[:, :, :, :].rearrange("p a b c -> p (a b c)"), both(0), ACT.Copy).then_inc(turned_sb, 1)
                act.wait_ge(made, i + 1)
                nc.scalar.activation(t.h[:, bass.ds(i * GRP, GRP), :].rearrange("p a b -> p (a b)"), both(4), ACT.Copy).then_inc(stored, 1)

        @block.tensor
        def _(pe):
            pe.wait_ge(loaded, 48)
            with pe.Fori(0, NG) as i:
                pe.wait_ge(norm_ready, i + 1)
                pe.wait_ge(turned_sb, i)
                for j in range(GRP):
                    for k in range(DC):
                        last = nc.tensor.transpose(half(0, j)[:, k * P:(k + 1) * P], norm[:, j, k * P:(k + 1) * P], t.ident_f[:, :])
                last.then_inc(turned, 1)
                pe.wait_ge(turned_sb, i + 1)
                pe.wait_ge(stored, i)
                for j in range(GRP):
                    for k in range(DC):
                        nc.tensor.matmul(half(4, j), normT[:, j, k, :], w[:, k, :], start=(k == 0), stop=False)
                    last = nc.tensor.matmul(half(4, j), t.ones_f[0:1, :], b[0:1, :], start=False, stop=True)
                last.then_inc(made, 1)


def gnn_layers(nc, t, Wl, bl, Wg, bg, gamma, beta, table):
    IT = M_GNN // (2 * CH)
    with ExitStack() as c:
        sb = lambda n, s, d=F32: c.enter_context(nc.sbuf_tensor("g_" + n, s, d))
        sem = semaphores(nc, c, "g_")
        two = lambda n: [sem(f"{n}{k}") for k in range(2)]
        msg = t.msg
        wl = sb("wl", [P, DC, D])
        wg = sb("wg", [P, DC, D])
        gam = sb("gam", [P, D])
        bet = sb("bet", [P, D])
        bias_l = sb("bias_l", [1, D])
        bias_g = sb("bias_g", [1, D])
        bias = sb("bias", [1, D])
        mean_row = sb("mean_row", [1, D])
        mean_col = sb("mean_col", [P, DC])
        rows = sb("rows", [P, GRP, D])
        idx_ring = sb("idx_ring", [P, 2, CH], I32)
        got = sb("got", [P, 2, CH, D])
        hot = sb("hot", [P, 2, CH, P])
        gotf = got[:, :, :, :].rearrange("p a b c -> p (a b c)")
        zin = gotf[:, 0:GRP * D].rearrange("p (a b) -> p a b", b=D)
        zT = gotf[:, GRP * D:2 * GRP * D].rearrange("p (a b c) -> p a b c", b=DC, c=P)
        s = statistics_tensors(nc, c, "g_")
        ps = c.enter_context(nc.psum_tensor("g_ps", [P, 8, 512], F32))
        half = lambda lo, j: ps[:, lo + j // 2, (j % 2) * D:(j % 2 + 1) * D]
        both = lambda lo: ps[:, lo:lo + 4, :].rearrange("p a b -> p (a b)")[:, 0:GRP * D]
        (weights_in, dv, msg_clear, table_rows, table_in, sum_done, mean_row_ready, mean_col_done,
         mean_col_ready, ctx_done, bias_ready, zin_ready, turned, turned_sb, made, relu_done, relu_used, var_ready,
         std_ready) = (sem(n) for n in (
             "weights_in", "dv", "msg_clear", "table_rows", "table_in", "sum_done", "mean_row_ready",
             "mean_col_done", "mean_col_ready", "ctx_done", "bias_ready", "zin_ready", "turned", "turned_sb", "made",
             "relu_done", "relu_used", "var_ready", "std_ready"))
        settled = sem("settled")
        idx_ready, gathered, hot_ready, summed, added = (two(n) for n in ("idx_ready", "gathered", "hot_ready", "summed", "added"))
        block = c.enter_context(nc.Block())
        table_v = table.rearrange("(b p) d -> p b d", p=P)

        @block.sync
        def _(sp):
            with sp.Fori(0, LAYERS) as l:
                sp.wait_ge(relu_used, l * NG)
                one = bass.ds(l, 1)
                sp.dma_start(wl[:, :, :], Wl[one, :, :].rearrange("l (c p) d -> p (l c) d", p=P)).then_inc(weights_in, 16)
                sp.dma_start(wg[:, :, :], Wg[one, :, :].rearrange("l (c p) d -> p (l c) d", p=P)).then_inc(weights_in, 16)
                sp.dma_start(gam[:, :], gamma[one, :].to_broadcast([P, D])).then_inc(weights_in, 16)
                sp.dma_start(bet[:, :], beta[one, :].to_broadcast([P, D])).then_inc(weights_in, 16)
                sp.dma_start(bias_l[:, :], bl[one, :]).then_inc(weights_in, 16)
                sp.dma_start(bias_g[:, :], bg[one, :]).then_inc(weights_in, 16)
                with sp.Fori(0, NG) as i:
                    sp.wait_ge(table_rows, l * NG + i + 1)
                    sp.dma_start(table_v[:, bass.ds(i * GRP, GRP), :], rows[:, :, :]).then_inc(table_in, 16)

        @block.gpsimd
        def _(gp):
            with gp.Fori(0, LAYERS) as l:
                gp.wait_ge(relu_used, l * NG)
                settle_gpsimd(gp, t, settled, l * (2 + 2 * IT))
                gp.memset(msg[:, :, :], 0.0).then_inc(msg_clear, 1)
                gp.wait_ge(table_in, (l + 1) * (16 * NG))
                settle_gpsimd(gp, t, settled, l * (2 + 2 * IT) + 1)
                with gp.Fori(0, IT) as i:
                    for k in range(2):
                        gp.wait_ge(idx_ready[k], l * IT + i + 1)
                        gp.wait_ge(summed[k], l * IT + i)
                        settle_gpsimd(gp, t, settled, l * (2 + 2 * IT) + (i * 2 + k + 2))
                        for j in range(CH):
                            gp.indirect_dma_start(
                                out=got[:, k, j, :], out_offset=None, in_=table,
                                in_offset=bass.IndirectOffsetOnAxis(ap=idx_ring[:, k, j:j + 1], axis=0)).then_inc(gathered[k], 16)

        @block.scalar
        def _(act):
            with act.Fori(0, LAYERS) as l:
                act.wait_ge(relu_used, l * NG)
                with act.Fori(0, NG) as i:
                    act.wait_ge(table_in, (l * NG + i) * 16)
                    for j in range(GRP):
                        b = i * GRP + j
                        last = nc.scalar.activation(rows[:, j, :], t.h[:, bass.ds(b, 1), :].rearrange("p a b -> p (a b)"),
                                                    ACT.Copy, scale=t.dinv[:, bass.ds(b, 1)])
                    last.then_inc(table_rows, 1)
                with act.Fori(0, IT) as i:
                    for k in range(2):
                        act.wait_ge(gathered[k], (l * IT + i) * (16 * CH))
                        nc.scalar.activation(idx_ring[:, k, :], t.gnn_idx[:, bass.ds(i * (2 * CH) + k * CH, CH)],
                                             ACT.Copy).then_inc(idx_ready[k], 1)
                with act.Fori(0, NG) as i:
                    g = l * NG + i
                    act.wait_ge(turned, g + 1)
                    nc.scalar.activation(zT.rearrange("p a b c -> p (a b c)"), both(0), ACT.Copy).then_inc(turned_sb, 1)
                    act.wait_ge(made, g + 1)
                    act.wait_ge(relu_used, g)
                    nc.scalar.activation(rows[:, :, :].rearrange("p a b -> p (a b)"), both(4), ACT.Relu).then_inc(relu_done, 1)
                    act.wait_ge(var_ready, g + 1)
                    nc.scalar.activation(s.std[:, :], s.var[:, :], ACT.Sqrt).then_inc(std_ready, 1)

        @block.tensor
        def _(pe):
            with pe.Fori(0, LAYERS) as l:
                pe.wait_ge(relu_used, l * NG)
                flat = lambda b: t.h[:, b, :].rearrange("p a b -> p (a b)")
                nc.tensor.matmul(ps[0:1, 0, 0:D], t.valid[:, 0:1], t.h[:, 0, :], start=True, stop=False)
                with pe.Fori(1, NB - 1) as b:
                    nc.tensor.matmul(ps[0:1, 0, 0:D], t.valid[:, 0:1], flat(bass.ds(b, 1)), start=False, stop=False)
                nc.tensor.matmul(ps[0:1, 0, 0:D], t.valid[:, 1:2], t.h[:, NB - 1, :], start=False, stop=True).then_inc(sum_done, 1)
                pe.wait_ge(mean_row_ready, l + 1)
                for k in range(DC):
                    last = nc.tensor.matmul(ps[:, 1, k:k + 1], mean_row[0:1, k * P:(k + 1) * P], t.ones_f[0:1, 0:1], start=True, stop=True)
                last.then_inc(mean_col_done, 1)
                pe.wait_ge(mean_col_ready, l + 1)
                pe.wait_ge(weights_in, (l + 1) * (16 * 6))
                for k in range(DC):
                    last = nc.tensor.matmul(ps[0:1, 0, 0:D], mean_col[:, k:k + 1], wg[:, k, :], start=(k == 0), stop=(k == DC - 1))
                last.then_inc(ctx_done, 1)
                with pe.Fori(0, IT) as i:
                    for k in range(2):
                        n = l * IT + i
                        pe.wait_ge(gathered[k], (n + 1) * (16 * CH))
                        pe.wait_ge(hot_ready[k], (l * (IT + 1 - k) + i) + 1)
                        pe.wait_ge(added[k], n)
                        for j in range(CH):
                            last = nc.tensor.matmul(half(4 * k, j), hot[:, k, j, :], got[:, k, j, :], start=True, stop=True)
                        last.then_inc(summed[k], 1)
                with pe.Fori(0, NG) as i:
                    g = l * NG + i
                    pe.wait_ge(zin_ready, g + 1)
                    pe.wait_ge(turned_sb, g)
                    for j in range(GRP):
                        for k in range(DC):
                            last = nc.tensor.transpose(half(0, j)[:, k * P:(k + 1) * P], zin[:, j, k * P:(k + 1) * P], t.ident_f[:, :])
                    last.then_inc(turned, 1)
                    pe.wait_ge(turned_sb, g + 1)
                    pe.wait_ge(relu_done, g)
                    for j in range(GRP):
                        for k in range(DC):
                            nc.tensor.matmul(half(4, j), zT[:, j, k, :], wl[:, k, :], start=(k == 0), stop=False)
                        last = nc.tensor.matmul(half(4, j), t.ones_f[0:1, :], bias[0:1, :], start=False, stop=True)
                    last.then_inc(made, 1)

        @block.vector
        def _(ve):
            v = nc.vector
            ch = Chain(ve, dv)
            PER_LAYER = 1 + 2 * (CH - 1) * IT + NG * (STAT_LINKS + 1)

            def build_hot(col, k):
                v.tensor_tensor(hot[:, k, :, :], t.gnn_node[:, bass.ds(col, CH)].unsqueeze(2).to_broadcast([P, CH, P]),
                                t.iota_f[:, :].unsqueeze(1).to_broadcast([P, CH, P]), ALU.is_equal).then_inc(hot_ready[k], 1)

            with ve.Fori(0, LAYERS) as l:
                base = l * PER_LAYER
                ve.wait_ge(sum_done, l + 1)
                v.tensor_scalar(mean_row[:, :], ps[0:1, 0, 0:D], 1.0 / N, None, ALU.mult).then_inc(mean_row_ready, 1)
                ve.wait_ge(mean_col_done, l + 1)
                v.tensor_copy(mean_col[:, :], ps[:, 1, 0:DC]).then_inc(mean_col_ready, 1)
                ve.wait_ge(weights_in, (l + 1) * (16 * 6))
                ve.wait_ge(ctx_done, l + 1)
                ch.base, ch.n = base, 0
                ch.link(v.tensor_tensor(bias[:, :], ps[0:1, 0, 0:D], bias_l[:, :], ALU.add))
                v.tensor_tensor(bias[:, :], bias[:, :], bias_g[:, :], ALU.add).then_inc(bias_ready, 1)
                ve.wait_ge(msg_clear, l + 1)
                build_hot(0, 0)
                with ve.Fori(0, IT) as i:
                    ch.base, ch.n = base + 1 + i * (2 * (CH - 1)), 0
                    for k in range(2):
                        other = 1 - k
                        ve.wait_ge(summed[other], l * IT + i + k)
                        build_hot(i * (2 * CH) + (k + 1) * CH, other)
                        ve.wait_ge(summed[k], l * IT + i + 1)
                        at = [ve.value_load(t.gnn_block[0:1, bass.ds(i * (2 * CH) + k * CH + j, 1)], min_val=0, max_val=NB - 1)
                              for j in range(CH)]
                        for j in range(CH):
                            m = msg[:, bass.ds(at[j], 1), :].rearrange("p a b -> p (a b)")
                            ins = v.tensor_tensor(m, m, half(4 * k, j), ALU.add)
                            if j < CH - 1:
                                ch.link(ins)
                        ins.then_inc(added[k], 1)
                        ve.wait_ge(added[k], l * IT + i + 1)
                tail = base + 1 + 2 * (CH - 1) * IT

                def make_zin(i):
                    for j in range(GRP):
                        one = bass.ds(i * GRP + j, 1)
                        f = lambda x: x[:, one, :].rearrange("p a b -> p (a b)")
                        last = v.scalar_tensor_tensor(zin[:, j, :], f(msg), t.dinv[:, one], f(t.h), ALU.mult, ALU.add)
                    last.then_inc(zin_ready, 1)

                def norm_group(i):
                    ch.base, ch.n = tail + i * (STAT_LINKS + 1), 0
                    ve.wait_ge(relu_done, l * NG + i + 1)
                    group_statistics(ve, v, t, ch, rows, s, var_ready, std_ready, l * NG + i)
                    for j in range(GRP):
                        last = v.scalar_tensor_tensor(rows[:, j, :], rows[:, j, :], s.mv[:, j, 0:1], gam[:, :], ALU.subtract, ALU.mult)
                    ch.link(last)
                    for j in range(GRP):
                        last = v.scalar_tensor_tensor(t.h[:, bass.ds(i * GRP + j, 1), :].rearrange("p a b -> p (a b)"), rows[:, j, :],
                                                      s.rstd[:, j:j + 1], bet[:, :], ALU.mult, ALU.add)
                    last.then_inc(relu_used, 1)

                make_zin(0)
                with ve.Fori(0, NG - 1) as i:
                    ve.wait_ge(turned, l * NG + i + 1)
                    make_zin(i + 1)
                    norm_group(i)
                norm_group(NG - 1)
                ve.wait_ge(relu_used, (l + 1) * NG)


def attention_rows(nc, t, x, W_gat, att_src, att_dst, x1, table):
    with ExitStack() as c:
        sb = lambda n, s, d=F32: c.enter_context(nc.sbuf_tensor("a_" + n, s, d))
        sem = semaphores(nc, c, "a_")
        xg = sb("xg", [P, GRP, D])
        w = sb("w", [P, DC, HE])
        att = sb("att", [P, 2, HE])
        norm = sb("norm", [P, GRP, D])
        normT = sb("normT", [P, GRP, DC, P])
        prod = sb("prod", [P, 2, GRP, HE])
        s = statistics_tensors(nc, c, "a_")
        ps = c.enter_context(nc.psum_tensor("a_ps", [P, 8, 512], F32))
        (weights_in, x_in, x1_ready, x1_out, dv, var_ready, std_ready, norm_ready, turned, turned_sb, made, rows_made,
         table_out) = (sem(n) for n in ("weights_in", "x_in", "x1_ready", "x1_out", "dv", "var_ready", "std_ready",
                                        "norm_ready", "turned", "turned_sb", "made", "rows_made", "table_out"))
        half = lambda lo, j: ps[:, lo + j // 2, (j % 2) * D:(j % 2 + 1) * D]
        both = lambda lo: ps[:, lo:lo + 4, :].rearrange("p a b -> p (a b)")[:, 0:GRP * D]
        block = c.enter_context(nc.Block())
        group = lambda i: bass.ds(i * GRP, GRP)

        @block.sync
        def _(sp):
            sp.dma_start(w[:, :, :], W_gat.rearrange("(c p) d -> p c d", p=P)).then_inc(weights_in, 16)
            sp.dma_start(att[:, 0, :], att_src.rearrange("(o a) b -> o (a b)", o=1).to_broadcast([P, HE])).then_inc(weights_in, 16)
            sp.dma_start(att[:, 1, :], att_dst.rearrange("(o a) b -> o (a b)", o=1).to_broadcast([P, HE])).then_inc(weights_in, 16)
            with sp.Fori(0, NG) as i:
                sp.wait_ge(x1_ready, i)
                sp.dma_start(xg[:, :, :], x.rearrange("(b p) d -> p b d", p=P)[:, group(i), :]).then_inc(x_in, 16)
            sp.wait_ge(x1_ready, NG)
            sp.dma_start(x1.rearrange("(b p) d -> p b d", p=P), t.h[:, :, :]).then_inc(x1_out, 16)
            sp.wait_ge(rows_made, NG)
            sp.dma_start(table.rearrange("(b p) d -> p b d", p=P), t.rows[:, :, :]).then_inc(table_out, 16)
            sp.wait_ge(x1_out, 16)
            sp.wait_ge(table_out, 16)

        @block.vector
        def _(ve):
            v = nc.vector
            ch = Chain(ve, dv)
            ve.wait_ge(weights_in, 48)
            with ve.Fori(0, NG) as i:
                ch.enter(i, STAT_LINKS + 1)
                h = t.h[:, group(i), :]
                ve.wait_ge(x_in, (i + 1) * 16)
                v.tensor_tensor(h, h, xg[:, :, :], ALU.add).then_inc(x1_ready, 1)
                ve.wait_ge(x1_ready, i + 1)
                group_statistics(ve, v, t, ch, h, s, var_ready, std_ready, i)
                ve.wait_ge(turned, i)
                for j in range(GRP):
                    last = v.tensor_scalar(norm[:, j, :], h[:, j, :], s.mv[:, j, 0:1], s.rstd[:, j:j + 1],
                                           ALU.subtract, ALU.mult)
                last.then_inc(norm_ready, 1)
                ve.wait_ge(made, i + 1)
                hp = ps[:, 4, 0:GRP * HE].rearrange("p (a b) -> p a b", b=HE)
                v.tensor_copy(t.rows[:, group(i), 0:HE], hp)
                for k in range(2):
                    last = v.tensor_tensor(prod[:, k, :, :], hp, att[:, k, :].unsqueeze(1).to_broadcast([P, GRP, HE]), ALU.mult)
                ch.link(last)
                per_head = lambda k: prod[:, k, :, :].rearrange("p a (b c) -> p a b c", c=EXPERTS)
                v.tensor_reduce(t.rows[:, group(i), HE:ROW], per_head(0), AX.X, ALU.add)
                v.tensor_reduce(t.adst[:, group(i), :], per_head(1), AX.X, ALU.add).then_inc(rows_made, 1)
            ch.leave(NG)

        @block.scalar
        def _(act):
            with act.Fori(0, NG) as i:
                act.wait_ge(var_ready, i + 1)
                nc.scalar.activation(s.std[:, :], s.var[:, :], ACT.Sqrt).then_inc(std_ready, 1)
                act.wait_ge(turned, i + 1)
                act.wait_ge(made, i)
                nc.scalar.activation(normT[:, :, :, :].rearrange("p a b c -> p (a b c)"), both(0), ACT.Copy).then_inc(turned_sb, 1)
                for k in range(DC):
                    last = nc.scalar.activation(
                        t.yT[:, k, bass.ds(i * (GRP * P), GRP * P)].rearrange("p (a b) -> p a b", b=P),
                        both(0).rearrange("p (a b c) -> p a b c", b=DC, c=P)[:, :, k, :], ACT.Copy)
                last.then_inc(turned_sb, 1)

        @block.tensor
        def _(pe):
            pe.wait_ge(weights_in, 48)
            with pe.Fori(0, NG) as i:
                pe.wait_ge(norm_ready, i + 1)
                pe.wait_ge(turned_sb, i * 2)
                for j in range(GRP):
                    for k in range(DC):
                        last = nc.tensor.transpose(half(0, j)[:, k * P:(k + 1) * P], norm[:, j, k * P:(k + 1) * P], t.ident_f[:, :])
                last.then_inc(turned, 1)
                pe.wait_ge(turned_sb, i * 2 + 1)
                pe.wait_ge(rows_made, i)
                for j in range(GRP):
                    for k in range(DC):
                        last = nc.tensor.matmul(ps[:, 4, j * HE:(j + 1) * HE], normT[:, j, k, :], w[:, k, :], start=(k == 0), stop=(k == DC - 1))
                last.then_inc(made, 1)


def attention_max(nc, t, table):
    CM = CH // 2
    IT = M_GAT // (2 * CM)
    with ExitStack() as c:
        sb = lambda n, s, d=F32: c.enter_context(nc.sbuf_tensor("m_" + n, s, d))
        sem = semaphores(nc, c, "m_")
        two = lambda n: [sem(f"{n}{k}") for k in range(2)]
        idx_ring = sb("idx_ring", [P, 2, CM], I32)
        got = sb("got", [P, 2, CM, ROW])
        not_hot = sb("not_hot", [P, 2, CM, P], BF16)
        tile_top = sb("tile_top", [P, CM, HEADS])
        ps = c.enter_context(nc.psum_tensor("m_ps", [P, 8, 512], F32))
        dv, top_set, settled = sem("dv"), sem("top_set"), sem("settled")
        idx_ready, gathered, kept, not_hot_ready, spread, maxed = (
            two(n) for n in ("idx_ready", "gathered", "kept", "not_hot_ready", "spread", "maxed"))
        block = c.enter_context(nc.Block())

        @block.gpsimd
        def _(gp):
            with gp.Fori(0, IT) as i:
                for k in range(2):
                    gp.wait_ge(idx_ready[k], i + 1)
                    gp.wait_ge(kept[k], i)
                    gp.wait_ge(spread[k], i)
                    settle_gpsimd(gp, t, settled, i * 2 + k)
                    for j in range(CM):
                        gp.indirect_dma_start(
                            out=got[:, k, j, :], out_offset=None, in_=table,
                            in_offset=bass.IndirectOffsetOnAxis(ap=idx_ring[:, k, j:j + 1], axis=0)).then_inc(gathered[k], 16)

        @block.scalar
        def _(act):
            def indices(col, k):
                nc.scalar.activation(idx_ring[:, k, :], t.gat_idx[:, bass.ds(col, CM)], ACT.Copy).then_inc(idx_ready[k], 1)

            for k in range(2):
                indices(k * CM, k)
            with act.Fori(0, IT) as i:
                for k in range(2):
                    act.wait_ge(gathered[k], (i + 1) * (16 * CM))
                    c0 = i * (2 * CM) + k * CM
                    nc.scalar.activation(t.edge_rows[:, bass.ds(c0, CM), :], got[:, k, :, :], ACT.Copy).then_inc(kept[k], 1)
                    indices(c0 + 2 * CM, k)

        @block.tensor
        def _(pe):
            with pe.Fori(0, IT) as i:
                for k in range(2):
                    pe.wait_ge(gathered[k], (i + 1) * (16 * CM))
                    pe.wait_ge(not_hot_ready[k], i + 1)
                    pe.wait_ge(maxed[k], i)
                    for j in range(CM):
                        nc.tensor.matmul(ps[:, CM * k + j, :].rearrange("p (a b) -> p a b", b=P), not_hot[:, k, j, :],
                                         t.neg_ident_b[:, :].unsqueeze(1).to_broadcast([P, HEADS, P]), start=True, stop=False)
                        for h in range(HEADS):
                            last = nc.tensor.matmul(ps[:, CM * k + j, h * P:(h + 1) * P],
                                                    got[:, k, j, HE + h:HE + h + 1].to_broadcast([P, P]), t.ident_f[:, :],
                                                    start=False, stop=(h == HEADS - 1))
                    last.then_inc(spread[k], 1)

        @block.vector
        def _(ve):
            v = nc.vector
            ch = Chain(ve, dv)

            def build_not_hot(col, k):
                v.tensor_tensor(not_hot[:, k, :, :], t.gat_node[:, bass.ds(col, CM)].unsqueeze(2).to_broadcast([P, CM, P]),
                                t.iota_f[:, :].unsqueeze(1).to_broadcast([P, CM, P]), ALU.not_equal).then_inc(not_hot_ready[k], 1)

            v.tensor_copy(t.top[:, :, :], t.rows[:, :, HE:ROW]).then_inc(top_set, 1)
            ve.wait_ge(top_set, 1)
            build_not_hot(0, 0)
            with ve.Fori(0, IT) as i:
                ch.enter(i, 2 * CM)
                for k in range(2):
                    other = 1 - k
                    ve.wait_ge(spread[other], i + k)
                    build_not_hot(i * (2 * CM) + (k + 1) * CM, other)
                    ve.wait_ge(spread[k], i + 1)
                    ch.link(v.tensor_reduce(tile_top[:, :, :], ps[:, CM * k:CM * (k + 1), :].rearrange("p a (b c) -> p a b c", c=P),
                                            AX.X, ALU.max))
                    at = [ve.value_load(t.gat_block[0:1, bass.ds(i * (2 * CM) + k * CM + j, 1)], min_val=0, max_val=NB - 1)
                          for j in range(CM)]
                    for j in range(CM):
                        m = t.top[:, bass.ds(at[j], 1), :].rearrange("p a b -> p (a b)")
                        ins = v.tensor_tensor(m, m, tile_top[:, j, :], ALU.max)
                        if j < CM - 1:
                            ch.link(ins)
                    ins.then_inc(maxed[k], 1)
                    ve.wait_ge(maxed[k], i + 1)
            ch.leave(IT)


def attention_sum(nc, t):
    IT = M_GAT // (2 * CH)
    with ExitStack() as c:
        sb = lambda n, s, d=F32: c.enter_context(nc.sbuf_tensor("s_" + n, s, d))
        sem = semaphores(nc, c, "s_")
        two = lambda n: [sem(f"{n}{k}") for k in range(2)]
        hot = sb("hot", [P, 2, CH, P])
        hotT = sb("hotT", [P, 2, CH, P])
        score = sb("score", [P, 2, CH, HEADS])
        weighted = sb("weighted", [P, 2, CH, ROW])
        ps = c.enter_context(nc.psum_tensor("s_ps", [P, 8, 512], F32))
        dv, node_ready = sem("dv"), sem("node_ready")
        hot_ready, turned, turned_sb, picked, score_ready, exp_done, weighted_ready, summed, added = (
            two(n) for n in ("hot_ready", "turned", "turned_sb", "picked", "score_ready", "exp_done", "weighted_ready", "summed", "added"))
        flat = lambda a: a.rearrange("p a b -> p (a b)")
        turned_ps = lambda k: flat(ps[:, 2 * k:2 * k + 2, :])
        picked_ps = lambda k: ps[:, 4 + k, 0:CH * 2 * HEADS].rearrange("p (a b) -> p a b", b=2 * HEADS)
        summed_ps = lambda k: ps[:, 6 + k, 0:CH * ROW].rearrange("p (a b) -> p a b", b=ROW)
        block = c.enter_context(nc.Block())

        @block.vector
        def _(ve):
            v = nc.vector
            ch = Chain(ve, dv)
            adst, emax = t.node[:, :, 0:HEADS], t.node[:, :, HEADS:2 * HEADS]
            v.memset(t.sums[:, :, :], 0.0)
            v.tensor_copy(adst, t.adst[:, :, :])
            ch.link(v.tensor_tensor(t.top[:, :, :], t.top[:, :, :], t.adst[:, :, :], ALU.add))
            v.scalar_tensor_tensor(emax, t.top[:, :, :], 0.2, t.top[:, :, :], ALU.mult, ALU.max).then_inc(node_ready, 1)
            ve.wait_ge(node_ready, 1)
            with ve.Fori(0, IT) as i:
                ch.enter(i, 2 * (3 + CH - 1))
                for k in range(2):
                    ve.wait_ge(summed[k], i)
                    v.tensor_tensor(hot[:, k, :, :], t.gat_node[:, bass.ds((i * 2 + k) * CH, CH)].unsqueeze(2).to_broadcast([P, CH, P]),
                                    t.iota_f[:, :].unsqueeze(1).to_broadcast([P, CH, P]), ALU.is_equal).then_inc(hot_ready[k], 1)
                for k in range(2):
                    ve.wait_ge(picked[k], i + 1)
                    a_src = t.edge_rows[:, bass.ds((i * 2 + k) * CH, CH), HE:ROW]
                    ch.link(v.tensor_tensor(score[:, k, :, :], picked_ps(k)[:, :, 0:HEADS], a_src, ALU.add))
                    ch.link(v.scalar_tensor_tensor(flat(score[:, k, :, :]), flat(score[:, k, :, :]), 0.2, flat(score[:, k, :, :]), ALU.mult, ALU.max))
                    ch.link(v.tensor_tensor(score[:, k, :, :], score[:, k, :, :], picked_ps(k)[:, :, HEADS:2 * HEADS], ALU.subtract))
                    v.tensor_scalar(flat(score[:, k, :, :]), flat(score[:, k, :, :]), 0.0, None, ALU.min).then_inc(score_ready[k], 1)
                for k in range(2):
                    ve.wait_ge(exp_done[k], i + 1)
                    v.tensor_tensor(weighted[:, k, :, 0:HE].rearrange("p a (b c) -> p a b c", c=EXPERTS),
                                    t.edge_rows[:, bass.ds((i * 2 + k) * CH, CH), 0:HE].rearrange("p a (b c) -> p a b c", c=EXPERTS),
                                    weighted[:, k, :, HE:ROW].unsqueeze(3).to_broadcast([P, CH, HEADS, EXPERTS]), ALU.mult).then_inc(weighted_ready[k], 1)
                for k in range(2):
                    at = [ve.value_load(t.gat_block[0:1, bass.ds((i * 2 + k) * CH + j, 1)], min_val=0, max_val=NB - 1)
                          for j in range(CH)]
                    ve.wait_ge(summed[k], i + 1)
                    for j in range(CH):
                        m = flat(t.sums[:, bass.ds(at[j], 1), :])
                        ins = v.tensor_tensor(m, m, summed_ps(k)[:, j, :], ALU.add)
                        if j < CH - 1:
                            ch.link(ins)
                    ins.then_inc(added[k], 1)
                    ve.wait_ge(added[k], i + 1)
            ch.leave(IT)

        @block.scalar
        def _(act):
            with act.Fori(0, IT) as i:
                for k in range(2):
                    act.wait_ge(turned[k], i + 1)
                    nc.scalar.activation(hotT[:, k, :, :].rearrange("p a b -> p (a b)"), turned_ps(k), ACT.Copy).then_inc(turned_sb[k], 1)
                for k in range(2):
                    act.wait_ge(score_ready[k], i + 1)
                    act.wait_ge(summed[k], i)
                    nc.scalar.activation(weighted[:, k, :, HE:ROW], score[:, k, :, :], ACT.Exp).then_inc(exp_done[k], 1)

        @block.tensor
        def _(pe):
            pe.wait_ge(node_ready, 1)
            with pe.Fori(0, IT) as i:
                for k in range(2):
                    pe.wait_ge(hot_ready[k], i + 1)
                    for j in range(CH):
                        last = nc.tensor.transpose(turned_ps(k)[:, j * P:(j + 1) * P], hot[:, k, j, :], t.ident_f[:, :])
                    last.then_inc(turned[k], 1)
                for k in range(2):
                    at = [pe.value_load(t.gat_block[0:1, bass.ds((i * 2 + k) * CH + j, 1)], min_val=0, max_val=NB - 1)
                          for j in range(CH)]
                    pe.wait_ge(turned_sb[k], i + 1)
                    for j in range(CH):
                        last = nc.tensor.matmul(picked_ps(k)[:, j, :], hotT[:, k, j, :], flat(t.node[:, bass.ds(at[j], 1), :]), start=True, stop=True)
                    last.then_inc(picked[k], 1)
                for k in range(2):
                    pe.wait_ge(weighted_ready[k], i + 1)
                    pe.wait_ge(added[k], i)
                    for j in range(CH):
                        last = nc.tensor.matmul(summed_ps(k)[:, j, :], hot[:, k, j, :], weighted[:, k, j, :], start=True, stop=True)
                    last.then_inc(summed[k], 1)


def attention_gates(nc, t, b_gat, ln_gamma, ln_beta):
    with ExitStack() as c:
        sb = lambda n, s, d=F32: c.enter_context(nc.sbuf_tensor("w_" + n, s, d))
        sem = semaphores(nc, c, "w_")
        par = sb("par", [P, 3, HE])
        own = sb("own", [P, NB, HEADS])
        den = sb("den", [P, NB, HEADS])
        agg = sb("agg", [P, NB, HE])
        sq = sb("sq", [P, NB, HE])
        stat = sb("stat", [P, 3, NB])
        std = sb("std", [P, NB])
        score = sb("score", [P, NB, EXPERTS])
        ahead = sb("ahead", [P, NB])
        rank = sb("rank", [P, NB, EXPERTS])
        prob = sb("prob", [P, NB, EXPERTS])
        par_in, dv, own_ready, own_exp, var_ready, std_ready, prob_ready, prob_exp = (
            sem(n) for n in ("par_in", "dv", "own_ready", "own_exp", "var_ready", "std_ready", "prob_ready", "prob_exp"))
        flat = lambda a: a.rearrange("p a b -> p (a b)")
        block = c.enter_context(nc.Block())

        @block.sync
        def _(sp):
            for k, a in enumerate((b_gat, ln_gamma, ln_beta)):
                sp.dma_start(par[:, k, :], a.rearrange("(o d) -> o d", o=1).to_broadcast([P, HE])).then_inc(par_in, 16)

        @block.scalar
        def _(act):
            act.wait_ge(own_ready, 1)
            nc.scalar.activation(flat(own[:, :, :]), flat(own[:, :, :]), ACT.Exp).then_inc(own_exp, 1)
            act.wait_ge(var_ready, 1)
            nc.scalar.activation(std[:, :], stat[:, 1, :], ACT.Sqrt).then_inc(std_ready, 1)
            act.wait_ge(prob_ready, 1)
            nc.scalar.activation(flat(prob[:, :, :]), flat(prob[:, :, :]), ACT.Exp).then_inc(prob_exp, 1)

        @block.vector
        def _(ve):
            v = nc.vector
            ch = Chain(ve, dv)
            link = ch.link
            heads = lambda a: a.rearrange("p a (b c) -> p a b c", c=EXPERTS)
            per_head = lambda a: a.unsqueeze(3).to_broadcast([P, NB, HEADS, EXPERTS])
            spread = lambda a, n: a.unsqueeze(2).to_broadcast([P, NB, n])
            param = lambda k: par[:, k, :].unsqueeze(1).to_broadcast([P, NB, HE])
            link(v.tensor_tensor(own[:, :, :], t.rows[:, :, HE:ROW], t.adst[:, :, :], ALU.add))
            link(v.scalar_tensor_tensor(flat(own[:, :, :]), flat(own[:, :, :]), 0.2, flat(own[:, :, :]), ALU.mult, ALU.max))
            v.tensor_tensor(own[:, :, :], own[:, :, :], t.node[:, :, HEADS:2 * HEADS], ALU.subtract).then_inc(own_ready, 1)
            ve.wait_ge(own_ready, 1)
            ve.wait_ge(own_exp, 1)
            link(v.tensor_tensor(den[:, :, :], t.sums[:, :, HE:ROW], own[:, :, :], ALU.add))
            link(v.tensor_scalar(flat(den[:, :, :]), flat(den[:, :, :]), 1e-16, None, ALU.add))
            link(v.reciprocal(flat(den[:, :, :]), flat(den[:, :, :])))
            link(v.tensor_tensor(heads(agg[:, :, :]), heads(t.rows[:, :, 0:HE]), per_head(own[:, :, :]), ALU.mult))
            link(v.tensor_tensor(agg[:, :, :], agg[:, :, :], t.sums[:, :, 0:HE], ALU.add))
            link(v.tensor_tensor(heads(agg[:, :, :]), heads(agg[:, :, :]), per_head(den[:, :, :]), ALU.mult))
            ve.wait_ge(par_in, 48)
            link(v.tensor_tensor(agg[:, :, :], agg[:, :, :], param(0), ALU.add))
            link(v.tensor_reduce(stat[:, 0, :], agg[:, :, :], AX.X, ALU.add))
            link(v.tensor_scalar(stat[:, 0, :], stat[:, 0, :], 1.0 / HE, None, ALU.mult))
            link(v.tensor_tensor(agg[:, :, :], agg[:, :, :], spread(stat[:, 0, :], HE), ALU.subtract))
            link(v.tensor_tensor(sq[:, :, :], agg[:, :, :], agg[:, :, :], ALU.mult))
            link(v.tensor_reduce(stat[:, 1, :], sq[:, :, :], AX.X, ALU.add))
            v.tensor_scalar(stat[:, 1, :], stat[:, 1, :], 1.0 / HE, EPS, ALU.mult, ALU.add).then_inc(var_ready, 1)
            ve.wait_ge(var_ready, 1)
            ve.wait_ge(std_ready, 1)
            link(v.reciprocal(stat[:, 2, :], std[:, :]))
            link(v.scalar_tensor_tensor(stat[:, 1, :], stat[:, 1, :], -0.5, stat[:, 2, :], ALU.mult, ALU.mult))
            link(v.tensor_tensor(stat[:, 1, :], stat[:, 1, :], stat[:, 2, :], ALU.mult))
            link(v.scalar_tensor_tensor(stat[:, 2, :], stat[:, 1, :], 1.5, stat[:, 2, :], ALU.add, ALU.mult))
            link(v.tensor_tensor(agg[:, :, :], agg[:, :, :], spread(stat[:, 2, :], HE), ALU.mult))
            link(v.tensor_tensor(agg[:, :, :], agg[:, :, :], param(1), ALU.mult))
            link(v.tensor_tensor(agg[:, :, :], agg[:, :, :], param(2), ALU.add))
            link(v.tensor_reduce(score[:, :, :], agg[:, :, :].rearrange("p a (b c) -> p a c b", c=EXPERTS), AX.X, ALU.add))
            link(v.tensor_scalar(flat(score[:, :, :]), flat(score[:, :, :]), 1.0 / HEADS, None, ALU.mult))
            link(v.memset(rank[:, :, :], 0.0))
            for a in range(EXPERTS):
                for b in range(EXPERTS):
                    if a != b:
                        link(v.tensor_tensor(ahead[:, :], score[:, :, b], score[:, :, a], ALU.is_ge if b < a else ALU.is_gt))
                        link(v.tensor_tensor(rank[:, :, a], rank[:, :, a], ahead[:, :], ALU.add))
            link(v.tensor_reduce(ahead[:, :], score[:, :, :], AX.X, ALU.max))
            link(v.tensor_scalar(flat(rank[:, :, :]), flat(rank[:, :, :]), float(TOPK), None, ALU.is_lt))
            v.tensor_tensor(prob[:, :, :], score[:, :, :], spread(ahead[:, :], EXPERTS), ALU.subtract).then_inc(prob_ready, 1)
            ve.wait_ge(prob_ready, 1)
            ve.wait_ge(prob_exp, 1)
            link(v.tensor_tensor(prob[:, :, :], prob[:, :, :], rank[:, :, :], ALU.mult))
            link(v.tensor_reduce(ahead[:, :], prob[:, :, :], AX.X, ALU.add))
            link(v.reciprocal(ahead[:, :], ahead[:, :]))
            link(v.tensor_tensor(t.gate[:, :, :], prob[:, :, :], spread(ahead[:, :], EXPERTS), ALU.mult))


def experts(nc, t, space, W1, b1, W2, b2, x1, out):
    TOK = GRP * P
    HALF = TOK // 2
    with ExitStack() as c:
        sb = lambda n, s, d=F32: c.enter_context(nc.sbuf_tensor("e_" + n, s, d))
        sem = semaphores(nc, c, "e_")
        two = lambda n: [sem(f"{n}{k}") for k in range(2)]
        n1, n2, n3, n4 = EXPERTS * DC * HID, EXPERTS * HM * D, 2 * HM * TOK, GRP * D
        w1 = space[:, 0:n1].rearrange("p (e c h) -> p e c h", e=EXPERTS, c=DC)
        w2 = space[:, n1:n1 + n2].rearrange("p (e m d) -> p e m d", e=EXPERTS, m=HM)
        hidden = space[:, n1 + n2:n1 + n2 + n3].rearrange("p (a m t) -> p a m t", a=2, m=HM)
        acc = space[:, n1 + n2 + n3:n1 + n2 + n3 + n4].rearrange("p (a b) -> p a b", b=D)
        b1t = sb("b1", [P, EXPERTS, HM])
        b2t = sb("b2", [EXPERTS, D])
        gate = sb("gate", [P, GRP, EXPERTS])
        gateT = sb("gateT", [EXPERTS, TOK])
        ps = c.enter_context(nc.psum_tensor("e_ps", [P, 8, 512], F32))
        weights_in, acc_in, acc_out, dv, gate_ready, gateT_done, gateT_ready, bias_done, y_done, y_added = (
            sem(n) for n in ("weights_in", "acc_in", "acc_out", "dv", "gate_ready", "gateT_done", "gateT_ready", "bias_done", "y_done", "y_added"))
        hid_done, hid_used = two("hid_done"), two("hid_used")
        y_ps = lambda j: ps[:, 4 + j // 2, (j % 2) * D:(j % 2 + 1) * D]
        gT_ps = lambda j: ps[0:EXPERTS, 4 + j // 4, (j % 4) * P:(j % 4 + 1) * P]
        YG = 1 + EXPERTS
        block = c.enter_context(nc.Block())

        @block.sync
        def _(sp):
            sp.dma_start(w1[:, :, :, :].rearrange("p e c h -> p (e c) h"), W1.rearrange("e (c p) h -> p (e c) h", p=P)).then_inc(weights_in, 16)
            sp.dma_start(w2[:, :, :, :].rearrange("p e m d -> p (e m) d"), W2.rearrange("e (m p) d -> p (e m) d", p=P)).then_inc(weights_in, 16)
            with nc.allow_non_contiguous_dma(reason="2048 biases, once"):
                sp.dma_start(b1t[:, :, :].rearrange("p e m -> p (e m)"), b1.rearrange("e (m p) -> p (e m)", p=P)).then_inc(weights_in, 16)
            sp.dma_start(b2t[:, :], b2).then_inc(weights_in, 16)
            group = lambda a, i: a.rearrange("(b p) d -> p b d", p=P)[:, bass.ds(i * GRP, GRP), :]
            with sp.Fori(0, NG) as i:
                sp.wait_ge(acc_out, i * 16)
                sp.dma_start(acc[:, :, :], group(x1, i)).then_inc(acc_in, 16)
                sp.wait_ge(y_added, (i + 1) * YG)
                sp.dma_start(group(out, i), acc[:, :, :]).then_inc(acc_out, 16)
            sp.wait_ge(acc_out, NG * 16)

        @block.tensor
        def _(pe):
            pe.wait_ge(weights_in, 64)
            with pe.Fori(0, NG) as i:
                pe.wait_ge(gate_ready, i + 1)
                pe.wait_ge(y_added, i * YG)
                for j in range(GRP):
                    last = nc.tensor.transpose(gT_ps(j), gate[:, j, :], t.ident_f[:, :])
                last.then_inc(gateT_done, 1)
                pe.wait_ge(gateT_ready, i + 1)
                for j in range(GRP):
                    last = nc.tensor.matmul(y_ps(j), gateT[:, j * P:(j + 1) * P], b2t[:, :], start=True, stop=True)
                last.then_inc(bias_done, 1)

                def up(e):
                    for m in range(HM):
                        pe.wait_ge(hid_used[m % 2], (i * EXPERTS + e) * (HM // 2) + m // 2)
                        for k in range(DC):
                            for f in range(2):
                                last = nc.tensor.matmul(ps[:, 2 * (m % 2) + f, 0:HALF], w1[:, e, k, m * P:(m + 1) * P],
                                                        t.yT[:, k, bass.ds(i * TOK + f * HALF, HALF)], start=(k == 0), stop=(k == DC - 1))
                        last.then_inc(hid_done[m % 2], 1)

                def down(e):
                    for q in range(2):
                        pe.wait_ge(hid_used[q], (i * EXPERTS + e + 1) * (HM // 2))
                    pe.wait_ge(y_added, i * YG + e + 1)
                    for j in range(GRP):
                        for m in range(HM):
                            last = nc.tensor.matmul(y_ps(j), hidden[:, e % 2, m, j * P:(j + 1) * P], w2[:, e, m, :], start=(m == 0), stop=(m == HM - 1))
                    last.then_inc(y_done, 1)

                up(0)
                for e in range(1, EXPERTS):
                    up(e)
                    down(e - 1)
                down(EXPERTS - 1)

        @block.scalar
        def _(act):
            act.wait_ge(weights_in, 64)
            with act.Fori(0, NG) as i:
                for e in range(EXPERTS):
                    if e >= 2:
                        act.wait_ge(y_done, i * EXPERTS + e - 1)
                    else:
                        act.wait_ge(y_done, i * EXPERTS)
                    for m in range(HM):
                        act.wait_ge(hid_done[m % 2], (i * EXPERTS + e) * (HM // 2) + m // 2 + 1)
                        nc.scalar.activation(hidden[:, e % 2, m, :].rearrange("p (a b) -> p a b", a=2),
                                             ps[:, 2 * (m % 2):2 * (m % 2) + 2, 0:HALF], ACT.Gelu,
                                             bias=b1t[:, e, m:m + 1]).then_inc(hid_used[m % 2], 1)

        @block.vector
        def _(ve):
            v = nc.vector
            ch = Chain(ve, dv)
            with ve.Fori(0, NG) as i:
                ve.wait_ge(gateT_done, i)
                ve.wait_ge(y_added, i * YG)
                v.tensor_copy(gate[:, :, :], t.gate[:, bass.ds(i * GRP, GRP), :]).then_inc(gate_ready, 1)
                ve.wait_ge(gateT_done, i + 1)
                ve.wait_ge(bias_done, i)
                for q in range(2):
                    w = min(4, GRP - 4 * q)
                    last = v.tensor_copy(gateT[:, 4 * q * P:(4 * q + w) * P], ps[0:EXPERTS, 4 + q, 0:w * P])
                last.then_inc(gateT_ready, 1)
                ve.wait_ge(acc_in, (i + 1) * 16)
                ve.wait_ge(bias_done, i + 1)
                for j in range(GRP):
                    last = v.tensor_tensor(acc[:, j, :], acc[:, j, :], y_ps(j), ALU.add)
                last.then_inc(y_added, 1)
                for e in range(EXPERTS):
                    ve.wait_ge(y_added, i * YG + e + 1)
                    ve.wait_ge(y_done, i * EXPERTS + e + 1)
                    for j in range(GRP):
                        last = v.scalar_tensor_tensor(acc[:, j, :], y_ps(j), gate[:, j, e:e + 1], acc[:, j, :], ALU.mult, ALU.add)
                    last.then_inc(y_added, 1)


def build(nc, a, out):
    t = Tensors()
    t.nc = nc
    dram = lambda n, s: nc.dram_tensor(n, s, F32, kind="Internal").ap()
    gnn_slots = dram("gnn_slots", [M_GNN * P, 1])
    gat_slots = dram("gat_slots", [M_GAT * P, 1])
    gnn_table = dram("gnn_table", [NP, D])
    gat_table = dram("gat_table", [NP, ROW])
    x1 = dram("x1", [NP, D])
    with ExitStack() as c:
        sb = lambda n, s, d=F32: c.enter_context(nc.sbuf_tensor(n, s, d))
        t.iota_f = sb("iota_f", [P, P])
        t.iota_b = sb("iota_b", [P, P], BF16)
        t.ident_f = sb("ident_f", [P, P])
        t.neg_ident_b = sb("neg_ident_b", [P, P], BF16)
        t.ones_f = sb("ones_f", [P, P])
        t.ones_b = sb("ones_b", [P, P], BF16)
        t.zero_b = sb("zero_b", [P, P], BF16)
        t.lower_b = sb("lower_b", [P, P], BF16)
        t.valid = sb("valid", [P, 2])
        t.spare = sb("spare", [P, 4])
        t.dinv = sb("dinv", [P, NB])
        t.gnn_idx = sb("gnn_idx", [P, M_GNN], I32)
        t.gnn_node = sb("gnn_node", [P, M_GNN + CH], BF16)
        t.gnn_block = sb("gnn_block", [1, M_GNN], I32)
        t.gat_idx = sb("gat_idx", [P, M_GAT + CH], I32)
        t.gat_node = sb("gat_node", [P, M_GAT + CH], BF16)
        t.gat_block = sb("gat_block", [1, M_GAT], I32)
        build_constants(nc, t)

        def load_gnn(sp, key, val, done):
            whole, rest = divmod(E_GNN, T_GNN)
            for tile, arr in ((key, a["src"]), (val, a["dst"])):
                sp.dma_start(tile[0:whole, :], arr[0:whole * T_GNN].rearrange("(p t) -> p t", t=T_GNN)).then_inc(done, 16)
                sp.dma_start(tile[whole:whole + 1, 0:rest], arr[whole * T_GNN:E_GNN].rearrange("(p t) -> p t", p=1)).then_inc(done, 16)

        def load_gat(sp, key, val, done):
            for tile, row in ((key, 1), (val, 0)):
                sp.dma_start(tile[:, :], a["L0_ffn_edge_index"][row, :].rearrange("(p t) -> p t", p=P)).then_inc(done, 16)

        sort_edges(nc, t, "gnn_", load_gnn, 4, T_GNN, M_GNN, gnn_slots, t.gnn_idx, t.gnn_node, t.gnn_block, t.dinv)
        sort_edges(nc, t, "gat_", load_gat, 2, T_GAT, M_GAT, gat_slots, t.gat_idx, t.gat_node, t.gat_block, None)
        region = sb("region", [P, NB * D + M_GAT * ROW])
        first, second = region[:, 0:NB * D], region[:, NB * D:NB * D + M_GAT * ROW]
        t.msg = first.rearrange("p (a b) -> p a b", b=D)
        t.yT = first.rearrange("p (a b) -> p a b", b=NP)
        t.h = second[:, 0:NB * D].rearrange("p (a b) -> p a b", b=D)
        t.edge_rows = second.rearrange("p (a b) -> p a b", b=ROW)
        project_input(nc, t, a["x"], a["L0_gnn_W_in"], a["L0_gnn_b_in"])
        gnn_layers(nc, t, a["L0_gnn_Wl"], a["L0_gnn_bl"], a["L0_gnn_Wg"], a["L0_gnn_bg"],
                   a["L0_gnn_gamma"], a["L0_gnn_beta"], gnn_table)
        t.rows = sb("rows", [P, NB, ROW])
        t.adst = sb("adst", [P, NB, HEADS])
        t.top = sb("top", [P, NB, HEADS])
        t.node = sb("node", [P, NB, 2 * HEADS])
        t.sums = sb("sums", [P, NB, ROW])
        t.gate = sb("gate", [P, NB, EXPERTS])
        attention_rows(nc, t, a["x"], a["L0_ffn_W_gat"], a["L0_ffn_att_src"], a["L0_ffn_att_dst"], x1, gat_table)
        attention_max(nc, t, gat_table)
        attention_sum(nc, t)
        attention_gates(nc, t, a["L0_ffn_b_gat"], a["L0_ffn_ln_gamma"], a["L0_ffn_ln_beta"])
        experts(nc, t, second, a["L0_ffn_W1"], a["L0_ffn_b1"], a["L0_ffn_W2"], a["L0_ffn_b2"], x1, out)


def kernel(**inputs):
    import numpy as np
    import concourse.bacc as bacc
    from concourse.bass_utils import run_bass_kernel_spmd

    nc = bacc.Bacc("TRN2", target_bir_lowering=False, num_devices=1)
    arrays, aps = {}, {}
    for name, value in inputs.items():
        value = np.ascontiguousarray(value)
        if name == "x":
            value = np.pad(value, ((0, NP - N), (0, 0)))
        arrays["in_" + name] = value
        aps[name] = nc.dram_tensor("in_" + name, value.shape, mybir.dt.from_np(value.dtype), kind="ExternalInput").ap()
    out = nc.dram_tensor("out", [NP, D], F32, kind="ExternalOutput").ap()
    build(nc, aps, out)
    result = run_bass_kernel_spmd(nc, [arrays], core_ids=[0])
    return result.results[0]["out"][0:N]
```

```python
import concourse.bass as bass
from concourse import mybir
from contextlib import ExitStack

F32 = mybir.dt.float32
BF16 = mybir.dt.bfloat16
I32 = mybir.dt.int32
ALU = mybir.AluOpType
ACT = mybir.ActivationFunctionType
AX = mybir.AxisListType

P = 128
N = 6250
NB = (N + P - 1) // P
NP = NB * P
LAST = N - (NB - 1) * P
D = 256
DC = D // P
LAYERS = 4
GRP = 7
NG = NB // GRP
EXPERTS, HEADS, TOPK = 4, 4, 2
HE = HEADS * EXPERTS
HID = 512
HM = HID // P
ROW = HE + HEADS
PARTS = 3
TROW = ROW + PARTS * HEADS // 2
EPS = 1e-5
NEG = -1e30
E_GNN = 100000
E_GAT = 131072
T_GNN = 784
T_GAT = E_GAT // P
CH = 8
LO_SHIFT = 13
NO_NODE = P
OUTSIDE = 8191
FAR = float(1 << 20)


def tiles_bound(edges, multiple):
    n = edges // P + NB
    return -(-n // multiple) * multiple


M_GNN = tiles_bound(E_GNN, 2 * CH)
M_GAT = tiles_bound(E_GAT, 2 * CH)


SET = 1
DMA_DONE = ("edges_in", "filled", "scattered", "rows_in", "loaded", "weights_in", "table_in", "gathered", "x_in", "x1_out",
            "table_out", "par_in", "acc_in", "acc_out")


class Chain:

    def __init__(self, eng, sem):
        self.eng, self.sem, self.base, self.n = eng, sem, 0, 0

    def link(self, ins):
        ins.then_inc(self.sem, 1)
        self.n += 1
        self.eng.wait_ge(self.sem, SET + self.base + self.n)

    def enter(self, it, per):
        self.start, self.per, self.first = self.base + self.n, per, True
        self.base, self.n = self.start + it * per, 0

    def leave(self, count):
        assert self.n == self.per, (self.n, self.per)
        self.base, self.n = self.start + count * self.per, 0


def semaphores(nc, c, tag):
    used = []

    def make(name):
        used.append(nc.alloc_semaphore(tag + name))
        if not name.startswith(DMA_DONE):
            nc.gpsimd.sem_inc(used[-1], SET)
        return used[-1]

    def clear():
        nc.clear_and_free_semaphores(used)
        nc.all_engine_barrier()

    c.callback(clear)
    return make


def settle(ve, t):
    ve.memset(t.spare[0:1, 3:4], 0.0)


def settle_gpsimd(gp, t, settled, before):
    gp.wait_ge(settled, SET + before)
    gp.tensor_tensor(t.spare[0:1, 0:1], t.spare[0:1, 1:2], t.spare[0:1, 2:3], ALU.add).then_inc(settled, 1)


def load_values(nc, eng, row, most):
    return nc.values_load_multi_w_load_instructions(row, engines=(eng.engine,), min_val=0, max_val=most)[1]


class Tensors:
    pass


def build_constants(nc, t):
    with ExitStack() as c:
        const_step = semaphores(nc, c, "const_")("step")
        nc.all_engine_barrier()
        block = c.enter_context(nc.Block())

        @block.gpsimd
        def _(gp):
            c = Chain(gp, const_step)
            gp.iota(t.iota_f[:, :], pattern=[[1, P]], base=0, channel_multiplier=0,
                    allow_small_or_imprecise_dtypes=True)
            gp.iota(t.iota_b[:, :], pattern=[[1, P]], base=0, channel_multiplier=0,
                    allow_small_or_imprecise_dtypes=True)
            gp.memset(t.ident_f[:, :], 0.0)
            gp.memset(t.neg_ident_b[:, :], 0.0)
            gp.memset(t.ident_b[:, :], 0.0)
            gp.memset(t.ones_f[:, :], 1.0)
            gp.memset(t.spare[:, :], 0.0)
            gp.memset(t.ones_b[:, :], 1.0)
            gp.memset(t.lower_b[:, :], 1.0)
            c.link(gp.memset(t.valid[:, :], 1.0))
            gp.affine_select(out=t.ident_f[:, :], in_=t.ident_f[:, :], compare_op=ALU.not_equal, fill=1.0,
                             base=0, pattern=[[-1, P]], channel_multiplier=1)
            gp.affine_select(out=t.ident_b[:, :], in_=t.ident_b[:, :], compare_op=ALU.not_equal, fill=1.0,
                             base=0, pattern=[[-1, P]], channel_multiplier=1)
            gp.affine_select(out=t.neg_ident_b[:, :], in_=t.neg_ident_b[:, :], compare_op=ALU.not_equal,
                             fill=NEG, base=0, pattern=[[-1, P]], channel_multiplier=1)
            gp.affine_select(out=t.lower_b[:, :], in_=t.lower_b[:, :], compare_op=ALU.is_gt, fill=0.0,
                             base=0, pattern=[[1, P]], channel_multiplier=-1)
            c.link(gp.affine_select(out=t.valid[:, 1:2], in_=t.valid[:, 1:2], compare_op=ALU.is_gt, fill=0.0,
                                    base=LAST, pattern=[[0, 1]], channel_multiplier=-1))
            c.link(gp.memset(t.zero_b[:, :], 0.0))


def sort_edges(nc, t, tag, load_edges, loads, T, M, slots_dram, gather_idx, node_of_slot, block_of_tile, dinv):
    NCH = T // CH
    with ExitStack() as c:
        sb = lambda n, s, d=F32: c.enter_context(nc.sbuf_tensor(tag + n, s, d))
        pb = lambda n, s, d=F32: c.enter_context(nc.psum_tensor(tag + n, s, d))
        sem = semaphores(nc, c, tag)
        key = sb("key", [P, T], I32)
        val = sb("val", [P, T], I32)
        tmp_i = sb("tmp_i", [P, T], I32)
        lo_b = sb("lo_b", [P, T], BF16)
        hi_b = sb("hi_b", [P, T], BF16)
        packed = sb("packed", [P, T + 2 * CH])
        dropped = sb("dropped", [P, T])
        in_block = sb("in_block", [P, T, NB], BF16)
        at_lane = sb("at_lane", [P, 2, CH, P], BF16)
        fill = sb("fill", [P, M])
        counts = sb("counts", [P, NB])
        counts_i = sb("counts_i", [P, NB], I32)
        ntiles = sb("ntiles", [P, NB])
        zeros = sb("zeros", [P, NB])
        end_tile = sb("end_tile", [P, NB])
        end_col = sb("end_col", [NB, 1])
        ended = sb("ended", [NB, M])
        tile_iota = sb("tile_iota", [NB, M])
        run = sb("run", [P, NB])
        ranked = sb("ranked", [P, CH, NB])
        picked = sb("picked", [P, CH, NB])
        pos = sb("pos", [P, CH])
        pos_ring = sb("pos_ring", [P, 2, CH], I32)
        pay_ring = sb("pay_ring", [P, 2, CH])
        G = next(g for g in range(-(-M // P), M + 1) if M % g == 0)
        RT = M // G
        BANK = 512 // RT
        rows = sb("rows", [RT, G, P])
        slot_i = sb("slot_i", [P, M], I32)
        rank_ps = pb("rank_ps", [P, 2, 512])
        total_ps = pb("total_ps", [P, 2, 512])
        hist_ps = pb("hist_ps", [P, 512])
        misc_ps = pb("misc_ps", [P, 3, 512])

        keys_clear = sem("keys_clear")
        edges_in = sem("edges_in")
        dv = sem("dv")
        hi_ready = sem("hi_ready")
        fill_ready = sem("fill_ready")
        filled = sem("filled")
        iota_ready = sem("iota_ready")
        blocks_ready = sem("blocks_ready")
        lane_ready = [sem(f"lane_ready{k}") for k in range(2)]
        lane_used = [sem(f"lane_used{k}") for k in range(2)]
        counted = sem("counted")
        hist_done = sem("hist_done")
        counts_ready = sem("counts_ready")
        end_row_ready = sem("end_row_ready")
        end_col_done = sem("end_col_done")
        ended_ready = sem("ended_ready")
        ended_done = sem("ended_done")
        rank_done = [sem(f"rank_done{k}") for k in range(2)]
        rank_used = [sem(f"rank_used{k}") for k in range(2)]
        pos_ready = [sem(f"pos_ready{k}") for k in range(2)]
        pay_ready = [sem(f"pay_ready{k}") for k in range(2)]
        packed_ready = sem("packed_ready")
        scattered = [sem(f"scattered{k}") for k in range(2)]
        rows_in = sem("rows_in")
        settled = sem("settled")
        turned = sem("turned")
        sqrt_in = sem("sqrt_in")
        sqrt_out = sem("sqrt_out")
        turned_ps = lambda g: [rank_ps, total_ps][g // BANK // 2][:, g // BANK % 2, g % BANK * RT:(g % BANK + 1) * RT]
        nc.all_engine_barrier()
        block = c.enter_context(nc.Block())

        @block.sync
        def _(sp):
            sp.wait_ge(keys_clear, SET + 2)
            load_edges(sp, key, val, edges_in)
            sp.wait_ge(fill_ready, SET + 1)
            sp.dma_start(slots_dram.rearrange("(p m) o -> p (m o)", p=P), fill[:, :]).then_inc(filled, 16)
            for k in range(2):
                sp.wait_ge(scattered[k], 16 * CH * NCH // 2)
            sp.dma_start(rows[:, :, :], slots_dram.rearrange("(g r s) o -> r g (s o)", g=G, s=P)).then_inc(rows_in, 16)

        @block.gpsimd
        def _(gp):
            gp.iota(tile_iota[:, :], pattern=[[1, M]], base=0, channel_multiplier=0,
                    allow_small_or_imprecise_dtypes=True).then_inc(iota_ready, 1)
            gp.wait_ge(filled, 16)
            with gp.Fori(0, NCH // 2) as i:
                for k in range(2):
                    gp.wait_ge(pos_ready[k], SET + i + 1)
                    gp.wait_ge(pay_ready[k], SET + i + 1)
                    settle_gpsimd(gp, t, settled, i * 2 + k)
                    for j in range(CH):
                        gp.indirect_dma_start(
                            out=slots_dram, out_offset=bass.IndirectOffsetOnAxis(ap=pos_ring[:, k, j:j + 1], axis=0),
                            in_=pay_ring[:, k, j:j + 1], in_offset=None,
                            bounds_check=M * P - 1, oob_is_err=False).then_inc(scattered[k], 16)

        @block.scalar
        def _(act):
            if dinv is not None:
                act.wait_ge(sqrt_in, SET + 1)
                nc.scalar.activation(dinv[:, :], dinv[:, :], ACT.Sqrt).then_inc(sqrt_out, 1)
            act.wait_ge(packed_ready, SET + 1)

            def payload(col, k):
                nc.scalar.activation(pay_ring[:, k, :], packed[:, bass.ds(col, CH)], ACT.Copy).then_inc(pay_ready[k], 1)

            for k in range(2):
                payload(k * CH, k)
            with act.Fori(0, NCH // 2) as i:
                for k in range(2):
                    act.wait_ge(scattered[k], (i + 1) * (16 * CH))
                    payload((i + 1) * (2 * CH) + k * CH, k)

        @block.tensor
        def _(pe):
            pe.wait_ge(hi_ready, SET + 1)
            if dinv is not None:
                nc.tensor.matmul(hist_ps[:, 0:NB], t.zero_b[:, :], in_block[:, 0, :], start=True, stop=False)
                with pe.Fori(0, NCH // 2) as i:
                    for k in range(2):
                        pe.wait_ge(lane_ready[k], SET + i + 1)
                        for j in range(CH):
                            last = nc.tensor.matmul(hist_ps[:, 0:NB], at_lane[:, k, j, :],
                                                    in_block[:, bass.ds(i * (2 * CH) + (k * CH + j), 1), :].rearrange("p a b -> p (a b)"),
                                                    start=False, stop=False)
                        last.then_inc(lane_used[k], 1)
                nc.tensor.matmul(hist_ps[:, 0:NB], t.zero_b[:, :], in_block[:, 0, :], start=False, stop=True).then_inc(counted, 1)
            else:
                pe.wait_ge(blocks_ready, SET + NCH)
                nc.tensor.matmul(hist_ps[:, 0:NB], t.zero_b[:, :], in_block[:, 0, :], start=True, stop=False)
                with pe.Fori(0, NCH) as i:
                    for j in range(CH):
                        nc.tensor.matmul(hist_ps[:, 0:NB], t.ones_b[:, :],
                                                in_block[:, bass.ds(i * CH + j, 1), :].rearrange("p a b -> p (a b)"),
                                                start=False, stop=False)
                nc.tensor.matmul(hist_ps[:, 0:NB], t.zero_b[:, :], in_block[:, 0, :], start=False, stop=True).then_inc(counted, 1)
            if dinv is not None:
                pe.wait_ge(counts_ready, SET + 1)
                nc.tensor.matmul(misc_ps[:, 0, 0:NB], t.ones_f[:, :], counts[:, :], start=True, stop=True).then_inc(hist_done, 1)
            pe.wait_ge(end_row_ready, SET + 1)
            nc.tensor.matmul(misc_ps[0:NB, 1, 0:1], end_tile[0:1, :], t.ones_f[0:1, 0:1], start=True, stop=True).then_inc(end_col_done, 1)
            pe.wait_ge(ended_ready, SET + 1)
            for h in range(0, M, 512):
                w = min(512, M - h)
                last = nc.tensor.matmul(misc_ps[0:1, h // 512, 0:w], t.ones_f[0:NB, 0:1], ended[:, h:h + w], start=True, stop=True)
            last.then_inc(ended_done, 1)
            with pe.Fori(0, NCH // 2) as i:
                for k in range(2):
                    pe.wait_ge(rank_used[k], SET + i)
                    c0 = i * (2 * CH) + k * CH
                    one = lambda j: in_block[:, bass.ds(c0 + j, 1), :]
                    nc.tensor.matmul(rank_ps[:, k, 0:CH * NB].rearrange("p (a b) -> p a b", b=NB), t.lower_b[:, :],
                                     in_block[:, bass.ds(c0, CH), :], start=True, stop=False)
                    for j in range(CH - 1):
                        nc.tensor.matmul(rank_ps[:, k, (j + 1) * NB:CH * NB].rearrange("p (a b) -> p a b", b=NB),
                                         t.ones_b[:, :], one(j).to_broadcast([P, CH - 1 - j, NB]),
                                         start=False, stop=(j == CH - 2))
                    for j in range(CH):
                        last = nc.tensor.matmul(total_ps[:, k, 0:NB], t.ones_b[:, :], one(j).rearrange("p a b -> p (a b)"),
                                                start=(j == 0), stop=(j == CH - 1))
                    last.then_inc(rank_done[k], 1)
            pe.wait_ge(rows_in, 16)
            for g in range(G):
                last = nc.tensor.transpose(turned_ps(g), rows[:, g, :], t.ident_f[0:RT, 0:RT])
            last.then_inc(turned, 1)

        @block.vector
        def _(ve):
            v = nc.vector
            ch = Chain(ve, dv)
            v.memset(key[:, :], OUTSIDE).then_inc(keys_clear, 1)
            v.memset(val[:, :], 0).then_inc(keys_clear, 1)
            v.memset(packed[:, :], 0.0)
            ch.link(v.memset(zeros[:, :], 0.0))
            v.memset(gather_idx[:, :], 0)
            v.memset(node_of_slot[:, :], float(NO_NODE))
            v.memset(fill[:, :], float(NO_NODE << LO_SHIFT)).then_inc(fill_ready, 1)
            ve.wait_ge(edges_in, 16 * loads)
            ch.link(v.tensor_scalar(val[:, :], val[:, :], float(N - 1), None, ALU.min))
            ch.link(v.tensor_scalar(tmp_i[:, :], key[:, :], 7, None, ALU.arith_shift_right))
            ch.link(v.tensor_copy(hi_b[:, :], tmp_i[:, :]))
            ch.link(v.tensor_scalar(tmp_i[:, :], key[:, :], P - 1, None, ALU.bitwise_and))
            ch.link(v.tensor_copy(lo_b[:, :], tmp_i[:, :]))
            v.scalar_tensor_tensor(packed[:, 0:T], tmp_i[:, :], float(1 << LO_SHIFT), val[:, :],
                                   ALU.mult, ALU.add).then_inc(packed_ready, 1)
            ch.link(v.tensor_scalar(dropped[:, :], key[:, :], float(NP), FAR, ALU.is_ge, ALU.mult))
            with ve.Fori(0, NCH) as i:
                v.tensor_tensor(in_block[:, bass.ds(i * CH, CH), :],
                                hi_b[:, bass.ds(i * CH, CH)].unsqueeze(2).to_broadcast([P, CH, NB]),
                                t.iota_b[:, 0:NB].unsqueeze(1).to_broadcast([P, CH, NB]), ALU.is_equal).then_inc(blocks_ready, 1)
            ve.wait_ge(blocks_ready, SET + NCH)
            v.memset(ranked[:, 0, 0:1], 0.0).then_inc(hi_ready, 1)
            if dinv is not None:
                with ve.Fori(0, NCH // 2) as i:
                    for k in range(2):
                        ve.wait_ge(lane_used[k], SET + i)
                        v.tensor_tensor(at_lane[:, k, :, :],
                                        lo_b[:, bass.ds(i * (2 * CH) + k * CH, CH)].unsqueeze(2).to_broadcast([P, CH, P]),
                                        t.iota_b[:, :].unsqueeze(1).to_broadcast([P, CH, P]), ALU.is_equal).then_inc(lane_ready[k], 1)
                ve.wait_ge(counted, SET + 1)
                v.tensor_copy(counts[:, :], hist_ps[:, 0:NB]).then_inc(counts_ready, 1)
                ve.wait_ge(counts_ready, SET + 1)
                v.tensor_scalar(dinv[:, :], counts[:, :], 1.0, None, ALU.add).then_inc(sqrt_in, 1)
                ve.wait_ge(hist_done, SET + 1)
                ch.link(v.tensor_copy(counts_i[:, :], misc_ps[:, 0, 0:NB]))
                ve.wait_ge(sqrt_out, SET + 1)
                ch.link(v.reciprocal(dinv[:, :], dinv[:, :]))
                ch.link(v.tensor_scalar(counts[:, :], counts[:, :], 1.0, -0.5, ALU.add, ALU.mult))
                ch.link(v.tensor_tensor(counts[:, :], counts[:, :], dinv[:, :], ALU.mult))
                ch.link(v.tensor_tensor(counts[:, :], counts[:, :], dinv[:, :], ALU.mult))
                ch.link(v.scalar_tensor_tensor(dinv[:, :], counts[:, :], 1.5, dinv[:, :], ALU.add, ALU.mult))
            else:
                ve.wait_ge(counted, SET + 1)
                ch.link(v.tensor_copy(counts_i[:, :], hist_ps[:, 0:NB]))
            ch.link(v.tensor_scalar(counts_i[:, :], counts_i[:, :], float(P - 1), None, ALU.add))
            ch.link(v.tensor_scalar(counts_i[:, :], counts_i[:, :], 7, None, ALU.arith_shift_right))
            ch.link(v.tensor_copy(ntiles[:, :], counts_i[:, :]))
            v.tensor_tensor_scan(end_tile[:, :], ntiles[:, :], zeros[:, :], 0.0, ALU.add, ALU.add).then_inc(end_row_ready, 1)
            ve.wait_ge(end_row_ready, SET + 1)
            ch.link(v.tensor_tensor(run[:, :], end_tile[:, :], ntiles[:, :], ALU.subtract))
            ch.link(v.tensor_scalar(run[:, :], run[:, :], float(P), None, ALU.mult))
            ve.wait_ge(end_col_done, SET + 1)
            ch.link(v.tensor_copy(end_col[:, :], misc_ps[0:NB, 1, 0:1]))
            ve.wait_ge(iota_ready, SET + 1)
            v.tensor_scalar(ended[:, :], tile_iota[:, :], end_col[:, 0:1], None, ALU.is_ge).then_inc(ended_ready, 1)
            ve.wait_ge(ended_done, SET + 1)
            for h in range(0, M, 512):
                w = min(512, M - h)
                last = v.tensor_scalar(block_of_tile[:, h:h + w], misc_ps[0:1, h // 512, 0:w], float(NB - 1), None, ALU.min)
            ch.link(last)

            def place(i, first):
                for k in range(2):
                    c0 = i * (2 * CH) + k * CH
                    ve.wait_ge(rank_done[k], SET + i + 1)
                    ch.link(v.tensor_tensor(ranked[:, :, :], rank_ps[:, k, 0:CH * NB].rearrange("p (a b) -> p a b", b=NB),
                                            run[:, :].unsqueeze(1).to_broadcast([P, CH, NB]), ALU.add))
                    v.tensor_tensor(run[:, :], run[:, :], total_ps[:, k, 0:NB], ALU.add).then_inc(rank_used[k], 1)
                    ve.wait_ge(rank_used[k], SET + i + 1)
                    ch.link(v.tensor_tensor(picked[:, :, :], ranked[:, :, :], in_block[:, bass.ds(c0, CH), :], ALU.mult))
                    ch.link(v.tensor_reduce(pos[:, :], picked[:, :, :], AX.X, ALU.add))
                    if not first:
                        ve.wait_ge(scattered[k], i * (16 * CH))
                    v.tensor_tensor(pos_ring[:, k, :], pos[:, :], dropped[:, bass.ds(c0, CH)], ALU.add).then_inc(pos_ready[k], 1)

            place(0, True)
            with ve.Fori(1, NCH // 2) as i:
                ch.enter(i - 1, 6)
                place(i, False)
            ch.leave(NCH // 2 - 1)
            ve.wait_ge(turned, SET + 1)
            for g in range(G):
                last = v.tensor_copy(slot_i[:, g * RT:(g + 1) * RT], turned_ps(g))
            ch.link(last)
            v.tensor_scalar(gather_idx[:, 0:M], slot_i[:, 0:M], (1 << LO_SHIFT) - 1, None, ALU.bitwise_and)
            ch.link(v.tensor_scalar(slot_i[:, 0:M], slot_i[:, 0:M], LO_SHIFT, None, ALU.arith_shift_right))
            ch.link(v.tensor_copy(node_of_slot[:, 0:M], slot_i[:, 0:M]))


def group_statistics(ve, v, t, ch, src, s, var_ready, std_ready, groups_before):
    settle(ve, t)
    for j in range(GRP):
        last = v.bn_stats(s.st[:, j, :], src[:, j, :])
    ch.link(last)
    settle(ve, t)
    for j in range(GRP):
        last = v.bn_aggr(s.mv[:, j, :], s.st[:, j, :])
    ch.link(last)
    v.tensor_scalar(s.var[:, :], s.mv[:, :, 1], EPS, None, ALU.add).then_inc(var_ready, 1)
    ve.wait_ge(std_ready, SET + groups_before + 1)
    ch.link(v.reciprocal(s.rstd[:, :], s.std[:, :]))
    ch.link(v.scalar_tensor_tensor(s.var[:, :], s.var[:, :], -0.5, s.rstd[:, :], ALU.mult, ALU.mult))
    ch.link(v.tensor_tensor(s.var[:, :], s.var[:, :], s.rstd[:, :], ALU.mult))
    ch.link(v.scalar_tensor_tensor(s.rstd[:, :], s.var[:, :], 1.5, s.rstd[:, :], ALU.add, ALU.mult))


STAT_LINKS = 6


def statistics_tensors(nc, c, tag):
    s = Tensors()
    s.st = c.enter_context(nc.sbuf_tensor(tag + "st", [P, GRP, 6], F32))
    s.mv = c.enter_context(nc.sbuf_tensor(tag + "mv", [P, GRP, 2], F32))
    s.var = c.enter_context(nc.sbuf_tensor(tag + "var", [P, GRP], F32))
    s.std = c.enter_context(nc.sbuf_tensor(tag + "std", [P, GRP], F32))
    s.rstd = c.enter_context(nc.sbuf_tensor(tag + "rstd", [P, GRP], F32))
    return s


def project_input(nc, t, x, W_in, b_in):
    with ExitStack() as c:
        sb = lambda n, s, d=F32: c.enter_context(nc.sbuf_tensor("in_" + n, s, d))
        sem = semaphores(nc, c, "in_")
        w = sb("w", [P, DC, D])
        b = sb("b", [1, D])
        norm = sb("norm", [P, GRP, D])
        normT = sb("normT", [P, GRP, DC, P])
        s = statistics_tensors(nc, c, "in_")
        ps = c.enter_context(nc.psum_tensor("in_ps", [P, 8, 512], F32))
        loaded, dv, var_ready, std_ready, norm_ready, turned, turned_sb, made, stored = (
            sem(n) for n in ("loaded", "dv", "var_ready", "std_ready", "norm_ready", "turned", "turned_sb", "made", "stored"))
        half = lambda lo, j: ps[:, lo + j // 2, (j % 2) * D:(j % 2 + 1) * D]
        both = lambda lo: ps[:, lo:lo + 4, :].rearrange("p a b -> p (a b)")[:, 0:GRP * D]
        nc.all_engine_barrier()
        block = c.enter_context(nc.Block())

        @block.sync
        def _(sp):
            sp.dma_start(t.h[:, :, :], x.rearrange("(b p) d -> p b d", p=P)).then_inc(loaded, 16)
            sp.dma_start(w[:, :, :], W_in.rearrange("(c p) d -> p c d", p=P)).then_inc(loaded, 16)
            sp.dma_start(b[:, :], b_in.rearrange("(o d) -> o d", o=1)).then_inc(loaded, 16)

        @block.vector
        def _(ve):
            v = nc.vector
            ch = Chain(ve, dv)
            ve.wait_ge(loaded, 48)
            with ve.Fori(0, NG) as i:
                ch.enter(i, STAT_LINKS)
                xg = t.h[:, bass.ds(i * GRP, GRP), :]
                group_statistics(ve, v, t, ch, xg, s, var_ready, std_ready, i)
                ve.wait_ge(turned, SET + i)
                for j in range(GRP):
                    last = v.tensor_scalar(norm[:, j, :], xg[:, j, :], s.mv[:, j, 0:1], s.rstd[:, j:j + 1],
                                           ALU.subtract, ALU.mult)
                last.then_inc(norm_ready, 1)
            ch.leave(NG)

        @block.scalar
        def _(act):
            with act.Fori(0, NG) as i:
                act.wait_ge(var_ready, SET + i + 1)
                nc.scalar.activation(s.std[:, :], s.var[:, :], ACT.Sqrt).then_inc(std_ready, 1)
                act.wait_ge(turned, SET + i + 1)
                nc.scalar.activation(normT[:, :, :, :].rearrange("p a b c -> p (a b c)"), both(0), ACT.Copy).then_inc(turned_sb, 1)
                act.wait_ge(made, SET + i + 1)
                nc.scalar.activation(t.h[:, bass.ds(i * GRP, GRP), :].rearrange("p a b -> p (a b)"), both(4), ACT.Copy).then_inc(stored, 1)

        @block.tensor
        def _(pe):
            pe.wait_ge(loaded, 48)
            with pe.Fori(0, NG) as i:
                pe.wait_ge(norm_ready, SET + i + 1)
                pe.wait_ge(turned_sb, SET + i)
                for j in range(GRP):
                    for k in range(DC):
                        last = nc.tensor.transpose(half(0, j)[:, k * P:(k + 1) * P], norm[:, j, k * P:(k + 1) * P], t.ident_f[:, :])
                last.then_inc(turned, 1)
                pe.wait_ge(turned_sb, SET + i + 1)
                pe.wait_ge(stored, SET + i)
                for j in range(GRP):
                    for k in range(DC):
                        nc.tensor.matmul(half(4, j), normT[:, j, k, :], w[:, k, :], start=(k == 0), stop=False)
                    last = nc.tensor.matmul(half(4, j), t.ones_f[0:1, :], b[0:1, :], start=False, stop=True)
                last.then_inc(made, 1)


def gnn_layers(nc, t, Wl, bl, Wg, bg, gamma, beta, table):
    IT = M_GNN // (2 * CH)
    with ExitStack() as c:
        sb = lambda n, s, d=F32: c.enter_context(nc.sbuf_tensor("g_" + n, s, d))
        sem = semaphores(nc, c, "g_")
        two = lambda n: [sem(f"{n}{k}") for k in range(2)]
        msg = t.msg
        wl = sb("wl", [P, DC, D])
        wg = sb("wg", [P, DC, D])
        gam = sb("gam", [P, D])
        bet = sb("bet", [P, D])
        bias_l = sb("bias_l", [1, D])
        bias_g = sb("bias_g", [1, D])
        bias = sb("bias", [1, D])
        mean_row = sb("mean_row", [1, D])
        mean_col = sb("mean_col", [P, DC])
        rows = sb("rows", [P, GRP, D])
        idx_ring = sb("idx_ring", [P, 2, CH], I32)
        got = sb("got", [P, 2, CH, D])
        hot = sb("hot", [P, 2, CH, P])
        gotf = got[:, :, :, :].rearrange("p a b c -> p (a b c)")
        zin = gotf[:, 0:GRP * D].rearrange("p (a b) -> p a b", b=D)
        zT = gotf[:, GRP * D:2 * GRP * D].rearrange("p (a b c) -> p a b c", b=DC, c=P)
        s = statistics_tensors(nc, c, "g_")
        ps = c.enter_context(nc.psum_tensor("g_ps", [P, 8, 512], F32))
        half = lambda lo, j: ps[:, lo + j // 2, (j % 2) * D:(j % 2 + 1) * D]
        both = lambda lo: ps[:, lo:lo + 4, :].rearrange("p a b -> p (a b)")[:, 0:GRP * D]
        (weights_in, dv, msg_clear, table_rows, table_in, sum_done, mean_row_ready, mean_col_done,
         mean_col_ready, ctx_done, bias_ready, zin_ready, turned, turned_sb, made, relu_done, relu_used, var_ready,
         std_ready) = (sem(n) for n in (
             "weights_in", "dv", "msg_clear", "table_rows", "table_in", "sum_done", "mean_row_ready",
             "mean_col_done", "mean_col_ready", "ctx_done", "bias_ready", "zin_ready", "turned", "turned_sb", "made",
             "relu_done", "relu_used", "var_ready", "std_ready"))
        settled = sem("settled")
        idx_ready, gathered, hot_ready, summed, added = (two(n) for n in ("idx_ready", "gathered", "hot_ready", "summed", "added"))
        nc.all_engine_barrier()
        block = c.enter_context(nc.Block())
        table_v = table.rearrange("(b p) d -> p b d", p=P)

        @block.sync
        def _(sp):
            with sp.Fori(0, LAYERS) as l:
                sp.wait_ge(relu_used, SET + l * NG)
                one = bass.ds(l, 1)
                sp.dma_start(wl[:, :, :], Wl[one, :, :].rearrange("l (c p) d -> p (l c) d", p=P)).then_inc(weights_in, 16)
                sp.dma_start(wg[:, :, :], Wg[one, :, :].rearrange("l (c p) d -> p (l c) d", p=P)).then_inc(weights_in, 16)
                sp.dma_start(gam[:, :], gamma[one, :].to_broadcast([P, D])).then_inc(weights_in, 16)
                sp.dma_start(bet[:, :], beta[one, :].to_broadcast([P, D])).then_inc(weights_in, 16)
                sp.dma_start(bias_l[:, :], bl[one, :]).then_inc(weights_in, 16)
                sp.dma_start(bias_g[:, :], bg[one, :]).then_inc(weights_in, 16)
                with sp.Fori(0, NG) as i:
                    sp.wait_ge(table_rows, SET + l * NG + i + 1)
                    sp.dma_start(table_v[:, bass.ds(i * GRP, GRP), :], rows[:, :, :]).then_inc(table_in, 16)

        @block.gpsimd
        def _(gp):
            with gp.Fori(0, LAYERS) as l:
                gp.wait_ge(relu_used, SET + l * NG)
                settle_gpsimd(gp, t, settled, l * (2 + 2 * IT))
                gp.memset(msg[:, :, :], 0.0).then_inc(msg_clear, 1)
                gp.wait_ge(table_in, (l + 1) * (16 * NG))
                settle_gpsimd(gp, t, settled, l * (2 + 2 * IT) + 1)
                with gp.Fori(0, IT) as i:
                    for k in range(2):
                        gp.wait_ge(idx_ready[k], SET + l * (IT + 1) + i + 1)
                        gp.wait_ge(summed[k], SET + l * IT + i)
                        settle_gpsimd(gp, t, settled, l * (2 + 2 * IT) + (i * 2 + k + 2))
                        for j in range(CH):
                            gp.indirect_dma_start(
                                out=got[:, k, j, :], out_offset=None, in_=table,
                                in_offset=bass.IndirectOffsetOnAxis(ap=idx_ring[:, k, j:j + 1], axis=0)).then_inc(gathered[k], 16)

        @block.scalar
        def _(act):
            def indices(col, k):
                nc.scalar.activation(idx_ring[:, k, :], t.gnn_idx[:, bass.ds(col, CH)], ACT.Copy).then_inc(idx_ready[k], 1)

            with act.Fori(0, LAYERS) as l:
                act.wait_ge(relu_used, SET + l * NG)
                with act.Fori(0, NG) as i:
                    for j in range(GRP):
                        b = i * GRP + j
                        last = nc.scalar.activation(rows[:, j, :], t.h[:, bass.ds(b, 1), :].rearrange("p a b -> p (a b)"),
                                                    ACT.Copy, scale=t.dinv[:, bass.ds(b, 1)])
                    last.then_inc(table_rows, 1)
                    act.wait_ge(table_in, (l * NG + i + 1) * 16)
                for k in range(2):
                    indices(k * CH, k)
                with act.Fori(0, IT) as i:
                    for k in range(2):
                        act.wait_ge(gathered[k], (l * IT + i + 1) * (16 * CH))
                        indices((i + 1) * (2 * CH) + k * CH, k)
                with act.Fori(0, NG) as i:
                    g = l * NG + i
                    act.wait_ge(turned, SET + g + 1)
                    nc.scalar.activation(zT.rearrange("p a b c -> p (a b c)"), both(0), ACT.Copy).then_inc(turned_sb, 1)
                    act.wait_ge(made, SET + g + 1)
                    act.wait_ge(relu_used, SET + g)
                    nc.scalar.activation(rows[:, :, :].rearrange("p a b -> p (a b)"), both(4), ACT.Relu).then_inc(relu_done, 1)
                    act.wait_ge(var_ready, SET + g + 1)
                    nc.scalar.activation(s.std[:, :], s.var[:, :], ACT.Sqrt).then_inc(std_ready, 1)

        @block.tensor
        def _(pe):
            with pe.Fori(0, LAYERS) as l:
                pe.wait_ge(relu_used, SET + l * NG)
                flat = lambda b: t.h[:, b, :].rearrange("p a b -> p (a b)")
                nc.tensor.matmul(ps[0:1, 0, 0:D], t.valid[:, 0:1], t.h[:, 0, :], start=True, stop=False)
                with pe.Fori(1, NB - 1) as b:
                    nc.tensor.matmul(ps[0:1, 0, 0:D], t.valid[:, 0:1], flat(bass.ds(b, 1)), start=False, stop=False)
                nc.tensor.matmul(ps[0:1, 0, 0:D], t.valid[:, 1:2], t.h[:, NB - 1, :], start=False, stop=True).then_inc(sum_done, 1)
                pe.wait_ge(mean_row_ready, SET + l + 1)
                for k in range(DC):
                    last = nc.tensor.matmul(ps[:, 1, k:k + 1], mean_row[0:1, k * P:(k + 1) * P], t.ones_f[0:1, 0:1], start=True, stop=True)
                last.then_inc(mean_col_done, 1)
                pe.wait_ge(mean_col_ready, SET + l + 1)
                pe.wait_ge(weights_in, (l + 1) * (16 * 6))
                for k in range(DC):
                    last = nc.tensor.matmul(ps[0:1, 0, 0:D], mean_col[:, k:k + 1], wg[:, k, :], start=(k == 0), stop=(k == DC - 1))
                last.then_inc(ctx_done, 1)
                with pe.Fori(0, IT) as i:
                    for k in range(2):
                        n = l * IT + i
                        pe.wait_ge(gathered[k], (n + 1) * (16 * CH))
                        pe.wait_ge(hot_ready[k], SET + (l * (IT + 1 - k) + i) + 1)
                        pe.wait_ge(added[k], SET + n)
                        for j in range(CH):
                            last = nc.tensor.matmul(half(4 * k, j), hot[:, k, j, :], got[:, k, j, :], start=True, stop=True)
                        last.then_inc(summed[k], 1)
                with pe.Fori(0, NG) as i:
                    g = l * NG + i
                    pe.wait_ge(zin_ready, SET + g + 1)
                    pe.wait_ge(turned_sb, SET + g)
                    for j in range(GRP):
                        for k in range(DC):
                            last = nc.tensor.transpose(half(0, j)[:, k * P:(k + 1) * P], zin[:, j, k * P:(k + 1) * P], t.ident_f[:, :])
                    last.then_inc(turned, 1)
                    pe.wait_ge(turned_sb, SET + g + 1)
                    pe.wait_ge(relu_done, SET + g)
                    for j in range(GRP):
                        for k in range(DC):
                            nc.tensor.matmul(half(4, j), zT[:, j, k, :], wl[:, k, :], start=(k == 0), stop=False)
                        last = nc.tensor.matmul(half(4, j), t.ones_f[0:1, :], bias[0:1, :], start=False, stop=True)
                    last.then_inc(made, 1)

        @block.vector
        def _(ve):
            v = nc.vector
            ch = Chain(ve, dv)
            PER_LAYER = 1 + 2 * (CH - 1) * IT + NG * (STAT_LINKS + 1)

            def build_hot(col, k):
                v.tensor_tensor(hot[:, k, :, :], t.gnn_node[:, bass.ds(col, CH)].unsqueeze(2).to_broadcast([P, CH, P]),
                                t.iota_f[:, :].unsqueeze(1).to_broadcast([P, CH, P]), ALU.is_equal).then_inc(hot_ready[k], 1)

            with ve.Fori(0, LAYERS) as l:
                base = l * PER_LAYER
                ve.wait_ge(sum_done, SET + l + 1)
                v.tensor_scalar(mean_row[:, :], ps[0:1, 0, 0:D], 1.0 / N, None, ALU.mult).then_inc(mean_row_ready, 1)
                ve.wait_ge(mean_col_done, SET + l + 1)
                v.tensor_copy(mean_col[:, :], ps[:, 1, 0:DC]).then_inc(mean_col_ready, 1)
                ve.wait_ge(weights_in, (l + 1) * (16 * 6))
                ve.wait_ge(ctx_done, SET + l + 1)
                ch.base, ch.n = base, 0
                ch.link(v.tensor_tensor(bias[:, :], ps[0:1, 0, 0:D], bias_l[:, :], ALU.add))
                v.tensor_tensor(bias[:, :], bias[:, :], bias_g[:, :], ALU.add).then_inc(bias_ready, 1)
                ve.wait_ge(msg_clear, SET + l + 1)
                build_hot(0, 0)
                with ve.Fori(0, IT) as i:
                    ch.base, ch.n = base + 1 + i * (2 * (CH - 1)), 0
                    for k in range(2):
                        other = 1 - k
                        ve.wait_ge(summed[other], SET + l * IT + i + k)
                        build_hot(i * (2 * CH) + (k + 1) * CH, other)
                        at = load_values(nc, ve, t.gnn_block[0:1, bass.ds(i * (2 * CH) + k * CH, CH)], NB - 1)
                        ve.wait_ge(summed[k], SET + l * IT + i + 1)
                        for j in range(CH):
                            m = msg[:, bass.ds(at[j], 1), :].rearrange("p a b -> p (a b)")
                            ins = v.tensor_tensor(m, m, half(4 * k, j), ALU.add)
                            if j < CH - 1:
                                ch.link(ins)
                        ins.then_inc(added[k], 1)
                        ve.wait_ge(added[k], SET + l * IT + i + 1)
                tail = base + 1 + 2 * (CH - 1) * IT

                def make_zin(i):
                    for j in range(GRP):
                        one = bass.ds(i * GRP + j, 1)
                        f = lambda x: x[:, one, :].rearrange("p a b -> p (a b)")
                        last = v.scalar_tensor_tensor(zin[:, j, :], f(msg), t.dinv[:, one], f(t.h), ALU.mult, ALU.add)
                    last.then_inc(zin_ready, 1)

                def norm_group(i):
                    ch.base, ch.n = tail + i * (STAT_LINKS + 1), 0
                    ve.wait_ge(relu_done, SET + l * NG + i + 1)
                    group_statistics(ve, v, t, ch, rows, s, var_ready, std_ready, l * NG + i)
                    for j in range(GRP):
                        last = v.scalar_tensor_tensor(rows[:, j, :], rows[:, j, :], s.mv[:, j, 0:1], gam[:, :], ALU.subtract, ALU.mult)
                    ch.link(last)
                    for j in range(GRP):
                        last = v.scalar_tensor_tensor(t.h[:, bass.ds(i * GRP + j, 1), :].rearrange("p a b -> p (a b)"), rows[:, j, :],
                                                      s.rstd[:, j:j + 1], bet[:, :], ALU.mult, ALU.add)
                    last.then_inc(relu_used, 1)

                make_zin(0)
                with ve.Fori(0, NG - 1) as i:
                    ve.wait_ge(turned, SET + l * NG + i + 1)
                    make_zin(i + 1)
                    norm_group(i)
                norm_group(NG - 1)
                ve.wait_ge(relu_used, SET + (l + 1) * NG)


def attention_rows(nc, t, x, W_gat, att_src, att_dst, x1, table):
    with ExitStack() as c:
        sb = lambda n, s, d=F32: c.enter_context(nc.sbuf_tensor("a_" + n, s, d))
        sem = semaphores(nc, c, "a_")
        xg = sb("xg", [P, GRP, D])
        w = sb("w", [P, DC, HE])
        att = sb("att", [P, 2, HE])
        norm = sb("norm", [P, GRP, D])
        normT = sb("normT", [P, GRP, DC, P])
        prod = sb("prod", [P, 2, GRP, HE])
        rest = sb("rest", [P, GRP, HEADS])
        s = statistics_tensors(nc, c, "a_")
        ps = c.enter_context(nc.psum_tensor("a_ps", [P, 8, 512], F32))
        (weights_in, x_in, x1_ready, x1_out, dv, var_ready, std_ready, norm_ready, turned, turned_sb, made, rows_made,
         table_out) = (sem(n) for n in ("weights_in", "x_in", "x1_ready", "x1_out", "dv", "var_ready", "std_ready",
                                        "norm_ready", "turned", "turned_sb", "made", "rows_made", "table_out"))
        half = lambda lo, j: ps[:, lo + j // 2, (j % 2) * D:(j % 2 + 1) * D]
        both = lambda lo: ps[:, lo:lo + 4, :].rearrange("p a b -> p (a b)")[:, 0:GRP * D]
        nc.all_engine_barrier()
        block = c.enter_context(nc.Block())
        group = lambda i: bass.ds(i * GRP, GRP)

        @block.sync
        def _(sp):
            sp.dma_start(w[:, :, :], W_gat.rearrange("(c p) d -> p c d", p=P)).then_inc(weights_in, 16)
            sp.dma_start(att[:, 0, :], att_src.rearrange("(o a) b -> o (a b)", o=1).to_broadcast([P, HE])).then_inc(weights_in, 16)
            sp.dma_start(att[:, 1, :], att_dst.rearrange("(o a) b -> o (a b)", o=1).to_broadcast([P, HE])).then_inc(weights_in, 16)
            with sp.Fori(0, NG) as i:
                sp.wait_ge(x1_ready, SET + i)
                sp.dma_start(xg[:, :, :], x.rearrange("(b p) d -> p b d", p=P)[:, group(i), :]).then_inc(x_in, 16)
            sp.wait_ge(x1_ready, SET + NG)
            sp.dma_start(x1.rearrange("(b p) d -> p b d", p=P), t.h[:, :, :]).then_inc(x1_out, 16)
            sp.wait_ge(rows_made, SET + NG)
            sp.dma_start(table.rearrange("(b p) d -> p b d", p=P), t.rows[:, :, :]).then_inc(table_out, 16)
            sp.wait_ge(x1_out, 16)
            sp.wait_ge(table_out, 16)

        @block.vector
        def _(ve):
            v = nc.vector
            ch = Chain(ve, dv)
            ve.wait_ge(weights_in, 48)
            with ve.Fori(0, NG) as i:
                ch.enter(i, STAT_LINKS + 2 + 2 * (PARTS - 1))
                h = t.h[:, group(i), :]
                ve.wait_ge(x_in, (i + 1) * 16)
                v.tensor_tensor(h, h, xg[:, :, :], ALU.add).then_inc(x1_ready, 1)
                ve.wait_ge(x1_ready, SET + i + 1)
                group_statistics(ve, v, t, ch, h, s, var_ready, std_ready, i)
                ve.wait_ge(turned, SET + i)
                for j in range(GRP):
                    last = v.tensor_scalar(norm[:, j, :], h[:, j, :], s.mv[:, j, 0:1], s.rstd[:, j:j + 1],
                                           ALU.subtract, ALU.mult)
                last.then_inc(norm_ready, 1)
                ve.wait_ge(made, SET + i + 1)
                hp = ps[:, 4, 0:GRP * HE].rearrange("p (a b) -> p a b", b=HE)
                v.tensor_copy(t.rows[:, group(i), 0:HE], hp)
                for k in range(2):
                    last = v.tensor_tensor(prod[:, k, :, :], hp, att[:, k, :].unsqueeze(1).to_broadcast([P, GRP, HE]), ALU.mult)
                ch.link(last)
                per_head = lambda k: prod[:, k, :, :].rearrange("p a (b c) -> p a b c", c=EXPERTS)
                v.tensor_reduce(t.rows[:, group(i), HE:ROW], per_head(0), AX.X, ALU.add)
                ch.link(v.tensor_reduce(t.adst[:, group(i), :], per_head(1), AX.X, ALU.add))
                settle(ve, t)
                v.tensor_copy(rest[:, :, :], t.rows[:, group(i), HE:ROW])
                for q in range(PARTS):
                    part = t.rows_b[:, group(i), 2 * ROW + q * HEADS:2 * ROW + (q + 1) * HEADS]
                    ins = v.tensor_copy(part, t.rows[:, group(i), HE:ROW]) if q == 0 else v.tensor_copy(part, rest[:, :, :])
                    if q < PARTS - 1:
                        ch.link(ins)
                        ch.link(v.tensor_tensor(rest[:, :, :], rest[:, :, :], part, ALU.subtract))
                ins.then_inc(rows_made, 1)
            ch.leave(NG)

        @block.scalar
        def _(act):
            with act.Fori(0, NG) as i:
                act.wait_ge(var_ready, SET + i + 1)
                nc.scalar.activation(s.std[:, :], s.var[:, :], ACT.Sqrt).then_inc(std_ready, 1)
                act.wait_ge(turned, SET + i + 1)
                act.wait_ge(made, SET + i)
                nc.scalar.activation(normT[:, :, :, :].rearrange("p a b c -> p (a b c)"), both(0), ACT.Copy).then_inc(turned_sb, 1)
                for k in range(DC):
                    last = nc.scalar.activation(
                        t.yT[:, k, bass.ds(i * (GRP * P), GRP * P)].rearrange("p (a b) -> p a b", b=P),
                        both(0).rearrange("p (a b c) -> p a b c", b=DC, c=P)[:, :, k, :], ACT.Copy)
                last.then_inc(turned_sb, 1)

        @block.tensor
        def _(pe):
            pe.wait_ge(weights_in, 48)
            with pe.Fori(0, NG) as i:
                pe.wait_ge(norm_ready, SET + i + 1)
                pe.wait_ge(turned_sb, SET + i * 2)
                for j in range(GRP):
                    for k in range(DC):
                        last = nc.tensor.transpose(half(0, j)[:, k * P:(k + 1) * P], norm[:, j, k * P:(k + 1) * P], t.ident_f[:, :])
                last.then_inc(turned, 1)
                pe.wait_ge(turned_sb, SET + i * 2 + 1)
                pe.wait_ge(rows_made, SET + i)
                for j in range(GRP):
                    for k in range(DC):
                        last = nc.tensor.matmul(ps[:, 4, j * HE:(j + 1) * HE], normT[:, j, k, :], w[:, k, :], start=(k == 0), stop=(k == DC - 1))
                last.then_inc(made, 1)


def attention_max(nc, t, table):
    CM = CH // 2
    IT = M_GAT // (2 * CM)
    with ExitStack() as c:
        sb = lambda n, s, d=F32: c.enter_context(nc.sbuf_tensor("m_" + n, s, d))
        sem = semaphores(nc, c, "m_")
        two = lambda n: [sem(f"{n}{k}") for k in range(2)]
        idx_ring = sb("idx_ring", [P, 2, CM], I32)
        got = sb("got", [P, 2, CM, TROW])
        got_b = got[:, :, :, :].rearrange("p a b c -> p (a b c)").bitcast(BF16).rearrange("p (a b c) -> p a b c", a=2, b=CM)
        not_hot = sb("not_hot", [P, 2, CM, P], BF16)
        tile_top = sb("tile_top", [P, CM, HEADS])
        ps = c.enter_context(nc.psum_tensor("m_ps", [P, 8, 512], F32))
        dv, top_set, settled = sem("dv"), sem("top_set"), sem("settled")
        idx_ready, gathered, kept, not_hot_ready, spread, maxed = (
            two(n) for n in ("idx_ready", "gathered", "kept", "not_hot_ready", "spread", "maxed"))
        nc.all_engine_barrier()
        block = c.enter_context(nc.Block())

        @block.gpsimd
        def _(gp):
            with gp.Fori(0, IT) as i:
                for k in range(2):
                    gp.wait_ge(idx_ready[k], SET + i + 1)
                    gp.wait_ge(kept[k], SET + i)
                    gp.wait_ge(spread[k], SET + i)
                    settle_gpsimd(gp, t, settled, i * 2 + k)
                    for j in range(CM):
                        gp.indirect_dma_start(
                            out=got[:, k, j, :], out_offset=None, in_=table,
                            in_offset=bass.IndirectOffsetOnAxis(ap=idx_ring[:, k, j:j + 1], axis=0)).then_inc(gathered[k], 16)

        @block.scalar
        def _(act):
            def indices(col, k):
                nc.scalar.activation(idx_ring[:, k, :], t.gat_idx[:, bass.ds(col, CM)], ACT.Copy).then_inc(idx_ready[k], 1)

            for k in range(2):
                indices(k * CM, k)
            with act.Fori(0, IT) as i:
                for k in range(2):
                    act.wait_ge(gathered[k], (i + 1) * (16 * CM))
                    c0 = i * (2 * CM) + k * CM
                    nc.scalar.activation(t.edge_rows[:, bass.ds(c0, CM), :], got[:, k, :, 0:ROW], ACT.Copy).then_inc(kept[k], 1)
                    indices(c0 + 2 * CM, k)

        @block.tensor
        def _(pe):
            with pe.Fori(0, IT) as i:
                for k in range(2):
                    pe.wait_ge(gathered[k], (i + 1) * (16 * CM))
                    pe.wait_ge(not_hot_ready[k], SET + i + 1)
                    pe.wait_ge(maxed[k], SET + i)
                    for j in range(CM):
                        nc.tensor.matmul(ps[:, CM * k + j, :].rearrange("p (a b) -> p a b", b=P), not_hot[:, k, j, :],
                                         t.neg_ident_b[:, :].unsqueeze(1).to_broadcast([P, HEADS, P]), start=True, stop=False)
                        for h in range(HEADS):
                            for q in range(PARTS):
                                at = 2 * ROW + q * HEADS + h
                                last = nc.tensor.matmul(ps[:, CM * k + j, h * P:(h + 1) * P],
                                                        got_b[:, k, j, at:at + 1].to_broadcast([P, P]), t.ident_b[:, :],
                                                        start=False, stop=(h == HEADS - 1 and q == PARTS - 1))
                    last.then_inc(spread[k], 1)

        @block.vector
        def _(ve):
            v = nc.vector
            ch = Chain(ve, dv)

            def build_not_hot(col, k):
                v.tensor_tensor(not_hot[:, k, :, :], t.gat_node[:, bass.ds(col, CM)].unsqueeze(2).to_broadcast([P, CM, P]),
                                t.iota_f[:, :].unsqueeze(1).to_broadcast([P, CM, P]), ALU.not_equal).then_inc(not_hot_ready[k], 1)

            v.tensor_copy(t.top[:, :, :], t.rows[:, :, HE:ROW]).then_inc(top_set, 1)
            ve.wait_ge(top_set, SET + 1)
            build_not_hot(0, 0)
            with ve.Fori(0, IT) as i:
                ch.enter(i, 2 * CM)
                for k in range(2):
                    other = 1 - k
                    ve.wait_ge(spread[other], SET + i + k)
                    build_not_hot(i * (2 * CM) + (k + 1) * CM, other)
                    ve.wait_ge(spread[k], SET + i + 1)
                    ch.link(v.tensor_reduce(tile_top[:, :, :], ps[:, CM * k:CM * (k + 1), :].rearrange("p a (b c) -> p a b c", c=P),
                                            AX.X, ALU.max))
                    at = load_values(nc, ve, t.gat_block[0:1, bass.ds(i * (2 * CM) + k * CM, CM)], NB - 1)
                    for j in range(CM):
                        m = t.top[:, bass.ds(at[j], 1), :].rearrange("p a b -> p (a b)")
                        ins = v.tensor_tensor(m, m, tile_top[:, j, :], ALU.max)
                        if j < CM - 1:
                            ch.link(ins)
                    ins.then_inc(maxed[k], 1)
                    ve.wait_ge(maxed[k], SET + i + 1)
            ch.leave(IT)


def attention_sum(nc, t):
    IT = M_GAT // (2 * CH)
    PER_BANK = 512 // ROW
    assert NB <= 2 * PER_BANK
    LONG = 4 * CH
    assert M_GAT % LONG == 0
    with ExitStack() as c:
        sb = lambda n, s, d=F32: c.enter_context(nc.sbuf_tensor("s_" + n, s, d))
        sem = semaphores(nc, c, "s_")
        two = lambda n: [sem(f"{n}{k}") for k in range(2)]
        hot_b = sb("hot_b", [P, 2, CH, P], BF16)
        hotT = sb("hotT", [P, 2, CH, P])
        hot = sb("hot", [P, 2, CH, P])
        score = sb("score", [P, 2, CH, HEADS])
        zero_f = sb("zero_f", [P, P])
        second_bank = sb("second_bank", [1, M_GAT])
        sum_at = sb("sum_at", [1, M_GAT], I32)
        ps = c.enter_context(nc.psum_tensor("s_ps", [P, 8, 512], F32))
        dv, node_ready, at_ready, scored, exp_done, weighted, all_summed = (
            sem(n) for n in ("dv", "node_ready", "at_ready", "scored", "exp_done", "weighted", "all_summed"))
        hot_b_ready, turned, turned_sb, picked, picked_used, hot_ready, summed = (
            two(n) for n in ("hot_b_ready", "turned", "turned_sb", "picked", "picked_used", "hot_ready", "summed"))
        flat = lambda a: a.rearrange("p a b -> p (a b)")
        turned_ps = lambda k: ps[:, k, :].bitcast(BF16)
        picked_ps = lambda k: ps[:, 4 + k, 0:CH * 2 * HEADS].rearrange("p (a b) -> p a b", b=2 * HEADS)
        sums_ps = flat(ps[:, 6:8, :])
        nc.all_engine_barrier()
        block = c.enter_context(nc.Block())

        @block.vector
        def _(ve):
            v = nc.vector
            ch = Chain(ve, dv)
            adst, emax = t.node[:, :, 0:HEADS], t.node[:, :, HEADS:2 * HEADS]
            v.tensor_copy(adst, t.adst[:, :, :])
            ch.link(v.tensor_tensor(t.top[:, :, :], t.top[:, :, :], t.adst[:, :, :], ALU.add))
            v.scalar_tensor_tensor(emax, t.top[:, :, :], 0.2, t.top[:, :, :], ALU.mult, ALU.max).then_inc(node_ready, 1)
            v.memset(zero_f[:, :], 0.0)
            ch.link(v.tensor_scalar(second_bank[:, :], t.gat_block[:, :], float(PER_BANK), float(512 - PER_BANK * ROW), ALU.is_ge, ALU.mult))
            v.scalar_tensor_tensor(sum_at[:, :], t.gat_block[:, :], float(ROW), second_bank[:, :], ALU.mult, ALU.add).then_inc(at_ready, 1)
            with ve.Fori(0, IT) as i:
                ch.enter(i, 2 * 3)
                for k in range(2):
                    ve.wait_ge(turned[k], SET + i)
                    v.tensor_tensor(hot_b[:, k, :, :], t.gat_node[:, bass.ds((i * 2 + k) * CH, CH)].unsqueeze(2).to_broadcast([P, CH, P]),
                                    t.iota_b[:, :].unsqueeze(1).to_broadcast([P, CH, P]), ALU.is_equal).then_inc(hot_b_ready[k], 1)
                for k in range(2):
                    ve.wait_ge(picked[k], SET + i + 1)
                    a_src = t.edge_rows[:, bass.ds((i * 2 + k) * CH, CH), HE:ROW]
                    ch.link(v.tensor_tensor(score[:, k, :, :], picked_ps(k)[:, :, 0:HEADS], a_src, ALU.add))
                    ch.link(v.scalar_tensor_tensor(flat(score[:, k, :, :]), flat(score[:, k, :, :]), 0.2, flat(score[:, k, :, :]), ALU.mult, ALU.max))
                    ch.link(v.tensor_tensor(score[:, k, :, :], score[:, k, :, :], picked_ps(k)[:, :, HEADS:2 * HEADS], ALU.subtract))
                    v.tensor_scalar(a_src, score[:, k, :, :], 0.0, None, ALU.min).then_inc(picked_used[k], 1)
            ch.leave(IT)
            with ve.Fori(0, M_GAT // LONG) as i:
                rows = t.edge_rows[:, bass.ds(i * LONG, LONG), :]
                ve.wait_ge(exp_done, SET + i + 1)
                h = rows[:, :, 0:HE].rearrange("p a (b c) -> p a b c", c=EXPERTS)
                v.tensor_tensor(h, h, rows[:, :, HE:ROW].unsqueeze(3).to_broadcast([P, LONG, HEADS, EXPERTS]), ALU.mult).then_inc(weighted, 1)
            with ve.Fori(0, IT) as i:
                for k in range(2):
                    ve.wait_ge(summed[k], SET + i)
                    v.tensor_tensor(hot[:, k, :, :], t.gat_node[:, bass.ds((i * 2 + k) * CH, CH)].unsqueeze(2).to_broadcast([P, CH, P]),
                                    t.iota_b[:, :].unsqueeze(1).to_broadcast([P, CH, P]), ALU.is_equal).then_inc(hot_ready[k], 1)
            ve.wait_ge(all_summed, SET + 1)
            for q in range(2):
                n = min(PER_BANK, NB - q * PER_BANK)
                v.tensor_copy(flat(t.sums[:, q * PER_BANK:q * PER_BANK + n, :]), ps[:, 6 + q, 0:n * ROW])

        @block.scalar
        def _(act):
            with act.Fori(0, IT) as i:
                for k in range(2):
                    act.wait_ge(turned[k], SET + i + 1)
                    act.wait_ge(picked[k], SET + i)
                    nc.scalar.activation(hotT[:, k, :, :].rearrange("p a b -> p (a b)"), turned_ps(k), ACT.Copy).then_inc(turned_sb[k], 1)
            for k in range(2):
                act.wait_ge(picked_used[k], SET + IT)
            with act.Fori(0, M_GAT // LONG) as i:
                e = t.edge_rows[:, bass.ds(i * LONG, LONG), HE:ROW]
                nc.scalar.activation(e, e, ACT.Exp).then_inc(exp_done, 1)

        @block.tensor
        def _(pe):
            pe.wait_ge(node_ready, SET + 1)
            with pe.Fori(0, IT) as i:
                for k in range(2):
                    pe.wait_ge(hot_b_ready[k], SET + i + 1)
                    pe.wait_ge(turned_sb[k], SET + i)
                    for j in range(CH):
                        last = nc.tensor.transpose(turned_ps(k)[:, j * P:(j + 1) * P], hot_b[:, k, j, :], t.ident_b[:, :])
                    last.then_inc(turned[k], 1)
                for k in range(2):
                    at = load_values(nc, pe, t.gat_block[0:1, bass.ds((i * 2 + k) * CH, CH)], NB - 1)
                    pe.wait_ge(turned_sb[k], SET + i + 1)
                    pe.wait_ge(picked_used[k], SET + i)
                    for j in range(CH):
                        last = nc.tensor.matmul(picked_ps(k)[:, j, :], hotT[:, k, j, :], flat(t.node[:, bass.ds(at[j], 1), :]), start=True, stop=True)
                    last.then_inc(picked[k], 1)
            pe.wait_ge(at_ready, SET + 1)
            for q in range(2):
                nc.tensor.matmul(ps[:, 6 + q, :].rearrange("p (a b) -> p a b", b=P), zero_f[:, :], t.ones_f[:, :].unsqueeze(1).to_broadcast([P, 4, P]), start=True, stop=False)
            pe.wait_ge(weighted, SET + M_GAT // LONG)
            with pe.Fori(0, IT) as i:
                for k in range(2):
                    at = load_values(nc, pe, sum_at[0:1, bass.ds((i * 2 + k) * CH, CH)], 512 + (NB - PER_BANK - 1) * ROW)
                    pe.wait_ge(hot_ready[k], SET + i + 1)
                    for j in range(CH):
                        last = nc.tensor.matmul(sums_ps[:, bass.ds(at[j], ROW)], hot[:, k, j, :],
                                                flat(t.edge_rows[:, bass.ds((i * 2 + k) * CH + j, 1), :]), start=False, stop=False)
                    last.then_inc(summed[k], 1)
            for q in range(2):
                last = nc.tensor.matmul(ps[:, 6 + q, :].rearrange("p (a b) -> p a b", b=P), zero_f[:, :], t.ones_f[:, :].unsqueeze(1).to_broadcast([P, 4, P]), start=False, stop=True)
            last.then_inc(all_summed, 1)


def attention_gates(nc, t, b_gat, ln_gamma, ln_beta):
    with ExitStack() as c:
        sb = lambda n, s, d=F32: c.enter_context(nc.sbuf_tensor("w_" + n, s, d))
        sem = semaphores(nc, c, "w_")
        par = sb("par", [P, 3, HE])
        own = sb("own", [P, NB, HEADS])
        den = sb("den", [P, NB, HEADS])
        agg = sb("agg", [P, NB, HE])
        sq = sb("sq", [P, NB, HE])
        stat = sb("stat", [P, 3, NB])
        std = sb("std", [P, NB])
        score = sb("score", [P, NB, EXPERTS])
        ahead = sb("ahead", [P, NB])
        rank = sb("rank", [P, NB, EXPERTS])
        prob = sb("prob", [P, NB, EXPERTS])
        par_in, dv, own_ready, own_exp, var_ready, std_ready, prob_ready, prob_exp = (
            sem(n) for n in ("par_in", "dv", "own_ready", "own_exp", "var_ready", "std_ready", "prob_ready", "prob_exp"))
        flat = lambda a: a.rearrange("p a b -> p (a b)")
        nc.all_engine_barrier()
        block = c.enter_context(nc.Block())

        @block.sync
        def _(sp):
            for k, a in enumerate((b_gat, ln_gamma, ln_beta)):
                sp.dma_start(par[:, k, :], a.rearrange("(o d) -> o d", o=1).to_broadcast([P, HE])).then_inc(par_in, 16)

        @block.scalar
        def _(act):
            act.wait_ge(own_ready, SET + 1)
            nc.scalar.activation(flat(own[:, :, :]), flat(own[:, :, :]), ACT.Exp).then_inc(own_exp, 1)
            act.wait_ge(var_ready, SET + 1)
            nc.scalar.activation(std[:, :], stat[:, 1, :], ACT.Sqrt).then_inc(std_ready, 1)
            act.wait_ge(prob_ready, SET + 1)
            nc.scalar.activation(flat(prob[:, :, :]), flat(prob[:, :, :]), ACT.Exp).then_inc(prob_exp, 1)

        @block.vector
        def _(ve):
            v = nc.vector
            ch = Chain(ve, dv)
            link = ch.link
            heads = lambda a: a.rearrange("p a (b c) -> p a b c", c=EXPERTS)
            per_head = lambda a: a.unsqueeze(3).to_broadcast([P, NB, HEADS, EXPERTS])
            spread = lambda a, n: a.unsqueeze(2).to_broadcast([P, NB, n])
            param = lambda k: par[:, k, :].unsqueeze(1).to_broadcast([P, NB, HE])
            link(v.tensor_tensor(own[:, :, :], t.rows[:, :, HE:ROW], t.adst[:, :, :], ALU.add))
            link(v.scalar_tensor_tensor(flat(own[:, :, :]), flat(own[:, :, :]), 0.2, flat(own[:, :, :]), ALU.mult, ALU.max))
            v.tensor_tensor(own[:, :, :], own[:, :, :], t.node[:, :, HEADS:2 * HEADS], ALU.subtract).then_inc(own_ready, 1)
            ve.wait_ge(own_ready, SET + 1)
            ve.wait_ge(own_exp, SET + 1)
            link(v.tensor_tensor(den[:, :, :], t.sums[:, :, HE:ROW], own[:, :, :], ALU.add))
            link(v.tensor_scalar(flat(den[:, :, :]), flat(den[:, :, :]), 1e-16, None, ALU.add))
            link(v.reciprocal(flat(den[:, :, :]), flat(den[:, :, :])))
            link(v.tensor_tensor(heads(agg[:, :, :]), heads(t.rows[:, :, 0:HE]), per_head(own[:, :, :]), ALU.mult))
            link(v.tensor_tensor(agg[:, :, :], agg[:, :, :], t.sums[:, :, 0:HE], ALU.add))
            link(v.tensor_tensor(heads(agg[:, :, :]), heads(agg[:, :, :]), per_head(den[:, :, :]), ALU.mult))
            ve.wait_ge(par_in, 48)
            link(v.tensor_tensor(agg[:, :, :], agg[:, :, :], param(0), ALU.add))
            link(v.tensor_reduce(stat[:, 0, :], agg[:, :, :], AX.X, ALU.add))
            link(v.tensor_scalar(stat[:, 0, :], stat[:, 0, :], 1.0 / HE, None, ALU.mult))
            link(v.tensor_tensor(agg[:, :, :], agg[:, :, :], spread(stat[:, 0, :], HE), ALU.subtract))
            link(v.tensor_tensor(sq[:, :, :], agg[:, :, :], agg[:, :, :], ALU.mult))
            link(v.tensor_reduce(stat[:, 1, :], sq[:, :, :], AX.X, ALU.add))
            v.tensor_scalar(stat[:, 1, :], stat[:, 1, :], 1.0 / HE, EPS, ALU.mult, ALU.add).then_inc(var_ready, 1)
            ve.wait_ge(var_ready, SET + 1)
            ve.wait_ge(std_ready, SET + 1)
            link(v.reciprocal(stat[:, 2, :], std[:, :]))
            link(v.scalar_tensor_tensor(stat[:, 1, :], stat[:, 1, :], -0.5, stat[:, 2, :], ALU.mult, ALU.mult))
            link(v.tensor_tensor(stat[:, 1, :], stat[:, 1, :], stat[:, 2, :], ALU.mult))
            link(v.scalar_tensor_tensor(stat[:, 2, :], stat[:, 1, :], 1.5, stat[:, 2, :], ALU.add, ALU.mult))
            link(v.tensor_tensor(agg[:, :, :], agg[:, :, :], spread(stat[:, 2, :], HE), ALU.mult))
            link(v.tensor_tensor(agg[:, :, :], agg[:, :, :], param(1), ALU.mult))
            link(v.tensor_tensor(agg[:, :, :], agg[:, :, :], param(2), ALU.add))
            link(v.tensor_reduce(score[:, :, :], agg[:, :, :].rearrange("p a (b c) -> p a c b", c=EXPERTS), AX.X, ALU.add))
            link(v.tensor_scalar(flat(score[:, :, :]), flat(score[:, :, :]), 1.0 / HEADS, None, ALU.mult))
            link(v.memset(rank[:, :, :], 0.0))
            for a in range(EXPERTS):
                for b in range(EXPERTS):
                    if a != b:
                        link(v.tensor_tensor(ahead[:, :], score[:, :, b], score[:, :, a], ALU.is_ge if b < a else ALU.is_gt))
                        link(v.tensor_tensor(rank[:, :, a], rank[:, :, a], ahead[:, :], ALU.add))
            link(v.tensor_reduce(ahead[:, :], score[:, :, :], AX.X, ALU.max))
            link(v.tensor_scalar(flat(rank[:, :, :]), flat(rank[:, :, :]), float(TOPK), None, ALU.is_lt))
            v.tensor_tensor(prob[:, :, :], score[:, :, :], spread(ahead[:, :], EXPERTS), ALU.subtract).then_inc(prob_ready, 1)
            ve.wait_ge(prob_ready, SET + 1)
            ve.wait_ge(prob_exp, SET + 1)
            link(v.tensor_tensor(prob[:, :, :], prob[:, :, :], rank[:, :, :], ALU.mult))
            link(v.tensor_reduce(ahead[:, :], prob[:, :, :], AX.X, ALU.add))
            link(v.reciprocal(ahead[:, :], ahead[:, :]))
            link(v.tensor_tensor(t.gate[:, :, :], prob[:, :, :], spread(ahead[:, :], EXPERTS), ALU.mult))


def experts(nc, t, space, W1, b1, W2, b2, x1, out):
    TOK = GRP * P
    HALF = TOK // 2
    with ExitStack() as c:
        sb = lambda n, s, d=F32: c.enter_context(nc.sbuf_tensor("e_" + n, s, d))
        sem = semaphores(nc, c, "e_")
        two = lambda n: [sem(f"{n}{k}") for k in range(2)]
        n1, n2, n3, n4 = EXPERTS * DC * HID, EXPERTS * HM * D, 2 * HM * TOK, GRP * D
        w1 = space[:, 0:n1].rearrange("p (e c h) -> p e c h", e=EXPERTS, c=DC)
        w2 = space[:, n1:n1 + n2].rearrange("p (e m d) -> p e m d", e=EXPERTS, m=HM)
        hidden = space[:, n1 + n2:n1 + n2 + n3].rearrange("p (a m t) -> p a m t", a=2, m=HM)
        acc = space[:, n1 + n2 + n3:n1 + n2 + n3 + n4].rearrange("p (a b) -> p a b", b=D)
        b1t = sb("b1", [P, EXPERTS, HM])
        b2t = sb("b2", [EXPERTS, D])
        gate = sb("gate", [P, GRP, EXPERTS])
        gateT = sb("gateT", [EXPERTS, TOK])
        ps = c.enter_context(nc.psum_tensor("e_ps", [P, 8, 512], F32))
        weights_in, acc_in, acc_out, dv, gate_ready, gateT_done, gateT_ready, bias_done, y_done, y_added = (
            sem(n) for n in ("weights_in", "acc_in", "acc_out", "dv", "gate_ready", "gateT_done", "gateT_ready", "bias_done", "y_done", "y_added"))
        hid_done, hid_used = two("hid_done"), two("hid_used")
        y_ps = lambda j: ps[:, 4 + j // 2, (j % 2) * D:(j % 2 + 1) * D]
        gT_ps = lambda j: ps[0:EXPERTS, 4 + j // 4, (j % 4) * P:(j % 4 + 1) * P]
        YG = 1 + EXPERTS
        nc.all_engine_barrier()
        block = c.enter_context(nc.Block())

        @block.sync
        def _(sp):
            sp.dma_start(w1[:, :, :, :].rearrange("p e c h -> p (e c) h"), W1.rearrange("e (c p) h -> p (e c) h", p=P)).then_inc(weights_in, 16)
            sp.dma_start(w2[:, :, :, :].rearrange("p e m d -> p (e m) d"), W2.rearrange("e (m p) d -> p (e m) d", p=P)).then_inc(weights_in, 16)
            with nc.allow_non_contiguous_dma(reason="2048 biases, once"):
                sp.dma_start(b1t[:, :, :].rearrange("p e m -> p (e m)"), b1.rearrange("e (m p) -> p (e m)", p=P)).then_inc(weights_in, 16)
            sp.dma_start(b2t[:, :], b2).then_inc(weights_in, 16)
            group = lambda a, i: a.rearrange("(b p) d -> p b d", p=P)[:, bass.ds(i * GRP, GRP), :]
            sp.dma_start(acc[:, :, :], group(x1, 0)).then_inc(acc_in, 16)
            with sp.Fori(0, NG - 1) as i:
                sp.wait_ge(y_added, SET + (i + 1) * YG)
                sp.dma_start(group(out, i), acc[:, :, :]).then_inc(acc_out, 16)
                sp.wait_ge(acc_out, (i + 1) * 16)
                sp.dma_start(acc[:, :, :], group(x1, i + 1)).then_inc(acc_in, 16)
            sp.wait_ge(y_added, SET + NG * YG)
            sp.dma_start(group(out, NG - 1), acc[:, :, :]).then_inc(acc_out, 16)
            sp.wait_ge(acc_out, NG * 16)

        @block.tensor
        def _(pe):
            pe.wait_ge(weights_in, 64)
            with pe.Fori(0, NG) as i:
                pe.wait_ge(gate_ready, SET + i + 1)
                pe.wait_ge(y_added, SET + i * YG)
                for j in range(GRP):
                    last = nc.tensor.transpose(gT_ps(j), gate[:, j, :], t.ident_f[:, :])
                last.then_inc(gateT_done, 1)
                pe.wait_ge(gateT_ready, SET + i + 1)
                for j in range(GRP):
                    last = nc.tensor.matmul(y_ps(j), gateT[:, j * P:(j + 1) * P], b2t[:, :], start=True, stop=True)
                last.then_inc(bias_done, 1)

                def up(e):
                    for m in range(HM):
                        pe.wait_ge(hid_used[m % 2], SET + (i * EXPERTS + e) * (HM // 2) + m // 2)
                        for k in range(DC):
                            for f in range(2):
                                last = nc.tensor.matmul(ps[:, 2 * (m % 2) + f, 0:HALF], w1[:, e, k, m * P:(m + 1) * P],
                                                        t.yT[:, k, bass.ds(i * TOK + f * HALF, HALF)], start=(k == 0), stop=(k == DC - 1))
                        last.then_inc(hid_done[m % 2], 1)

                def down(e):
                    for q in range(2):
                        pe.wait_ge(hid_used[q], SET + (i * EXPERTS + e + 1) * (HM // 2))
                    pe.wait_ge(y_added, SET + i * YG + e + 1)
                    for j in range(GRP):
                        for m in range(HM):
                            last = nc.tensor.matmul(y_ps(j), hidden[:, e % 2, m, j * P:(j + 1) * P], w2[:, e, m, :], start=(m == 0), stop=(m == HM - 1))
                    last.then_inc(y_done, 1)

                up(0)
                for e in range(1, EXPERTS):
                    up(e)
                    down(e - 1)
                down(EXPERTS - 1)

        @block.scalar
        def _(act):
            act.wait_ge(weights_in, 64)
            with act.Fori(0, NG) as i:
                for e in range(EXPERTS):
                    if e >= 2:
                        act.wait_ge(y_done, SET + i * EXPERTS + e - 1)
                    else:
                        act.wait_ge(y_done, SET + i * EXPERTS)
                    for m in range(HM):
                        act.wait_ge(hid_done[m % 2], SET + (i * EXPERTS + e) * (HM // 2) + m // 2 + 1)
                        nc.scalar.activation(hidden[:, e % 2, m, :].rearrange("p (a b) -> p a b", a=2),
                                             ps[:, 2 * (m % 2):2 * (m % 2) + 2, 0:HALF], ACT.Gelu,
                                             bias=b1t[:, e, m:m + 1]).then_inc(hid_used[m % 2], 1)

        @block.vector
        def _(ve):
            v = nc.vector
            ch = Chain(ve, dv)
            with ve.Fori(0, NG) as i:
                ve.wait_ge(gateT_done, SET + i)
                ve.wait_ge(y_added, SET + i * YG)
                v.tensor_copy(gate[:, :, :], t.gate[:, bass.ds(i * GRP, GRP), :]).then_inc(gate_ready, 1)
                ve.wait_ge(gateT_done, SET + i + 1)
                ve.wait_ge(bias_done, SET + i)
                for q in range(2):
                    w = min(4, GRP - 4 * q)
                    last = v.tensor_copy(gateT[:, 4 * q * P:(4 * q + w) * P], ps[0:EXPERTS, 4 + q, 0:w * P])
                last.then_inc(gateT_ready, 1)
                ve.wait_ge(acc_in, (i + 1) * 16)
                ve.wait_ge(bias_done, SET + i + 1)
                for j in range(GRP):
                    last = v.tensor_tensor(acc[:, j, :], acc[:, j, :], y_ps(j), ALU.add)
                last.then_inc(y_added, 1)
                for e in range(EXPERTS):
                    ve.wait_ge(y_added, SET + i * YG + e + 1)
                    ve.wait_ge(y_done, SET + i * EXPERTS + e + 1)
                    for j in range(GRP):
                        last = v.scalar_tensor_tensor(acc[:, j, :], y_ps(j), gate[:, j, e:e + 1], acc[:, j, :], ALU.mult, ALU.add)
                    last.then_inc(y_added, 1)


def build(nc, a, out):
    t = Tensors()
    t.nc = nc
    dram = lambda n, s: nc.dram_tensor(n, s, F32, kind="Internal").ap()
    gnn_slots = dram("gnn_slots", [M_GNN * P, 1])
    gat_slots = dram("gat_slots", [M_GAT * P, 1])
    gnn_table = dram("gnn_table", [NP, D])
    gat_table = dram("gat_table", [NP, TROW])
    x1 = dram("x1", [NP, D])
    with ExitStack() as c:
        sb = lambda n, s, d=F32: c.enter_context(nc.sbuf_tensor(n, s, d))
        t.iota_f = sb("iota_f", [P, P])
        t.iota_b = sb("iota_b", [P, P], BF16)
        t.ident_f = sb("ident_f", [P, P])
        t.ident_b = sb("ident_b", [P, P], BF16)
        t.neg_ident_b = sb("neg_ident_b", [P, P], BF16)
        t.ones_f = sb("ones_f", [P, P])
        t.ones_b = sb("ones_b", [P, P], BF16)
        t.zero_b = sb("zero_b", [P, P], BF16)
        t.lower_b = sb("lower_b", [P, P], BF16)
        t.valid = sb("valid", [P, 2])
        t.spare = sb("spare", [P, 4])
        t.dinv = sb("dinv", [P, NB])
        t.gnn_idx = sb("gnn_idx", [P, M_GNN + 2 * CH], I32)
        t.gnn_node = sb("gnn_node", [P, M_GNN + CH], BF16)
        t.gnn_block = sb("gnn_block", [1, M_GNN], I32)
        t.gat_idx = sb("gat_idx", [P, M_GAT + CH], I32)
        t.gat_node = sb("gat_node", [P, M_GAT + CH], BF16)
        t.gat_block = sb("gat_block", [1, M_GAT], I32)
        build_constants(nc, t)

        def load_gnn(sp, key, val, done):
            whole, rest = divmod(E_GNN, T_GNN)
            for tile, arr in ((key, a["src"]), (val, a["dst"])):
                sp.dma_start(tile[0:whole, :], arr[0:whole * T_GNN].rearrange("(p t) -> p t", t=T_GNN)).then_inc(done, 16)
                sp.dma_start(tile[whole:whole + 1, 0:rest], arr[whole * T_GNN:E_GNN].rearrange("(p t) -> p t", p=1)).then_inc(done, 16)

        def load_gat(sp, key, val, done):
            for tile, row in ((key, 1), (val, 0)):
                sp.dma_start(tile[:, :], a["L0_ffn_edge_index"][row, :].rearrange("(p t) -> p t", p=P)).then_inc(done, 16)

        sort_edges(nc, t, "gnn_", load_gnn, 4, T_GNN, M_GNN, gnn_slots, t.gnn_idx, t.gnn_node, t.gnn_block, t.dinv)
        sort_edges(nc, t, "gat_", load_gat, 2, T_GAT, M_GAT, gat_slots, t.gat_idx, t.gat_node, t.gat_block, None)
        region = sb("region", [P, NB * D + M_GAT * ROW])
        first, second = region[:, 0:NB * D], region[:, NB * D:NB * D + M_GAT * ROW]
        t.msg = first.rearrange("p (a b) -> p a b", b=D)
        t.yT = first.rearrange("p (a b) -> p a b", b=NP)
        t.h = second[:, 0:NB * D].rearrange("p (a b) -> p a b", b=D)
        t.edge_rows = second.rearrange("p (a b) -> p a b", b=ROW)
        project_input(nc, t, a["x"], a["L0_gnn_W_in"], a["L0_gnn_b_in"])
        gnn_layers(nc, t, a["L0_gnn_Wl"], a["L0_gnn_bl"], a["L0_gnn_Wg"], a["L0_gnn_bg"],
                   a["L0_gnn_gamma"], a["L0_gnn_beta"], gnn_table)
        t.rows = sb("rows", [P, NB, TROW])
        t.adst = sb("adst", [P, NB, HEADS])
        t.top = sb("top", [P, NB, HEADS])
        t.node = sb("node", [P, NB, 2 * HEADS])
        t.sums = sb("sums", [P, NB, ROW])
        t.gate = sb("gate", [P, NB, EXPERTS])
        t.rows_b = t.rows[:, :, :].bitcast(BF16)
        attention_rows(nc, t, a["x"], a["L0_ffn_W_gat"], a["L0_ffn_att_src"], a["L0_ffn_att_dst"], x1, gat_table)
        attention_max(nc, t, gat_table)
        attention_sum(nc, t)
        attention_gates(nc, t, a["L0_ffn_b_gat"], a["L0_ffn_ln_gamma"], a["L0_ffn_ln_beta"])
        experts(nc, t, second, a["L0_ffn_W1"], a["L0_ffn_b1"], a["L0_ffn_W2"], a["L0_ffn_b2"], x1, out)


def kernel(**inputs):
    import numpy as np
    import concourse.bacc as bacc
    from concourse.bass_utils import run_bass_kernel_spmd

    nc = bacc.Bacc("TRN2", target_bir_lowering=False, num_devices=1)
    arrays, aps = {}, {}
    for name, value in inputs.items():
        value = np.ascontiguousarray(value)
        if name == "x":
            value = np.pad(value, ((0, NP - N), (0, 0)))
        arrays["in_" + name] = value
        aps[name] = nc.dram_tensor("in_" + name, value.shape, mybir.dt.from_np(value.dtype), kind="ExternalInput").ap()
    out = nc.dram_tensor("out", [NP, D], F32, kind="ExternalOutput").ap()
    build(nc, aps, out)
    result = run_bass_kernel_spmd(nc, [arrays], core_ids=[0])
    return result.results[0]["out"][0:N]
```

```python
import concourse.bass as bass
from concourse import mybir
from contextlib import ExitStack

F32 = mybir.dt.float32
BF16 = mybir.dt.bfloat16
I32 = mybir.dt.int32
ALU = mybir.AluOpType
ACT = mybir.ActivationFunctionType
AX = mybir.AxisListType

P = 128
N = 6250
NB = (N + P - 1) // P
NP = NB * P
LAST = N - (NB - 1) * P
D = 256
DC = D // P
LAYERS = 4
GRP = 7
NG = NB // GRP
EXPERTS, HEADS, TOPK = 4, 4, 2
HE = HEADS * EXPERTS
HID = 512
HM = HID // P
ROW = HE + HEADS
PARTS = 3
TROW = ROW + PARTS * HEADS // 2
EPS = 1e-5
NEG = -1e30
E_GNN = 100000
E_GAT = 131072
T_GNN = 784
T_GAT = E_GAT // P
CH = 8
LO_SHIFT = 13
NO_NODE = P
OUTSIDE = 8191
FAR = float(1 << 20)


def tiles_bound(edges, multiple):
    n = (edges + NB * (P - 1)) // P
    return -(-n // multiple) * multiple


M_GNN = tiles_bound(E_GNN, 2 * CH)
M_GAT = tiles_bound(E_GAT, 2 * CH)
REGION = NB * D + M_GAT * ROW
GAT_KEPT = 2 * T_GAT


RING = 4

SET = 2 * CH
DMA_DONE = ("edges_in", "filled", "scattered", "rows_in", "loaded", "weights_in", "table_in", "gathered", "x_in", "x1_out",
            "table_out", "par_in", "acc_in", "acc_out")


class Chain:

    def __init__(self, eng, sem):
        self.eng, self.sem, self.base, self.n = eng, sem, 0, 0

    def link(self, ins):
        ins.then_inc(self.sem, 1)
        self.n += 1
        self.eng.wait_ge(self.sem, SET + self.base + self.n)

    def enter(self, it, per):
        self.start, self.per, self.first = self.base + self.n, per, True
        self.base, self.n = self.start + it * per, 0

    def leave(self, count):
        assert self.n == self.per, (self.n, self.per)
        self.base, self.n = self.start + count * self.per, 0


def semaphores(nc, c, tag):
    used = []

    def make(name):
        used.append(nc.alloc_semaphore(tag + name))
        if not name.startswith(DMA_DONE):
            nc.gpsimd.sem_inc(used[-1], SET)
        return used[-1]

    def clear():
        nc.clear_and_free_semaphores(used)
        nc.all_engine_barrier()

    c.callback(clear)
    return make


def settle(ve, t, element=3):
    ve.memset(t.spare[0:1, element:element + 1], 0.0)


def settle_gpsimd(gp, t, settled, before, element=0):
    gp.wait_ge(settled, SET + before)
    gp.tensor_tensor(t.spare[0:1, element:element + 1], t.spare[0:1, 1:2], t.spare[0:1, 2:3], ALU.add).then_inc(settled, 1)


def load_values(nc, eng, row, most):
    return nc.values_load_multi_w_load_instructions(
        row, engines=(eng.engine,), min_val=0, max_val=most,
        skip_runtime_bounds_check_because="the rows come from block_of_tile: a count of blocks, at most NB - 1 by its min")[1]


def pipeline(eng, chunks, step):
    loops = chunks // RING - 2
    there = lambda n: lambda d: 0 <= n + d < chunks
    for n in range(RING):
        step(n, n + RING, there(n))
    with eng.Fori(0, loops) as i:
        for k in range(RING):
            step(i * RING + (k + RING), k + RING, lambda d: True)
    for n in range((loops + 1) * RING, chunks):
        step(n, n, there(n))


class Tensors:
    pass


def build_constants(nc, t):
    with ExitStack() as c:
        const_step = semaphores(nc, c, "const_")("step")
        nc.all_engine_barrier()
        block = c.enter_context(nc.Block())

        @block.gpsimd
        def _(gp):
            c = Chain(gp, const_step)
            gp.iota(t.iota_f[:, :], pattern=[[1, P]], base=0, channel_multiplier=0,
                    allow_small_or_imprecise_dtypes=True)
            gp.iota(t.iota_b[:, :], pattern=[[1, P]], base=0, channel_multiplier=0,
                    allow_small_or_imprecise_dtypes=True)
            gp.memset(t.ident_f[:, :], 0.0)
            gp.memset(t.neg_ident_b[:, :], 0.0)
            gp.memset(t.ident_b[:, :], 0.0)
            gp.memset(t.ones_f[:, :], 1.0)
            gp.memset(t.spare[:, :], 0.0)
            gp.memset(t.ones_b[:, :], 1.0)
            gp.memset(t.lower_b[:, :], 1.0)
            c.link(gp.memset(t.valid[:, :], 1.0))
            gp.affine_select(out=t.ident_f[:, :], in_=t.ident_f[:, :], compare_op=ALU.not_equal, fill=1.0,
                             base=0, pattern=[[-1, P]], channel_multiplier=1)
            gp.affine_select(out=t.ident_b[:, :], in_=t.ident_b[:, :], compare_op=ALU.not_equal, fill=1.0,
                             base=0, pattern=[[-1, P]], channel_multiplier=1)
            gp.affine_select(out=t.neg_ident_b[:, :], in_=t.neg_ident_b[:, :], compare_op=ALU.not_equal,
                             fill=NEG, base=0, pattern=[[-1, P]], channel_multiplier=1)
            gp.affine_select(out=t.lower_b[:, :], in_=t.lower_b[:, :], compare_op=ALU.is_gt, fill=0.0,
                             base=0, pattern=[[1, P]], channel_multiplier=-1)
            c.link(gp.affine_select(out=t.valid[:, 1:2], in_=t.valid[:, 1:2], compare_op=ALU.is_gt, fill=0.0,
                                    base=LAST, pattern=[[0, 1]], channel_multiplier=-1))
            c.link(gp.memset(t.zero_b[:, :], 0.0))


STEP = 2 * CH
ROUNDS_INPUT = 4
ROUNDS_LAYER = 6
ROUNDS_ROWS = T_GAT // (2 * STEP) - ROUNDS_INPUT - LAYERS * ROUNDS_LAYER


def attention_scatters(nc, t, c, sem, tag, gat_slots, first):
    pos_ring = c.enter_context(nc.sbuf_tensor(tag + "gat_pos_ring", [P, 2, STEP], I32))
    pay_ring = c.enter_context(nc.sbuf_tensor(tag + "gat_pay_ring", [P, 2, STEP], F32))
    ring_ready, settled = sem("gat_ring_ready"), sem("gat_settled")
    scattered = [sem(f"scattered_gat{k}") for k in range(2)]

    def one_round(gp, at, peeled):
        done = at - first
        for k in range(2):
            if not peeled:
                gp.wait_ge(scattered[k], done * (16 * STEP))
            settle_gpsimd(gp, t, settled, done * 4 + 2 * k, 4)
            col = bass.ds((at * 2 + k) * STEP, STEP)
            gp.tensor_copy(pos_ring[:, k, :], t.gat_pos[:, col]).then_inc(ring_ready, 1)
            gp.tensor_copy(pay_ring[:, k, :], t.gat_packed[:, col]).then_inc(ring_ready, 1)
            gp.wait_ge(ring_ready, SET + (done * 2 + k + 1) * 2)
            settle_gpsimd(gp, t, settled, done * 4 + 2 * k + 1, 4)
            for j in range(STEP):
                gp.indirect_dma_start(
                    out=gat_slots, out_offset=bass.IndirectOffsetOnAxis(ap=pos_ring[:, k, j:j + 1], axis=0),
                    in_=pay_ring[:, k, j:j + 1], in_offset=None,
                    bounds_check=M_GAT * P - 1, oob_is_err=False).then_inc(scattered[k], 16)

    def run(gp, at, count):
        one_round(gp, at, True)
        with gp.Fori(1, count) as i:
            one_round(gp, at + i, False)
        for k in range(2):
            gp.wait_ge(scattered[k], (at - first + count) * (16 * STEP))

    return run


def sort_edges(nc, t, region, load_gnn, load_gat, gnn_slots, gat_slots):
    with ExitStack() as c:
        sb = lambda n, s, d=F32: c.enter_context(nc.sbuf_tensor("sort_" + n, s, d))
        pb = lambda n, s, d=F32: c.enter_context(nc.psum_tensor("sort_" + n, s, d))
        u = Tensors()
        used = [0]

        def take(columns):
            used[0] += columns
            assert used[0] <= REGION - GAT_KEPT
            return region[:, used[0] - columns:used[0]]

        u.in_block = take(T_GAT * NB // 2).bitcast(BF16).rearrange("p (a b) -> p a b", b=NB)
        u.key, u.val, u.tmp_i = (take(T_GAT).bitcast(I32) for _ in range(3))
        u.dropped = take(T_GAT)
        u.fill = take(M_GAT)
        gnn_packed = take(T_GNN)
        gnn_pos = take(T_GNN).bitcast(I32)
        u.lo_b = sb("lo_b", [P, T_GAT], BF16)
        u.hi_b = sb("hi_b", [P, T_GAT], BF16)
        u.at_lane = sb("at_lane", [P, 2, CH, P], BF16)
        u.counts = sb("counts", [P, NB])
        u.degree = sb("degree", [P, NB])
        u.counts_i = sb("counts_i", [P, NB], I32)
        u.ntiles = sb("ntiles", [P, NB])
        u.zeros = sb("zeros", [P, NB])
        u.end_tile = sb("end_tile", [P, NB])
        u.end_col = sb("end_col", [NB, 1])
        u.ended = sb("ended", [NB, M_GAT])
        u.tile_iota = sb("tile_iota", [NB, M_GAT])
        u.run = sb("run", [P, NB])
        u.ranked = sb("ranked", [P, CH, NB])
        u.picked = sb("picked", [P, CH, NB])
        u.slot = sb("slot", [P, CH])
        pos_ring = sb("pos_ring", [P, 2, CH], I32)
        pay_ring = sb("pay_ring", [P, 2, CH])
        u.rank_ps = pb("rank_ps", [P, 2, 512])
        u.total_ps = pb("total_ps", [P, 2, 512])
        u.hist_ps = pb("hist_ps", [P, 512])
        u.misc_ps = pb("misc_ps", [P, 3, 512])
        sem = semaphores(nc, c, "sort_")
        u.iota_ready = sem("iota_ready")
        u.fill_ready = sem("fill_ready")
        filled, ring_ready, settled = sem("filled"), sem("ring_ready"), sem("settled")
        scattered = [sem(f"scattered{k}") for k in range(2)]
        gnn = placing(nc, t, u, semaphores(nc, c, "gnn_"), T_GNN, M_GNN, 4, gnn_packed, gnn_pos, t.gnn_block, t.dinv)
        gat = placing(nc, t, u, semaphores(nc, c, "gat_"), T_GAT, M_GAT, 2, t.gat_packed, t.gat_pos, t.gat_block, None)
        NCH = T_GNN // CH
        nc.all_engine_barrier()
        block = c.enter_context(nc.Block())

        @block.sync
        def _(sp):
            sp.wait_ge(gnn.keys_clear, SET + 1)
            load_gnn(sp, u.key, u.val, gnn.edges_in)
            sp.wait_ge(u.fill_ready, SET + 1)
            sp.dma_start(gnn_slots.rearrange("(p m) o -> p (m o)", p=P), u.fill[:, 0:M_GNN]).then_inc(filled, 16)
            sp.dma_start(gat_slots.rearrange("(p m) o -> p (m o)", p=P), u.fill[:, :]).then_inc(filled, 16)
            sp.wait_ge(gat.keys_clear, SET + 1)
            load_gat(sp, u.key, u.val, gat.edges_in)

        @block.gpsimd
        def _(gp):
            gp.iota(u.tile_iota[:, :], pattern=[[1, M_GAT]], base=0, channel_multiplier=0,
                    allow_small_or_imprecise_dtypes=True).then_inc(u.iota_ready, 1)
            gp.wait_ge(filled, 32)
            with gp.Fori(0, NCH // 2) as i:
                for k in range(2):
                    gp.wait_ge(ring_ready, SET + (i * 2 + k + 1) * 2)
                    settle_gpsimd(gp, t, settled, i * 2 + k)
                    for j in range(CH):
                        gp.indirect_dma_start(
                            out=gnn_slots, out_offset=bass.IndirectOffsetOnAxis(ap=pos_ring[:, k, j:j + 1], axis=0),
                            in_=pay_ring[:, k, j:j + 1], in_offset=None,
                            bounds_check=M_GNN * P - 1, oob_is_err=False).then_inc(scattered[k], 16)
            for k in range(2):
                gp.wait_ge(scattered[k], 16 * CH * NCH // 2)

        @block.scalar
        def _(act):
            def into_ring(n, k):
                act.wait_ge(gnn.pos_ready, SET + n + 1)
                nc.scalar.activation(pos_ring[:, k, :], gnn_pos[:, bass.ds(n * CH, CH)], ACT.Copy).then_inc(ring_ready, 1)
                nc.scalar.activation(pay_ring[:, k, :], gnn_packed[:, bass.ds(n * CH, CH)], ACT.Copy).then_inc(ring_ready, 1)

            for k in range(2):
                into_ring(k, k)
            with act.Fori(0, NCH // 2 - 1) as i:
                for k in range(2):
                    act.wait_ge(scattered[k], (i + 1) * (16 * CH))
                    into_ring(i * 2 + (k + 2), k)
            act.wait_ge(gnn.sqrt_in, SET + 1)
            nc.scalar.activation(t.dinv[:, :], t.dinv[:, :], ACT.Sqrt).then_inc(gnn.sqrt_out, 1)

        @block.tensor
        def _(pe):
            gnn.tensor(pe)
            gat.tensor(pe)

        @block.vector
        def _(ve):
            v = nc.vector
            v.memset(u.zeros[:, :], 0.0)
            v.memset(u.fill[:, :], float(NO_NODE << LO_SHIFT)).then_inc(u.fill_ready, 1)
            gnn.vector(ve)
            gat.vector(ve)
            gnn.root(ve)


def placing(nc, t, u, sem, T, M, loads, packed, slot_of_edge, block_of_tile, dinv):
    NCH = T // CH
    in_block, rank_ps, total_ps, hist_ps, misc_ps = u.in_block, u.rank_ps, u.total_ps, u.hist_ps, u.misc_ps
    (keys_clear, edges_in, dv, blocks_ready, counted, nodes_counted, end_row_ready, end_col_done,
     ended_ready, ended_done, pos_ready, sqrt_in, sqrt_out, root_step) = (sem(n) for n in (
         "keys_clear", "edges_in", "dv", "blocks_ready", "counted", "nodes_counted",
         "end_row_ready", "end_col_done", "ended_ready", "ended_done", "pos_ready", "sqrt_in", "sqrt_out", "root_step"))
    lane_ready, lane_used, rank_done, rank_used = ([sem(f"{n}{k}") for k in range(2)] for n in (
        "lane_ready", "lane_used", "rank_done", "rank_used"))
    programs = Tensors()
    programs.keys_clear, programs.edges_in, programs.pos_ready = keys_clear, edges_in, pos_ready
    programs.sqrt_in, programs.sqrt_out = sqrt_in, sqrt_out

    def tensor(pe):
        chunk_counts = hist_ps[:, 0:CH * NB].rearrange("p (a b) -> p a b", b=NB)
        pe.wait_ge(blocks_ready, SET + 1)
        nc.tensor.matmul(chunk_counts, t.zero_b[:, :], in_block[:, 0:CH, :], start=True, stop=False)
        with pe.Fori(0, NCH // 2) as i:
            for k in range(2):
                pe.wait_ge(blocks_ready, SET + i * 2 + k + 1)
                nc.tensor.matmul(chunk_counts, t.ones_b[:, :], in_block[:, bass.ds((i * 2 + k) * CH, CH), :], start=False, stop=False)
        nc.tensor.matmul(chunk_counts, t.zero_b[:, :], in_block[:, 0:CH, :], start=False, stop=True).then_inc(counted, 1)
        pe.wait_ge(end_row_ready, SET + 1)
        nc.tensor.matmul(misc_ps[0:NB, 1, 0:1], u.end_tile[0:1, :], t.ones_f[0:1, 0:1], start=True, stop=True).then_inc(end_col_done, 1)
        pe.wait_ge(ended_ready, SET + 1)
        for h in range(0, M, 512):
            w = min(512, M - h)
            last = nc.tensor.matmul(misc_ps[0:1, h // 512, 0:w], t.ones_f[0:NB, 0:1], u.ended[:, h:h + w], start=True, stop=True)
        last.then_inc(ended_done, 1)
        with pe.Fori(0, NCH // 2) as i:
            for k in range(2):
                pe.wait_ge(rank_used[k], SET + i)
                c0 = i * (2 * CH) + k * CH
                one = lambda j: in_block[:, bass.ds(c0 + j, 1), :]
                nc.tensor.matmul(rank_ps[:, k, 0:CH * NB].rearrange("p (a b) -> p a b", b=NB), t.lower_b[:, :],
                                 in_block[:, bass.ds(c0, CH), :], start=True, stop=False)
                for j in range(CH - 1):
                    nc.tensor.matmul(rank_ps[:, k, (j + 1) * NB:CH * NB].rearrange("p (a b) -> p a b", b=NB),
                                     t.ones_b[:, :], one(j).to_broadcast([P, CH - 1 - j, NB]),
                                     start=False, stop=(j == CH - 2))
                for j in range(CH):
                    last = nc.tensor.matmul(total_ps[:, k, 0:NB], t.ones_b[:, :], one(j).rearrange("p a b -> p (a b)"),
                                            start=(j == 0), stop=(j == CH - 1))
                last.then_inc(rank_done[k], 1)
        if dinv is not None:
            nc.tensor.matmul(hist_ps[:, 0:NB], t.zero_b[:, :], in_block[:, 0, :], start=True, stop=False)
            with pe.Fori(0, NCH // 2) as i:
                for k in range(2):
                    pe.wait_ge(lane_ready[k], SET + i + 1)
                    for j in range(CH):
                        last = nc.tensor.matmul(hist_ps[:, 0:NB], u.at_lane[:, k, j, :],
                                                in_block[:, bass.ds(i * (2 * CH) + (k * CH + j), 1), :].rearrange("p a b -> p (a b)"),
                                                start=False, stop=False)
                    last.then_inc(lane_used[k], 1)
            nc.tensor.matmul(hist_ps[:, 0:NB], t.zero_b[:, :], in_block[:, 0, :], start=False, stop=True).then_inc(nodes_counted, 1)

    def vector(ve):
        v = nc.vector
        ch = Chain(ve, dv)
        key, val, tmp_i, dropped = (x[:, 0:T] for x in (u.key, u.val, u.tmp_i, u.dropped))
        hi_b, lo_b, run, counts_i, ntiles = u.hi_b, u.lo_b, u.run, u.counts_i, u.ntiles
        v.memset(key, OUTSIDE)
        v.memset(val, 0).then_inc(keys_clear, 1)
        ve.wait_ge(edges_in, 16 * loads)
        ch.link(v.tensor_scalar(val, val, float(N - 1), None, ALU.min))
        ch.link(v.tensor_scalar(tmp_i, key, 7, None, ALU.arith_shift_right))
        ch.link(v.tensor_copy(hi_b[:, 0:T], tmp_i))
        ch.link(v.tensor_scalar(tmp_i, key, P - 1, None, ALU.bitwise_and))
        ch.link(v.tensor_copy(lo_b[:, 0:T], tmp_i))
        v.scalar_tensor_tensor(packed, tmp_i, float(1 << LO_SHIFT), val, ALU.mult, ALU.add)
        ch.link(v.tensor_scalar(dropped, key, float(NP), FAR, ALU.is_ge, ALU.mult))
        with ve.Fori(0, NCH // 2) as i:
            for k in range(2):
                chunk = bass.ds((i * 2 + k) * CH, CH)
                v.tensor_tensor(in_block[:, chunk, :], hi_b[:, chunk].unsqueeze(2).to_broadcast([P, CH, NB]),
                                t.iota_b[:, 0:NB].unsqueeze(1).to_broadcast([P, CH, NB]), ALU.is_equal).then_inc(blocks_ready, 1)
        ve.wait_ge(blocks_ready, SET + NCH)
        ve.wait_ge(counted, SET + 1)
        ch.link(v.tensor_reduce(u.counts[:, :], hist_ps[:, 0:CH * NB].rearrange("p (a b) -> p b a", b=NB), AX.X, ALU.add))
        ch.link(v.tensor_copy(counts_i[:, :], u.counts[:, :]))
        ch.link(v.tensor_scalar(counts_i[:, :], counts_i[:, :], float(P - 1), None, ALU.add))
        ch.link(v.tensor_scalar(counts_i[:, :], counts_i[:, :], 7, None, ALU.arith_shift_right))
        ch.link(v.tensor_copy(ntiles[:, :], counts_i[:, :]))
        v.tensor_tensor_scan(u.end_tile[:, :], ntiles[:, :], u.zeros[:, :], 0.0, ALU.add, ALU.add).then_inc(end_row_ready, 1)
        ve.wait_ge(end_row_ready, SET + 1)
        ch.link(v.tensor_tensor(run[:, :], u.end_tile[:, :], ntiles[:, :], ALU.subtract))
        ch.link(v.tensor_scalar(run[:, :], run[:, :], float(P), None, ALU.mult))
        ve.wait_ge(end_col_done, SET + 1)
        ch.link(v.tensor_copy(u.end_col[:, :], misc_ps[0:NB, 1, 0:1]))
        ve.wait_ge(u.iota_ready, SET + 1)
        v.tensor_scalar(u.ended[:, 0:M], u.tile_iota[:, 0:M], u.end_col[:, 0:1], None, ALU.is_ge).then_inc(ended_ready, 1)
        ve.wait_ge(ended_done, SET + 1)
        for h in range(0, M, 512):
            w = min(512, M - h)
            last = v.tensor_scalar(block_of_tile[:, h:h + w], misc_ps[0:1, h // 512, 0:w], float(NB - 1), None, ALU.min)
        ch.link(last)
        with ve.Fori(0, NCH // 2) as i:
            ch.enter(i, 6)
            for k in range(2):
                c0 = i * (2 * CH) + k * CH
                ve.wait_ge(rank_done[k], SET + i + 1)
                ch.link(v.tensor_tensor(u.ranked[:, :, :], rank_ps[:, k, 0:CH * NB].rearrange("p (a b) -> p a b", b=NB),
                                        run[:, :].unsqueeze(1).to_broadcast([P, CH, NB]), ALU.add))
                v.tensor_tensor(run[:, :], run[:, :], total_ps[:, k, 0:NB], ALU.add).then_inc(rank_used[k], 1)
                ve.wait_ge(rank_used[k], SET + i + 1)
                ch.link(v.tensor_tensor(u.picked[:, :, :], u.ranked[:, :, :], in_block[:, bass.ds(c0, CH), :], ALU.mult))
                ch.link(v.tensor_reduce(u.slot[:, :], u.picked[:, :, :], AX.X, ALU.add))
                v.tensor_tensor(slot_of_edge[:, bass.ds(c0, CH)], u.slot[:, :], dropped[:, bass.ds(c0, CH)], ALU.add).then_inc(pos_ready, 1)
        ch.leave(NCH // 2)
        ve.wait_ge(pos_ready, SET + NCH)
        if dinv is not None:
            with ve.Fori(0, NCH // 2) as i:
                for k in range(2):
                    ve.wait_ge(lane_used[k], SET + i)
                    v.tensor_tensor(u.at_lane[:, k, :, :],
                                    lo_b[:, bass.ds(i * (2 * CH) + k * CH, CH)].unsqueeze(2).to_broadcast([P, CH, P]),
                                    t.iota_b[:, :].unsqueeze(1).to_broadcast([P, CH, P]), ALU.is_equal).then_inc(lane_ready[k], 1)
            ve.wait_ge(nodes_counted, SET + 1)
            v.tensor_scalar(u.degree[:, :], hist_ps[:, 0:NB], 1.0, -0.5, ALU.add, ALU.mult)
            v.tensor_scalar(dinv[:, :], hist_ps[:, 0:NB], 1.0, None, ALU.add).then_inc(sqrt_in, 1)
            ve.wait_ge(sqrt_in, SET + 1)

    def root(ve):
        v = nc.vector
        ch = Chain(ve, root_step)
        ve.wait_ge(sqrt_out, SET + 1)
        ch.link(v.reciprocal(dinv[:, :], dinv[:, :]))
        ch.link(v.tensor_tensor(u.degree[:, :], u.degree[:, :], dinv[:, :], ALU.mult))
        ch.link(v.tensor_tensor(u.degree[:, :], u.degree[:, :], dinv[:, :], ALU.mult))
        ch.link(v.scalar_tensor_tensor(dinv[:, :], u.degree[:, :], 1.5, dinv[:, :], ALU.add, ALU.mult))

    programs.tensor, programs.vector, programs.root = tensor, vector, root
    return programs


def unpack_slots(nc, t, tag, M, slots_dram, gather_idx, node_of_slot):
    with ExitStack() as c:
        sb = lambda n, s, d=F32: c.enter_context(nc.sbuf_tensor(tag + n, s, d))
        sem = semaphores(nc, c, tag)
        G = next(g for g in range(-(-M // P), M + 1) if M % g == 0)
        RT = M // G
        BANK = 512 // RT
        rows = sb("rows", [RT, G, P])
        slot_i = sb("slot_i", [P, M], I32)
        ps = c.enter_context(nc.psum_tensor(tag + "turned_ps", [P, -(-G // BANK), 512], F32))
        turned_ps = lambda g: ps[:, g // BANK, g % BANK * RT:(g % BANK + 1) * RT]
        rows_in, turned, dv = sem("rows_in"), sem("turned"), sem("dv")
        nc.all_engine_barrier()
        block = c.enter_context(nc.Block())

        @block.sync
        def _(sp):
            sp.dma_start(rows[:, :, :], slots_dram.rearrange("(g r s) o -> r g (s o)", g=G, s=P)).then_inc(rows_in, 16)

        @block.tensor
        def _(pe):
            pe.wait_ge(rows_in, 16)
            for g in range(G):
                last = nc.tensor.transpose(turned_ps(g), rows[:, g, :], t.ident_f[0:RT, 0:RT])
            last.then_inc(turned, 1)

        @block.vector
        def _(ve):
            v = nc.vector
            ch = Chain(ve, dv)
            v.memset(gather_idx[:, :], 0)
            v.memset(node_of_slot[:, :], float(NO_NODE))
            ve.wait_ge(turned, SET + 1)
            for g in range(G):
                last = v.tensor_copy(slot_i[:, g * RT:(g + 1) * RT], turned_ps(g))
            ch.link(last)
            v.tensor_scalar(gather_idx[:, 0:M], slot_i[:, 0:M], (1 << LO_SHIFT) - 1, None, ALU.bitwise_and)
            ch.link(v.tensor_scalar(slot_i[:, 0:M], slot_i[:, 0:M], LO_SHIFT, None, ALU.arith_shift_right))
            ch.link(v.tensor_copy(node_of_slot[:, 0:M], slot_i[:, 0:M]))


def group_statistics(ve, v, t, ch, src, s, var_ready, std_ready, groups_before):
    settle(ve, t)
    for j in range(GRP):
        last = v.bn_stats(s.st[:, j, :], src[:, j, :])
    ch.link(last)
    settle(ve, t)
    for j in range(GRP):
        last = v.bn_aggr(s.mv[:, j, :], s.st[:, j, :])
    ch.link(last)
    v.tensor_scalar(s.var[:, :], s.mv[:, :, 1], EPS, None, ALU.add).then_inc(var_ready, 1)
    ve.wait_ge(std_ready, SET + groups_before + 1)
    ch.link(v.reciprocal(s.rstd[:, :], s.std[:, :]))
    ch.link(v.scalar_tensor_tensor(s.var[:, :], s.var[:, :], -0.5, s.rstd[:, :], ALU.mult, ALU.mult))
    ch.link(v.tensor_tensor(s.var[:, :], s.var[:, :], s.rstd[:, :], ALU.mult))
    ch.link(v.scalar_tensor_tensor(s.rstd[:, :], s.var[:, :], 1.5, s.rstd[:, :], ALU.add, ALU.mult))


STAT_LINKS = 6


def statistics_tensors(nc, c, tag):
    s = Tensors()
    s.st = c.enter_context(nc.sbuf_tensor(tag + "st", [P, GRP, 6], F32))
    s.mv = c.enter_context(nc.sbuf_tensor(tag + "mv", [P, GRP, 2], F32))
    s.var = c.enter_context(nc.sbuf_tensor(tag + "var", [P, GRP], F32))
    s.std = c.enter_context(nc.sbuf_tensor(tag + "std", [P, GRP], F32))
    s.rstd = c.enter_context(nc.sbuf_tensor(tag + "rstd", [P, GRP], F32))
    return s


def project_input(nc, t, gat_slots, x, W_in, b_in):
    with ExitStack() as c:
        sb = lambda n, s, d=F32: c.enter_context(nc.sbuf_tensor("in_" + n, s, d))
        sem = semaphores(nc, c, "in_")
        w = sb("w", [P, DC, D])
        b = sb("b", [1, D])
        norm = sb("norm", [P, GRP, D])
        normT = sb("normT", [P, GRP, DC, P])
        s = statistics_tensors(nc, c, "in_")
        ps = c.enter_context(nc.psum_tensor("in_ps", [P, 8, 512], F32))
        loaded_first = sem("loaded_first")
        loaded, dv, var_ready, std_ready, norm_ready, turned, turned_sb, made, stored = (
            sem(n) for n in ("loaded", "dv", "var_ready", "std_ready", "norm_ready", "turned", "turned_sb", "made", "stored"))
        half = lambda lo, j: ps[:, lo + j // 2, (j % 2) * D:(j % 2 + 1) * D]
        both = lambda lo: ps[:, lo:lo + 4, :].rearrange("p a b -> p (a b)")[:, 0:GRP * D]
        scatters = attention_scatters(nc, t, c, sem, "in_", gat_slots, 0)
        nc.all_engine_barrier()
        block = c.enter_context(nc.Block())

        @block.gpsimd
        def _(gp):
            scatters(gp, 0, ROUNDS_INPUT)

        @block.sync
        def _(sp):
            blocks = x.rearrange("(b p) d -> p b d", p=P)
            sp.dma_start(t.h[:, 0:GRP, :], blocks[:, 0:GRP, :]).then_inc(loaded_first, 16)
            sp.dma_start(t.h[:, GRP:NB, :], blocks[:, GRP:NB, :]).then_inc(loaded, 16)
            sp.dma_start(w[:, :, :], W_in.rearrange("(c p) d -> p c d", p=P)).then_inc(loaded, 16)
            sp.dma_start(b[:, :], b_in.rearrange("(o d) -> o d", o=1)).then_inc(loaded, 16)

        @block.vector
        def _(ve):
            v = nc.vector
            ch = Chain(ve, dv)

            def normalise(i):
                ch.base, ch.n = i * STAT_LINKS, 0
                xg = t.h[:, bass.ds(i * GRP, GRP), :]
                group_statistics(ve, v, t, ch, xg, s, var_ready, std_ready, i)
                ve.wait_ge(turned, SET + i)
                for j in range(GRP):
                    last = v.tensor_scalar(norm[:, j, :], xg[:, j, :], s.mv[:, j, 0:1], s.rstd[:, j:j + 1],
                                           ALU.subtract, ALU.mult)
                last.then_inc(norm_ready, 1)

            def store(i):
                ve.wait_ge(made, SET + i + 1)
                settle(ve, t, 5)
                v.tensor_copy(t.h[:, bass.ds(i * GRP, GRP), :].rearrange("p a b -> p (a b)"), both(4)).then_inc(stored, 1)

            ve.wait_ge(loaded_first, 16)
            normalise(0)
            ve.wait_ge(loaded, 48)
            normalise(1)
            with ve.Fori(0, NG - 2) as i:
                normalise(i + 2)
                store(i)
            for i in range(NG - 2, NG):
                ve.wait_ge(made, SET + i + 1)
                v.tensor_copy(t.h[:, i * GRP:(i + 1) * GRP, :].rearrange("p a b -> p (a b)"), both(4)).then_inc(stored, 1)

        @block.scalar
        def _(act):
            def root(i):
                act.wait_ge(var_ready, SET + i + 1)
                nc.scalar.activation(s.std[:, :], s.var[:, :], ACT.Sqrt).then_inc(std_ready, 1)

            def turn(i):
                act.wait_ge(turned, SET + i + 1)
                act.wait_ge(made, SET + i)
                nc.scalar.activation(normT[:, :, :, :].rearrange("p a b c -> p (a b c)"), both(0), ACT.Copy).then_inc(turned_sb, 1)

            root(0)
            with act.Fori(0, NG - 1) as i:
                turn(i)
                root(i + 1)
            turn(NG - 1)

        @block.tensor
        def _(pe):
            pe.wait_ge(loaded, 48)
            def turn(i):
                pe.wait_ge(norm_ready, SET + i + 1)
                pe.wait_ge(turned_sb, SET + i)
                for j in range(GRP):
                    for k in range(DC):
                        last = nc.tensor.transpose(half(0, j)[:, k * P:(k + 1) * P], norm[:, j, k * P:(k + 1) * P], t.ident_f[:, :])
                last.then_inc(turned, 1)

            def multiply(i):
                pe.wait_ge(turned_sb, SET + i + 1)
                pe.wait_ge(stored, SET + i)
                for j in range(GRP):
                    for k in range(DC):
                        nc.tensor.matmul(half(4, j), normT[:, j, k, :], w[:, k, :], start=(k == 0), stop=False)
                    last = nc.tensor.matmul(half(4, j), t.ones_f[0:1, :], b[0:1, :], start=False, stop=True)
                last.then_inc(made, 1)

            turn(0)
            with pe.Fori(0, NG - 1) as i:
                turn(i + 1)
                multiply(i)
            multiply(NG - 1)


def gnn_layers(nc, t, gat_slots, Wl, bl, Wg, bg, gamma, beta, table):
    IT = M_GNN // (2 * CH)
    with ExitStack() as c:
        sb = lambda n, s, d=F32: c.enter_context(nc.sbuf_tensor("g_" + n, s, d))
        sem = semaphores(nc, c, "g_")
        two = lambda n: [sem(f"{n}{k}") for k in range(2)]
        msg = t.msg
        wl = sb("wl", [P, DC, D])
        wg = sb("wg", [P, DC, D])
        gam = sb("gam", [P, D])
        bet = sb("bet", [P, D])
        bias_l = sb("bias_l", [1, D])
        bias_g = sb("bias_g", [1, D])
        bias = sb("bias", [1, D])
        mean_row = sb("mean_row", [1, D])
        mean_col = sb("mean_col", [P, DC])
        rows = sb("rows", [P, GRP, D])
        idx_ring = sb("idx_ring", [P, 2, CH], I32)
        got = sb("got", [P, 2, CH, D])
        hot = sb("hot", [P, 2, CH, P])
        gotf = got[:, :, :, :].rearrange("p a b c -> p (a b c)")
        zin = gotf[:, 0:GRP * D].rearrange("p (a b) -> p a b", b=D)
        zT = gotf[:, GRP * D:2 * GRP * D].rearrange("p (a b c) -> p a b c", b=DC, c=P)
        staged = (rows[:, :, :], zin)
        IN_HALF = (NG - NG // 2, NG // 2)
        table_in = two("table_in")
        s = statistics_tensors(nc, c, "g_")
        ps = c.enter_context(nc.psum_tensor("g_ps", [P, 8, 512], F32))
        half = lambda lo, j: ps[:, lo + j // 2, (j % 2) * D:(j % 2 + 1) * D]
        both = lambda lo: ps[:, lo:lo + 4, :].rearrange("p a b -> p (a b)")[:, 0:GRP * D]
        (weights_in, dv, msg_clear, table_rows, sum_done, mean_row_ready, mean_col_done,
         mean_col_ready, ctx_done, bias_ready, zin_ready, turned, turned_sb, made, relu_done, relu_used, var_ready,
         std_ready) = (sem(n) for n in (
             "weights_in", "dv", "msg_clear", "table_rows", "sum_done", "mean_row_ready",
             "mean_col_done", "mean_col_ready", "ctx_done", "bias_ready", "zin_ready", "turned", "turned_sb", "made",
             "relu_done", "relu_used", "var_ready", "std_ready"))
        settled = sem("settled")
        scatters = attention_scatters(nc, t, c, sem, "g_", gat_slots, ROUNDS_INPUT)
        idx_ready, gathered, hot_ready, summed, added = (two(n) for n in ("idx_ready", "gathered", "hot_ready", "summed", "added"))
        nc.all_engine_barrier()
        block = c.enter_context(nc.Block())
        table_v = table.rearrange("(b p) d -> p b d", p=P)

        @block.sync
        def _(sp):
            with sp.Fori(0, LAYERS) as l:
                sp.wait_ge(relu_used, SET + l * NG)
                one = bass.ds(l, 1)
                sp.dma_start(wl[:, :, :], Wl[one, :, :].rearrange("l (c p) d -> p (l c) d", p=P)).then_inc(weights_in, 16)
                sp.dma_start(wg[:, :, :], Wg[one, :, :].rearrange("l (c p) d -> p (l c) d", p=P)).then_inc(weights_in, 16)
                sp.dma_start(gam[:, :], gamma[one, :].to_broadcast([P, D])).then_inc(weights_in, 16)
                sp.dma_start(bet[:, :], beta[one, :].to_broadcast([P, D])).then_inc(weights_in, 16)
                sp.dma_start(bias_l[:, :], bl[one, :]).then_inc(weights_in, 16)
                sp.dma_start(bias_g[:, :], bg[one, :]).then_inc(weights_in, 16)

                def write(i, k):
                    sp.wait_ge(table_rows, SET + l * NG + i + 1)
                    sp.dma_start(table_v[:, bass.ds(i * GRP, GRP), :], staged[k]).then_inc(table_in[k], 16)

                with sp.Fori(0, NG // 2) as i:
                    for k in range(2):
                        write(i * 2 + k, k)
                write(NG - 1, 0)

        @block.gpsimd
        def _(gp):
            SETTLES = 1 + 2 * IT
            with gp.Fori(0, LAYERS) as l:
                for k in range(2):
                    gp.wait_ge(table_in[k], (l + 1) * (16 * IN_HALF[k]))
                settle_gpsimd(gp, t, settled, l * SETTLES)
                with gp.Fori(0, IT) as i:
                    for k in range(2):
                        gp.wait_ge(idx_ready[k], SET + l * (IT + 1) + i + 1)
                        gp.wait_ge(summed[k], SET + l * IT + i)
                        settle_gpsimd(gp, t, settled, l * SETTLES + (i * 2 + k + 1))
                        for j in range(CH):
                            gp.indirect_dma_start(
                                out=got[:, k, j, :], out_offset=None, in_=table,
                                in_offset=bass.IndirectOffsetOnAxis(ap=idx_ring[:, k, j:j + 1], axis=0)).then_inc(gathered[k], 16)
                scatters(gp, ROUNDS_INPUT + l * ROUNDS_LAYER, ROUNDS_LAYER)

        @block.scalar
        def _(act):
            def indices(col, k):
                nc.scalar.activation(idx_ring[:, k, :], t.gnn_idx[:, bass.ds(col, CH)], ACT.Copy).then_inc(idx_ready[k], 1)

            with act.Fori(0, LAYERS) as l:
                act.wait_ge(relu_used, SET + l * NG)

                def scale_group(i, k):
                    for j in range(GRP):
                        b = i * GRP + j
                        last = nc.scalar.activation(staged[k][:, j, :], t.h[:, bass.ds(b, 1), :].rearrange("p a b -> p (a b)"),
                                                    ACT.Copy, scale=t.dinv[:, bass.ds(b, 1)])
                    last.then_inc(table_rows, 1)

                for k in range(2):
                    scale_group(k, k)
                with act.Fori(1, NG // 2) as i:
                    for k in range(2):
                        act.wait_ge(table_in[k], (l * IN_HALF[k] + i) * 16)
                        scale_group(i * 2 + k, k)
                act.wait_ge(table_in[0], (l * IN_HALF[0] + NG // 2) * 16)
                scale_group(NG - 1, 0)
                for k in range(2):
                    indices(k * CH, k)
                with act.Fori(0, IT) as i:
                    for k in range(2):
                        act.wait_ge(gathered[k], (l * IT + i + 1) * (16 * CH))
                        indices((i + 1) * (2 * CH) + k * CH, k)
                with act.Fori(0, NG) as i:
                    g = l * NG + i
                    act.wait_ge(turned, SET + g + 1)
                    nc.scalar.activation(zT.rearrange("p a b c -> p (a b c)"), both(0), ACT.Copy).then_inc(turned_sb, 1)
                    act.wait_ge(made, SET + g + 1)
                    act.wait_ge(relu_used, SET + g)
                    nc.scalar.activation(rows[:, :, :].rearrange("p a b -> p (a b)"), both(4), ACT.Relu).then_inc(relu_done, 1)
                    act.wait_ge(var_ready, SET + g + 1)
                    nc.scalar.activation(s.std[:, :], s.var[:, :], ACT.Sqrt).then_inc(std_ready, 1)

        @block.tensor
        def _(pe):
            with pe.Fori(0, LAYERS) as l:
                pe.wait_ge(relu_used, SET + l * NG)
                flat = lambda b: t.h[:, b, :].rearrange("p a b -> p (a b)")
                nc.tensor.matmul(ps[0:1, 0, 0:D], t.valid[:, 0:1], t.h[:, 0, :], start=True, stop=False)
                with pe.Fori(1, NB - 1) as b:
                    nc.tensor.matmul(ps[0:1, 0, 0:D], t.valid[:, 0:1], flat(bass.ds(b, 1)), start=False, stop=False)
                nc.tensor.matmul(ps[0:1, 0, 0:D], t.valid[:, 1:2], t.h[:, NB - 1, :], start=False, stop=True).then_inc(sum_done, 1)
                pe.wait_ge(mean_row_ready, SET + l + 1)
                for k in range(DC):
                    last = nc.tensor.matmul(ps[:, 1, k:k + 1], mean_row[0:1, k * P:(k + 1) * P], t.ones_f[0:1, 0:1], start=True, stop=True)
                last.then_inc(mean_col_done, 1)
                pe.wait_ge(mean_col_ready, SET + l + 1)
                pe.wait_ge(weights_in, (l + 1) * (16 * 6))
                for k in range(DC):
                    last = nc.tensor.matmul(ps[0:1, 0, 0:D], mean_col[:, k:k + 1], wg[:, k, :], start=(k == 0), stop=(k == DC - 1))
                last.then_inc(ctx_done, 1)
                with pe.Fori(0, IT) as i:
                    for k in range(2):
                        n = l * IT + i
                        pe.wait_ge(gathered[k], (n + 1) * (16 * CH))
                        pe.wait_ge(hot_ready[k], SET + (l * (IT + 1 - k) + i) + 1)
                        pe.wait_ge(added[k], SET + n)
                        for j in range(CH):
                            last = nc.tensor.matmul(half(4 * k, j), hot[:, k, j, :], got[:, k, j, :], start=True, stop=True)
                        last.then_inc(summed[k], 1)
                with pe.Fori(0, NG) as i:
                    g = l * NG + i
                    pe.wait_ge(zin_ready, SET + g + 1)
                    pe.wait_ge(turned_sb, SET + g)
                    for j in range(GRP):
                        for k in range(DC):
                            last = nc.tensor.transpose(half(0, j)[:, k * P:(k + 1) * P], zin[:, j, k * P:(k + 1) * P], t.ident_f[:, :])
                    last.then_inc(turned, 1)
                    pe.wait_ge(turned_sb, SET + g + 1)
                    pe.wait_ge(relu_done, SET + g)
                    for j in range(GRP):
                        for k in range(DC):
                            nc.tensor.matmul(half(4, j), zT[:, j, k, :], wl[:, k, :], start=(k == 0), stop=False)
                        last = nc.tensor.matmul(half(4, j), t.ones_f[0:1, :], bias[0:1, :], start=False, stop=True)
                    last.then_inc(made, 1)

        @block.vector
        def _(ve):
            v = nc.vector
            ch = Chain(ve, dv)
            PER_LAYER = 1 + 2 * (CH - 1) * IT + NG * (STAT_LINKS + 1)

            def build_hot(col, k):
                v.tensor_tensor(hot[:, k, :, :], t.gnn_node[:, bass.ds(col, CH)].unsqueeze(2).to_broadcast([P, CH, P]),
                                t.iota_f[:, :].unsqueeze(1).to_broadcast([P, CH, P]), ALU.is_equal).then_inc(hot_ready[k], 1)

            with ve.Fori(0, LAYERS) as l:
                base = l * PER_LAYER
                ve.wait_ge(sum_done, SET + l + 1)
                v.tensor_scalar(mean_row[:, :], ps[0:1, 0, 0:D], 1.0 / N, None, ALU.mult).then_inc(mean_row_ready, 1)
                ve.wait_ge(mean_col_done, SET + l + 1)
                v.tensor_copy(mean_col[:, :], ps[:, 1, 0:DC]).then_inc(mean_col_ready, 1)
                ve.wait_ge(weights_in, (l + 1) * (16 * 6))
                ve.wait_ge(ctx_done, SET + l + 1)
                ch.base, ch.n = base, 0
                ch.link(v.tensor_tensor(bias[:, :], ps[0:1, 0, 0:D], bias_l[:, :], ALU.add))
                v.tensor_tensor(bias[:, :], bias[:, :], bias_g[:, :], ALU.add).then_inc(bias_ready, 1)
                v.memset(msg[:, :, :], 0.0).then_inc(msg_clear, 1)
                ve.wait_ge(msg_clear, SET + l + 1)
                build_hot(0, 0)
                with ve.Fori(0, IT) as i:
                    ch.base, ch.n = base + 1 + i * (2 * (CH - 1)), 0
                    for k in range(2):
                        other = 1 - k
                        ve.wait_ge(summed[other], SET + l * IT + i + k)
                        build_hot(i * (2 * CH) + (k + 1) * CH, other)
                        at = load_values(nc, ve, t.gnn_block[0:1, bass.ds(i * (2 * CH) + k * CH, CH)], NB - 1)
                        ve.wait_ge(summed[k], SET + l * IT + i + 1)
                        for j in range(CH):
                            m = msg[:, bass.ds(at[j], 1), :].rearrange("p a b -> p (a b)")
                            ins = v.tensor_tensor(m, m, half(4 * k, j), ALU.add)
                            if j < CH - 1:
                                ch.link(ins)
                        ins.then_inc(added[k], 1)
                        ve.wait_ge(added[k], SET + l * IT + i + 1)
                tail = base + 1 + 2 * (CH - 1) * IT

                def make_zin(i):
                    for j in range(GRP):
                        one = bass.ds(i * GRP + j, 1)
                        f = lambda x: x[:, one, :].rearrange("p a b -> p (a b)")
                        last = v.scalar_tensor_tensor(zin[:, j, :], f(msg), t.dinv[:, one], f(t.h), ALU.mult, ALU.add)
                    last.then_inc(zin_ready, 1)

                def norm_group(i):
                    ch.base, ch.n = tail + i * (STAT_LINKS + 1), 0
                    ve.wait_ge(relu_done, SET + l * NG + i + 1)
                    group_statistics(ve, v, t, ch, rows, s, var_ready, std_ready, l * NG + i)
                    for j in range(GRP):
                        last = v.scalar_tensor_tensor(rows[:, j, :], rows[:, j, :], s.mv[:, j, 0:1], gam[:, :], ALU.subtract, ALU.mult)
                    ch.link(last)
                    for j in range(GRP):
                        last = v.scalar_tensor_tensor(t.h[:, bass.ds(i * GRP + j, 1), :].rearrange("p a b -> p (a b)"), rows[:, j, :],
                                                      s.rstd[:, j:j + 1], bet[:, :], ALU.mult, ALU.add)
                    last.then_inc(relu_used, 1)

                make_zin(0)
                with ve.Fori(0, NG - 1) as i:
                    ve.wait_ge(turned, SET + l * NG + i + 1)
                    make_zin(i + 1)
                    norm_group(i)
                norm_group(NG - 1)
                ve.wait_ge(relu_used, SET + (l + 1) * NG)


def attention_rows(nc, t, gat_slots, x, W_gat, att_src, att_dst, x1, table):
    with ExitStack() as c:
        sb = lambda n, s, d=F32: c.enter_context(nc.sbuf_tensor("a_" + n, s, d))
        sem = semaphores(nc, c, "a_")
        xg = sb("xg", [P, GRP, D])
        w = sb("w", [P, DC, HE])
        att = sb("att", [P, 2, HE])
        norm = sb("norm", [P, GRP, D])
        normT = sb("normT", [P, GRP, DC, P])
        prod = sb("prod", [P, 2, GRP, HE])
        rest = sb("rest", [P, GRP, HEADS])
        s = statistics_tensors(nc, c, "a_")
        ps = c.enter_context(nc.psum_tensor("a_ps", [P, 8, 512], F32))
        (weights_in, x_in, x1_ready, x1_out, dv, var_ready, std_ready, norm_ready, turned, turned_sb, made, rows_made,
         table_out) = (sem(n) for n in ("weights_in", "x_in", "x1_ready", "x1_out", "dv", "var_ready", "std_ready",
                                        "norm_ready", "turned", "turned_sb", "made", "rows_made", "table_out"))
        half = lambda lo, j: ps[:, lo + j // 2, (j % 2) * D:(j % 2 + 1) * D]
        both = lambda lo: ps[:, lo:lo + 4, :].rearrange("p a b -> p (a b)")[:, 0:GRP * D]
        before = ROUNDS_INPUT + LAYERS * ROUNDS_LAYER
        split_step = sem("split_step")
        scatters = attention_scatters(nc, t, c, sem, "a_", gat_slots, before)
        nc.all_engine_barrier()
        block = c.enter_context(nc.Block())

        @block.gpsimd
        def _(gp):
            scatters(gp, before, ROUNDS_ROWS)
        group = lambda i: bass.ds(i * GRP, GRP)

        @block.sync
        def _(sp):
            sp.dma_start(w[:, :, :], W_gat.rearrange("(c p) d -> p c d", p=P)).then_inc(weights_in, 16)
            sp.dma_start(att[:, 0, :], att_src.rearrange("(o a) b -> o (a b)", o=1).to_broadcast([P, HE])).then_inc(weights_in, 16)
            sp.dma_start(att[:, 1, :], att_dst.rearrange("(o a) b -> o (a b)", o=1).to_broadcast([P, HE])).then_inc(weights_in, 16)
            with sp.Fori(0, NG) as i:
                sp.wait_ge(x1_ready, SET + i)
                sp.dma_start(xg[:, :, :], x.rearrange("(b p) d -> p b d", p=P)[:, group(i), :]).then_inc(x_in, 16)
            sp.wait_ge(x1_ready, SET + NG)
            sp.dma_start(x1.rearrange("(b p) d -> p b d", p=P), t.h[:, :, :]).then_inc(x1_out, 16)
            sp.wait_ge(rows_made, SET + NG)
            sp.dma_start(table.rearrange("(b p) d -> p b d", p=P), t.rows[:, :, :]).then_inc(table_out, 16)
            sp.wait_ge(x1_out, 16)
            sp.wait_ge(table_out, 16)

        @block.vector
        def _(ve):
            v = nc.vector
            stat, split = Chain(ve, dv), Chain(ve, split_step)

            def normalise(i):
                stat.base, stat.n = i * STAT_LINKS, 0
                h = t.h[:, group(i), :]
                ve.wait_ge(x_in, (i + 1) * 16)
                v.tensor_tensor(h, h, xg[:, :, :], ALU.add).then_inc(x1_ready, 1)
                ve.wait_ge(x1_ready, SET + i + 1)
                group_statistics(ve, v, t, stat, h, s, var_ready, std_ready, i)
                ve.wait_ge(turned, SET + i)
                for j in range(GRP):
                    last = v.tensor_scalar(norm[:, j, :], h[:, j, :], s.mv[:, j, 0:1], s.rstd[:, j:j + 1],
                                           ALU.subtract, ALU.mult)
                last.then_inc(norm_ready, 1)

            def rows_of(i):
                split.base, split.n = i * (2 + 2 * (PARTS - 1)), 0
                ve.wait_ge(made, SET + i + 1)
                hp = ps[:, 4, 0:GRP * HE].rearrange("p (a b) -> p a b", b=HE)
                v.tensor_copy(t.rows[:, group(i), 0:HE], hp)
                for k in range(2):
                    last = v.tensor_tensor(prod[:, k, :, :], hp, att[:, k, :].unsqueeze(1).to_broadcast([P, GRP, HE]), ALU.mult)
                split.link(last)
                per_head = lambda k: prod[:, k, :, :].rearrange("p a (b c) -> p a b c", c=EXPERTS)
                v.tensor_reduce(t.rows[:, group(i), HE:ROW], per_head(0), AX.X, ALU.add)
                split.link(v.tensor_reduce(t.adst[:, group(i), :], per_head(1), AX.X, ALU.add))
                settle(ve, t)
                v.tensor_copy(rest[:, :, :], t.rows[:, group(i), HE:ROW])
                for q in range(PARTS):
                    part = t.rows_b[:, group(i), 2 * ROW + q * HEADS:2 * ROW + (q + 1) * HEADS]
                    ins = v.tensor_copy(part, t.rows[:, group(i), HE:ROW]) if q == 0 else v.tensor_copy(part, rest[:, :, :])
                    if q < PARTS - 1:
                        split.link(ins)
                        split.link(v.tensor_tensor(rest[:, :, :], rest[:, :, :], part, ALU.subtract))
                ins.then_inc(rows_made, 1)

            ve.wait_ge(weights_in, 48)
            normalise(0)
            with ve.Fori(0, NG - 1) as i:
                normalise(i + 1)
                rows_of(i)
            rows_of(NG - 1)

        @block.scalar
        def _(act):
            def root(i):
                act.wait_ge(var_ready, SET + i + 1)
                nc.scalar.activation(s.std[:, :], s.var[:, :], ACT.Sqrt).then_inc(std_ready, 1)

            def turn(i):
                act.wait_ge(turned, SET + i + 1)
                act.wait_ge(made, SET + i)
                nc.scalar.activation(normT[:, :, :, :].rearrange("p a b c -> p (a b c)"), both(0), ACT.Copy).then_inc(turned_sb, 1)
                for k in range(DC):
                    last = nc.scalar.activation(
                        t.yT[:, k, bass.ds(i * (GRP * P), GRP * P)].rearrange("p (a b) -> p a b", b=P),
                        both(0).rearrange("p (a b c) -> p a b c", b=DC, c=P)[:, :, k, :], ACT.Copy)
                last.then_inc(turned_sb, 1)

            root(0)
            with act.Fori(0, NG - 1) as i:
                turn(i)
                root(i + 1)
            turn(NG - 1)

        @block.tensor
        def _(pe):
            pe.wait_ge(weights_in, 48)
            with pe.Fori(0, NG) as i:
                pe.wait_ge(norm_ready, SET + i + 1)
                pe.wait_ge(turned_sb, SET + i * 2)
                for j in range(GRP):
                    for k in range(DC):
                        last = nc.tensor.transpose(half(0, j)[:, k * P:(k + 1) * P], norm[:, j, k * P:(k + 1) * P], t.ident_f[:, :])
                last.then_inc(turned, 1)
                pe.wait_ge(turned_sb, SET + i * 2 + 1)
                pe.wait_ge(rows_made, SET + i)
                for j in range(GRP):
                    for k in range(DC):
                        last = nc.tensor.matmul(ps[:, 4, j * HE:(j + 1) * HE], normT[:, j, k, :], w[:, k, :], start=(k == 0), stop=(k == DC - 1))
                last.then_inc(made, 1)


def attention_max(nc, t, table):
    CM = CH // 2
    CHUNKS = M_GAT // CM
    with ExitStack() as c:
        sb = lambda n, s, d=F32: c.enter_context(nc.sbuf_tensor("m_" + n, s, d))
        sem = semaphores(nc, c, "m_")
        idx_ring = sb("idx_ring", [P, RING, CM], I32)
        got = sb("got", [P, RING, CM, TROW])
        got_b = got[:, :, :, :].rearrange("p a b c -> p (a b c)").bitcast(BF16).rearrange("p (a b c) -> p a b c", a=RING, b=CM)
        not_hot = sb("not_hot", [P, 2, CM, P], BF16)
        tile_top = sb("tile_top", [P, 2, CM, HEADS])
        ps = c.enter_context(nc.psum_tensor("m_ps", [P, 8, 512], F32))
        topped, top_set, settled = sem("topped"), sem("top_set"), sem("settled")
        idx_ready, kept, not_hot_ready, spread, reduced = (
            sem(n) for n in ("idx_ready", "kept", "not_hot_ready", "spread", "reduced"))
        gathered = [sem(f"gathered{k}") for k in range(RING)]
        nc.all_engine_barrier()
        block = c.enter_context(nc.Block())

        @block.gpsimd
        def _(gp):
            with gp.Fori(0, CHUNKS // RING) as i:
                for k in range(RING):
                    n = i * RING + k
                    gp.wait_ge(idx_ready, SET + n + 1)
                    gp.wait_ge(kept, SET + n + 1 - RING)
                    gp.wait_ge(spread, SET + n + 1 - RING)
                    settle_gpsimd(gp, t, settled, n)
                    for j in range(CM):
                        gp.indirect_dma_start(
                            out=got[:, k, j, :], out_offset=None, in_=table,
                            in_offset=bass.IndirectOffsetOnAxis(ap=idx_ring[:, k, j:j + 1], axis=0)).then_inc(gathered[k], 16)

        @block.scalar
        def _(act):
            def indices(n, k):
                nc.scalar.activation(idx_ring[:, k, :], t.gat_idx[:, bass.ds(n * CM, CM)], ACT.Copy).then_inc(idx_ready, 1)

            for k in range(RING):
                indices(k, k)
            with act.Fori(0, CHUNKS // RING) as i:
                for k in range(RING):
                    n = i * RING + k
                    act.wait_ge(gathered[k], (i + 1) * (16 * CM))
                    nc.scalar.activation(t.edge_rows[:, bass.ds(n * CM, CM), :], got[:, k, :, 0:ROW], ACT.Copy).then_inc(kept, 1)
                    indices(n + RING, k)

        @block.tensor
        def _(pe):
            with pe.Fori(0, CHUNKS // RING) as i:
                for k in range(RING):
                    n = i * RING + k
                    pe.wait_ge(gathered[k], (i + 1) * (16 * CM))
                    pe.wait_ge(not_hot_ready, SET + n + 1)
                    pe.wait_ge(reduced, SET + (n - 1) * CM)
                    for j in range(CM):
                        bank = CM * (k % 2) + j
                        nc.tensor.matmul(ps[:, bank, :].rearrange("p (a b) -> p a b", b=P), not_hot[:, k % 2, j, :],
                                         t.neg_ident_b[:, :].unsqueeze(1).to_broadcast([P, HEADS, P]), start=True, stop=False)
                        for h in range(HEADS):
                            for q in range(PARTS):
                                at = 2 * ROW + q * HEADS + h
                                last = nc.tensor.matmul(ps[:, bank, h * P:(h + 1) * P],
                                                        got_b[:, k, j, at:at + 1].to_broadcast([P, P]), t.ident_b[:, :],
                                                        start=False, stop=(h == HEADS - 1 and q == PARTS - 1))
                    last.then_inc(spread, 1)

        @block.vector
        def _(ve):
            v = nc.vector

            def build_not_hot(n, k):
                v.tensor_tensor(not_hot[:, k % 2, :, :], t.gat_node[:, bass.ds(n * CM, CM)].unsqueeze(2).to_broadcast([P, CM, P]),
                                t.iota_b[:, :].unsqueeze(1).to_broadcast([P, CM, P]), ALU.not_equal).then_inc(not_hot_ready, 1)

            def update(n, k, at, j):
                ve.wait_ge(reduced, SET + n * CM + j + 1)
                ve.wait_ge(topped, SET + n * CM + j)
                m = t.top[:, bass.ds(at[j], 1), :].rearrange("p a b -> p (a b)")
                v.tensor_tensor(m, m, tile_top[:, k % 2, j, :], ALU.max).then_inc(topped, 1)

            def step(n, k, has):
                if has(-1):
                    at = load_values(nc, ve, t.gat_block[0:1, bass.ds((n - 1) * CM, CM)], NB - 1)
                if has(1):
                    ve.wait_ge(spread, SET + n)
                    build_not_hot(n + 1, k + 1)
                ve.wait_ge(spread, SET + n + 1)
                ve.wait_ge(topped, SET + (n - 1) * CM)
                for j in range(CM):
                    v.tensor_reduce(tile_top[:, k % 2, j, :], ps[:, CM * (k % 2) + j, :].rearrange("p (b c) -> p b c", c=P),
                                    AX.X, ALU.max).then_inc(reduced, 1)
                    if has(-1):
                        update(n - 1, k - 1, at, j)

            v.tensor_copy(t.top[:, :, :], t.rows[:, :, HE:ROW]).then_inc(top_set, 1)
            ve.wait_ge(top_set, SET + 1)
            build_not_hot(0, 0)
            pipeline(ve, CHUNKS, step)
            at = load_values(nc, ve, t.gat_block[0:1, bass.ds((CHUNKS - 1) * CM, CM)], NB - 1)
            for j in range(CM):
                update(CHUNKS - 1, CHUNKS - 1, at, j)


def attention_sum(nc, t):
    CS = 2 * CH
    CHUNKS = M_GAT // CS
    PER_BANK = 512 // ROW
    assert NB <= 2 * PER_BANK
    with ExitStack() as c:
        sb = lambda n, s, d=F32: c.enter_context(nc.sbuf_tensor("s_" + n, s, d))
        sem = semaphores(nc, c, "s_")
        hot = sb("hot", [P, RING, CS, P], BF16)
        hotT = sb("hotT", [P, 2, CS, P], BF16)
        product = sb("product", [P, 2, CS, ROW])
        left = sb("left", [P, CS, ROW])
        part = sb("part", [P, 2, PARTS, CS, ROW], BF16)
        value = sb("value", [P, 2, CS, 2 * HEADS])
        score = sb("score", [P, 2, CS, HEADS])
        sum_at = t.gat_block
        node_b = sb("node_b", [P, PARTS, 2 * 512], BF16)
        early = hot[:, :, :, :].rearrange("p a b c -> p (a b c)").bitcast(F32)
        rest = early[:, 0:NB * 2 * HEADS].rearrange("p (a b) -> p a b", b=2 * HEADS)
        second_bank = early[0:1, NB * 2 * HEADS:NB * 2 * HEADS + M_GAT]
        ps = c.enter_context(nc.psum_tensor("s_ps", [P, 8, 512], F32))
        (dv, node_ready, at_ready, hot_ready, turned, turned_sb, picked, scored, exp_done, weighted, summed,
         all_summed) = (sem(n) for n in ("dv", "node_ready", "at_ready", "hot_ready", "turned", "turned_sb", "picked",
                                         "scored", "exp_done", "weighted", "summed", "all_summed"))
        flat = lambda a: a.rearrange("p a b -> p (a b)")
        split, split_step = sem("split"), sem("split_step")
        turned_ps = lambda k: flat(ps[:, 2 * (k % 2):2 * (k % 2) + 2, :]).bitcast(BF16)
        picked_ps = lambda k: ps[:, 4 + k % 2, 0:CS * PARTS * 2 * HEADS].rearrange("p (a q b) -> p a q b", q=PARTS, b=2 * HEADS)
        sums_ps = flat(ps[:, 6:8, :])
        rows_of = lambda n: t.edge_rows[:, bass.ds(n * CS, CS), :]
        nc.all_engine_barrier()
        block = c.enter_context(nc.Block())

        @block.vector
        def _(ve):
            v = nc.vector
            ch = Chain(ve, dv)
            adst, emax = t.node[:, :, 0:HEADS], t.node[:, :, HEADS:2 * HEADS]
            v.tensor_copy(adst, t.adst[:, :, :])
            ch.link(v.tensor_tensor(t.top[:, :, :], t.top[:, :, :], t.adst[:, :, :], ALU.add))
            ch.link(v.scalar_tensor_tensor(emax, t.top[:, :, :], 0.2, t.top[:, :, :], ALU.mult, ALU.max))
            ch.link(v.tensor_copy(rest[:, :, :], t.node[:, :, :]))
            for q in range(PARTS):
                for bank in range(2):
                    blocks = min(PER_BANK, NB - bank * PER_BANK)
                    node_part = node_b[:, q, bank * 512:bank * 512 + blocks * ROW].rearrange("p (a b) -> p a b", b=ROW)[:, :, 0:2 * HEADS]
                    node_left = rest[:, bank * PER_BANK:bank * PER_BANK + blocks, :]
                    last = v.tensor_copy(node_part, node_left)
                    if q < PARTS - 1:
                        ch.link(last)
                        ch.link(v.tensor_tensor(node_left, node_left, node_part, ALU.subtract))
            last.then_inc(node_ready, 1)
            ch.link(v.tensor_scalar(second_bank, t.gat_block[:, :], float(PER_BANK), float(512 - PER_BANK * ROW), ALU.is_ge, ALU.mult))
            v.scalar_tensor_tensor(sum_at[:, :], t.gat_block[:, :], float(ROW), second_bank, ALU.mult, ALU.add).then_inc(at_ready, 1)
            ve.wait_ge(at_ready, SET + 1)
            before = ch.n

            def build_hot(n, k):
                v.tensor_tensor(hot[:, k % RING, :, :], t.gat_node[:, bass.ds(n * CS, CS)].unsqueeze(2).to_broadcast([P, CS, P]),
                                t.iota_b[:, :].unsqueeze(1).to_broadcast([P, CS, P]), ALU.is_equal).then_inc(hot_ready, 1)

            def weight(n, k):
                ve.wait_ge(exp_done, SET + n + 1)
                heads = lambda a: a[:, :, 0:HE].rearrange("p a (b c) -> p a b c", c=EXPERTS)
                one = product[:, k % 2, :, :]
                v.tensor_tensor(heads(one), heads(rows_of(n)), one[:, :, HE:ROW].unsqueeze(3).to_broadcast([P, CS, HEADS, EXPERTS]),
                                ALU.mult).then_inc(weighted, 1)

            def step(n, k, has):
                if has(-1):
                    weight(n - 1, k - 1)
                if has(2):
                    ve.wait_ge(summed, SET + n - 1)
                    build_hot(n + 2, k + 2)
                ve.wait_ge(picked, SET + n + 1)
                ch.base, ch.n = before + n * 3, 0
                two = value[:, k % 2, :, :]
                one = score[:, k % 2, :, :]
                ch.link(v.tensor_reduce(two, picked_ps(k).rearrange("p a q b -> p a b q"), AX.X, ALU.add))
                ch.link(v.tensor_tensor(one, two[:, :, 0:HEADS], rows_of(n)[:, :, HE:ROW], ALU.add))
                ch.link(v.scalar_tensor_tensor(flat(one), flat(one), 0.2, flat(one), ALU.mult, ALU.max))
                v.tensor_tensor(rows_of(n)[:, :, HE:ROW], one, two[:, :, HEADS:2 * HEADS], ALU.subtract).then_inc(scored, 1)

            build_hot(0, 0)
            build_hot(1, 1)
            pipeline(ve, CHUNKS, step)
            weight(CHUNKS - 1, CHUNKS - 1)
            ve.wait_ge(all_summed, SET + 1)
            for q in range(2):
                blocks = min(PER_BANK, NB - q * PER_BANK)
                v.tensor_copy(flat(t.sums[:, q * PER_BANK:q * PER_BANK + blocks, :]), ps[:, 6 + q, 0:blocks * ROW])

        @block.scalar
        def _(act):
            def turn(n, k):
                act.wait_ge(turned, SET + n + 1)
                act.wait_ge(picked, SET + n - 1)
                nc.scalar.activation(hotT[:, k % 2, :, :].rearrange("p a b -> p (a b)"), turned_ps(k), ACT.Copy).then_inc(turned_sb, 1)

            def step(n, k, has):
                if has(1):
                    turn(n + 1, k + 1)
                act.wait_ge(scored, SET + n + 1)
                act.wait_ge(split, SET + n - 1)
                nc.scalar.activation(product[:, k % 2, :, HE:ROW], rows_of(n)[:, :, HE:ROW], ACT.Exp).then_inc(exp_done, 1)

            turn(0, 0)
            pipeline(act, CHUNKS, step)

        @block.gpsimd
        def _(gp):
            ch = Chain(gp, split_step)
            zeros = t.zero_b[:, 0:ROW].unsqueeze(1).to_broadcast([P, CS, ROW])

            def step(n, k, has):
                ch.base, ch.n = n * 3, 0
                gp.wait_ge(weighted, SET + n + 1)
                gp.wait_ge(summed, SET + n - 1)
                whole = product[:, k % 2, :, :]
                ch.link(gp.tensor_tensor(part[:, k % 2, 0, :, :], whole, zeros, ALU.add))
                ch.link(gp.tensor_tensor(left[:, :, :], whole, part[:, k % 2, 0, :, :], ALU.subtract))
                ch.link(gp.tensor_tensor(part[:, k % 2, 1, :, :], left[:, :, :], zeros, ALU.add))
                gp.tensor_tensor(part[:, k % 2, 2, :, :], left[:, :, :], part[:, k % 2, 1, :, :], ALU.subtract).then_inc(split, 1)
                gp.wait_ge(split, SET + n + 1)

            pipeline(gp, CHUNKS, step)

        @block.tensor
        def _(pe):
            def turn(n, k):
                pe.wait_ge(hot_ready, SET + n + 1)
                pe.wait_ge(turned_sb, SET + n - 1)
                for j in range(CS):
                    last = nc.tensor.transpose(turned_ps(k)[:, j * P:(j + 1) * P], hot[:, k % RING, j, :], t.ident_b[:, :])
                last.then_inc(turned, 1)

            def pick(n, k):
                at = load_values(nc, pe, sum_at[0:1, bass.ds(n * CS, CS)], LAST_AT)
                pe.wait_ge(turned_sb, SET + n + 1)
                pe.wait_ge(scored, SET + n - 1)
                for j in range(CS):
                    last = nc.tensor.matmul(picked_ps(k)[:, j, :, :], hotT[:, k % 2, j, :], node_b[:, :, bass.ds(at[j], 2 * HEADS)], start=True, stop=True)
                last.then_inc(picked, 1)

            def add_up(n, k):
                at = load_values(nc, pe, sum_at[0:1, bass.ds(n * CS, CS)], LAST_AT)
                pe.wait_ge(split, SET + n + 1)
                for j in range(CS):
                    for q in range(PARTS):
                        last = nc.tensor.matmul(sums_ps[:, bass.ds(at[j], ROW)], hot[:, k % RING, j, :],
                                                part[:, k % 2, q, j, :], start=False, stop=False)
                last.then_inc(summed, 1)

            def step(n, k, has):
                if has(-2):
                    add_up(n - 2, k - 2)
                if has(1):
                    turn(n + 1, k + 1)
                pick(n, k)

            LAST_AT = 512 + (NB - PER_BANK - 1) * ROW
            pe.wait_ge(node_ready, SET + 1)
            pe.wait_ge(at_ready, SET + 1)
            for q in range(2):
                nc.tensor.matmul(ps[:, 6 + q, :].rearrange("p (a b) -> p a b", b=P), t.zero_b[:, :], t.ones_b[:, :].unsqueeze(1).to_broadcast([P, 4, P]), start=True, stop=False)
            turn(0, 0)
            pipeline(pe, CHUNKS, step)
            for n in range(CHUNKS - 2, CHUNKS):
                add_up(n, n)
            for q in range(2):
                last = nc.tensor.matmul(ps[:, 6 + q, :].rearrange("p (a b) -> p a b", b=P), t.zero_b[:, :], t.ones_b[:, :].unsqueeze(1).to_broadcast([P, 4, P]), start=False, stop=True)
            last.then_inc(all_summed, 1)


def attention_gates(nc, t, space, b_gat, ln_gamma, ln_beta, W1, W2):
    with ExitStack() as c:
        sb = lambda n, s, d=F32: c.enter_context(nc.sbuf_tensor("w_" + n, s, d))
        sem = semaphores(nc, c, "w_")
        par = sb("par", [P, 3, HE])
        own = sb("own", [P, NB, HEADS])
        den = sb("den", [P, NB, HEADS])
        agg = sb("agg", [P, NB, HE])
        sq = sb("sq", [P, NB, HE])
        stat = sb("stat", [P, 3, NB])
        std = sb("std", [P, NB])
        score = sb("score", [P, NB, EXPERTS])
        ahead = sb("ahead", [P, NB])
        rank = sb("rank", [P, NB, EXPERTS])
        prob = sb("prob", [P, NB, EXPERTS])
        weights_in = sem("weights_in")
        par_in, dv, own_ready, own_exp, var_ready, std_ready, prob_ready, prob_exp = (
            sem(n) for n in ("par_in", "dv", "own_ready", "own_exp", "var_ready", "std_ready", "prob_ready", "prob_exp"))
        flat = lambda a: a.rearrange("p a b -> p (a b)")
        nc.all_engine_barrier()
        block = c.enter_context(nc.Block())

        @block.sync
        def _(sp):
            for k, a in enumerate((b_gat, ln_gamma, ln_beta)):
                sp.dma_start(par[:, k, :], a.rearrange("(o d) -> o d", o=1).to_broadcast([P, HE])).then_inc(par_in, 16)
            w1, w2, _ = expert_weights(space)
            sp.dma_start(w1[:, :, :, :].rearrange("p e c h -> p (e c) h"), W1.rearrange("e (c p) h -> p (e c) h", p=P)).then_inc(weights_in, 16)
            sp.dma_start(w2[:, :, :, :].rearrange("p e m d -> p (e m) d"), W2.rearrange("e (m p) d -> p (e m) d", p=P)).then_inc(weights_in, 16)
            sp.wait_ge(weights_in, 32)

        @block.scalar
        def _(act):
            act.wait_ge(own_ready, SET + 1)
            nc.scalar.activation(flat(own[:, :, :]), flat(own[:, :, :]), ACT.Exp).then_inc(own_exp, 1)
            act.wait_ge(var_ready, SET + 1)
            nc.scalar.activation(std[:, :], stat[:, 1, :], ACT.Sqrt).then_inc(std_ready, 1)
            act.wait_ge(prob_ready, SET + 1)
            nc.scalar.activation(flat(prob[:, :, :]), flat(prob[:, :, :]), ACT.Exp).then_inc(prob_exp, 1)

        @block.vector
        def _(ve):
            v = nc.vector
            ch = Chain(ve, dv)
            link = ch.link
            heads = lambda a: a.rearrange("p a (b c) -> p a b c", c=EXPERTS)
            per_head = lambda a: a.unsqueeze(3).to_broadcast([P, NB, HEADS, EXPERTS])
            spread = lambda a, n: a.unsqueeze(2).to_broadcast([P, NB, n])
            param = lambda k: par[:, k, :].unsqueeze(1).to_broadcast([P, NB, HE])
            link(v.tensor_tensor(own[:, :, :], t.rows[:, :, HE:ROW], t.adst[:, :, :], ALU.add))
            link(v.scalar_tensor_tensor(flat(own[:, :, :]), flat(own[:, :, :]), 0.2, flat(own[:, :, :]), ALU.mult, ALU.max))
            v.tensor_tensor(own[:, :, :], own[:, :, :], t.node[:, :, HEADS:2 * HEADS], ALU.subtract).then_inc(own_ready, 1)
            ve.wait_ge(own_ready, SET + 1)
            ve.wait_ge(own_exp, SET + 1)
            link(v.tensor_tensor(den[:, :, :], t.sums[:, :, HE:ROW], own[:, :, :], ALU.add))
            link(v.tensor_scalar(flat(den[:, :, :]), flat(den[:, :, :]), 1e-16, None, ALU.add))
            link(v.reciprocal(flat(den[:, :, :]), flat(den[:, :, :])))
            link(v.tensor_tensor(heads(agg[:, :, :]), heads(t.rows[:, :, 0:HE]), per_head(own[:, :, :]), ALU.mult))
            link(v.tensor_tensor(agg[:, :, :], agg[:, :, :], t.sums[:, :, 0:HE], ALU.add))
            link(v.tensor_tensor(heads(agg[:, :, :]), heads(agg[:, :, :]), per_head(den[:, :, :]), ALU.mult))
            ve.wait_ge(par_in, 48)
            link(v.tensor_tensor(agg[:, :, :], agg[:, :, :], param(0), ALU.add))
            link(v.tensor_reduce(stat[:, 0, :], agg[:, :, :], AX.X, ALU.add))
            link(v.tensor_scalar(stat[:, 0, :], stat[:, 0, :], 1.0 / HE, None, ALU.mult))
            link(v.tensor_tensor(agg[:, :, :], agg[:, :, :], spread(stat[:, 0, :], HE), ALU.subtract))
            link(v.tensor_tensor(sq[:, :, :], agg[:, :, :], agg[:, :, :], ALU.mult))
            link(v.tensor_reduce(stat[:, 1, :], sq[:, :, :], AX.X, ALU.add))
            v.tensor_scalar(stat[:, 1, :], stat[:, 1, :], 1.0 / HE, EPS, ALU.mult, ALU.add).then_inc(var_ready, 1)
            ve.wait_ge(var_ready, SET + 1)
            ve.wait_ge(std_ready, SET + 1)
            link(v.reciprocal(stat[:, 2, :], std[:, :]))
            link(v.scalar_tensor_tensor(stat[:, 1, :], stat[:, 1, :], -0.5, stat[:, 2, :], ALU.mult, ALU.mult))
            link(v.tensor_tensor(stat[:, 1, :], stat[:, 1, :], stat[:, 2, :], ALU.mult))
            link(v.scalar_tensor_tensor(stat[:, 2, :], stat[:, 1, :], 1.5, stat[:, 2, :], ALU.add, ALU.mult))
            link(v.tensor_tensor(agg[:, :, :], agg[:, :, :], spread(stat[:, 2, :], HE), ALU.mult))
            link(v.tensor_tensor(agg[:, :, :], agg[:, :, :], param(1), ALU.mult))
            link(v.tensor_tensor(agg[:, :, :], agg[:, :, :], param(2), ALU.add))
            link(v.tensor_reduce(score[:, :, :], agg[:, :, :].rearrange("p a (b c) -> p a c b", c=EXPERTS), AX.X, ALU.add))
            link(v.tensor_scalar(flat(score[:, :, :]), flat(score[:, :, :]), 1.0 / HEADS, None, ALU.mult))
            link(v.memset(rank[:, :, :], 0.0))
            for a in range(EXPERTS):
                for b in range(EXPERTS):
                    if a != b:
                        link(v.tensor_tensor(ahead[:, :], score[:, :, b], score[:, :, a], ALU.is_ge if b < a else ALU.is_gt))
                        link(v.tensor_tensor(rank[:, :, a], rank[:, :, a], ahead[:, :], ALU.add))
            link(v.tensor_reduce(ahead[:, :], score[:, :, :], AX.X, ALU.max))
            link(v.tensor_scalar(flat(rank[:, :, :]), flat(rank[:, :, :]), float(TOPK), None, ALU.is_lt))
            v.tensor_tensor(prob[:, :, :], score[:, :, :], spread(ahead[:, :], EXPERTS), ALU.subtract).then_inc(prob_ready, 1)
            ve.wait_ge(prob_ready, SET + 1)
            ve.wait_ge(prob_exp, SET + 1)
            link(v.tensor_tensor(prob[:, :, :], prob[:, :, :], rank[:, :, :], ALU.mult))
            link(v.tensor_reduce(ahead[:, :], prob[:, :, :], AX.X, ALU.add))
            link(v.reciprocal(ahead[:, :], ahead[:, :]))
            link(v.tensor_tensor(t.gate[:, :, :], prob[:, :, :], spread(ahead[:, :], EXPERTS), ALU.mult))


def expert_weights(space):
    n1, n2 = EXPERTS * DC * HID, EXPERTS * HM * D
    return (space[:, 0:n1].rearrange("p (e c h) -> p e c h", e=EXPERTS, c=DC),
            space[:, n1:n1 + n2].rearrange("p (e m d) -> p e m d", e=EXPERTS, m=HM), n1 + n2)


def experts(nc, t, space, b1, b2, x1, out):
    TOK = GRP * P
    HALF = TOK // 2
    with ExitStack() as c:
        sb = lambda n, s, d=F32: c.enter_context(nc.sbuf_tensor("e_" + n, s, d))
        sem = semaphores(nc, c, "e_")
        two = lambda n: [sem(f"{n}{k}") for k in range(2)]
        n3, n4 = 2 * HM * TOK, GRP * D
        w1, w2, front = expert_weights(space)
        hidden = space[:, front:front + n3].rearrange("p (a m t) -> p a m t", a=2, m=HM)
        acc = space[:, front + n3:front + n3 + n4].rearrange("p (a b) -> p a b", b=D)
        b1t = sb("b1", [P, EXPERTS, HM])
        b2t = sb("b2", [EXPERTS, D])
        gate = sb("gate", [P, GRP, EXPERTS])
        gateT = sb("gateT", [EXPERTS, TOK])
        ps = c.enter_context(nc.psum_tensor("e_ps", [P, 8, 512], F32))
        weights_in, acc_in, acc_out, dv, gate_ready, gateT_done, gateT_ready, bias_done, y_done, y_added = (
            sem(n) for n in ("weights_in", "acc_in", "acc_out", "dv", "gate_ready", "gateT_done", "gateT_ready", "bias_done", "y_done", "y_added"))
        hid_done, hid_used = two("hid_done"), two("hid_used")
        y_ps = lambda j: ps[:, 4 + j // 2, (j % 2) * D:(j % 2 + 1) * D]
        gT_ps = lambda j: ps[0:EXPERTS, 4 + j // 4, (j % 4) * P:(j % 4 + 1) * P]
        YG = 1 + EXPERTS
        nc.all_engine_barrier()
        block = c.enter_context(nc.Block())

        @block.sync
        def _(sp):
            with nc.allow_non_contiguous_dma(reason="2048 biases, once"):
                sp.dma_start(b1t[:, :, :].rearrange("p e m -> p (e m)"), b1.rearrange("e (m p) -> p (e m)", p=P)).then_inc(weights_in, 16)
            sp.dma_start(b2t[:, :], b2).then_inc(weights_in, 16)
            group = lambda a, i: a.rearrange("(b p) d -> p b d", p=P)[:, bass.ds(i * GRP, GRP), :]
            sp.dma_start(acc[:, :, :], group(x1, 0)).then_inc(acc_in, 16)
            with sp.Fori(0, NG - 1) as i:
                sp.wait_ge(y_added, SET + (i + 1) * YG)
                sp.dma_start(group(out, i), acc[:, :, :]).then_inc(acc_out, 16)
                sp.wait_ge(acc_out, (i + 1) * 16)
                sp.dma_start(acc[:, :, :], group(x1, i + 1)).then_inc(acc_in, 16)
            sp.wait_ge(y_added, SET + NG * YG)
            sp.dma_start(group(out, NG - 1), acc[:, :, :]).then_inc(acc_out, 16)
            sp.wait_ge(acc_out, NG * 16)

        @block.tensor
        def _(pe):
            pe.wait_ge(weights_in, 32)
            with pe.Fori(0, NG) as i:
                pe.wait_ge(gate_ready, SET + i + 1)
                pe.wait_ge(y_added, SET + i * YG)
                for j in range(GRP):
                    last = nc.tensor.transpose(gT_ps(j), gate[:, j, :], t.ident_f[:, :])
                last.then_inc(gateT_done, 1)
                pe.wait_ge(gateT_ready, SET + i + 1)
                for j in range(GRP):
                    last = nc.tensor.matmul(y_ps(j), gateT[:, j * P:(j + 1) * P], b2t[:, :], start=True, stop=True)
                last.then_inc(bias_done, 1)

                def up(e):
                    for m in range(HM):
                        pe.wait_ge(hid_used[m % 2], SET + (i * EXPERTS + e) * (HM // 2) + m // 2)
                        for k in range(DC):
                            for f in range(2):
                                last = nc.tensor.matmul(ps[:, 2 * (m % 2) + f, 0:HALF], w1[:, e, k, m * P:(m + 1) * P],
                                                        t.yT[:, k, bass.ds(i * TOK + f * HALF, HALF)], start=(k == 0), stop=(k == DC - 1))
                        last.then_inc(hid_done[m % 2], 1)

                def down(e):
                    for q in range(2):
                        pe.wait_ge(hid_used[q], SET + (i * EXPERTS + e + 1) * (HM // 2))
                    pe.wait_ge(y_added, SET + i * YG + e + 1)
                    for j in range(GRP):
                        for m in range(HM):
                            last = nc.tensor.matmul(y_ps(j), hidden[:, e % 2, m, j * P:(j + 1) * P], w2[:, e, m, :], start=(m == 0), stop=(m == HM - 1))
                    last.then_inc(y_done, 1)

                up(0)
                for e in range(1, EXPERTS):
                    up(e)
                    down(e - 1)
                down(EXPERTS - 1)

        @block.scalar
        def _(act):
            act.wait_ge(weights_in, 32)
            with act.Fori(0, NG) as i:
                for e in range(EXPERTS):
                    if e >= 2:
                        act.wait_ge(y_done, SET + i * EXPERTS + e - 1)
                    else:
                        act.wait_ge(y_done, SET + i * EXPERTS)
                    for m in range(HM):
                        act.wait_ge(hid_done[m % 2], SET + (i * EXPERTS + e) * (HM // 2) + m // 2 + 1)
                        nc.scalar.activation(hidden[:, e % 2, m, :].rearrange("p (a b) -> p a b", a=2),
                                             ps[:, 2 * (m % 2):2 * (m % 2) + 2, 0:HALF], ACT.Gelu,
                                             bias=b1t[:, e, m:m + 1]).then_inc(hid_used[m % 2], 1)

        @block.vector
        def _(ve):
            v = nc.vector
            ch = Chain(ve, dv)
            with ve.Fori(0, NG) as i:
                ve.wait_ge(gateT_done, SET + i)
                ve.wait_ge(y_added, SET + i * YG)
                v.tensor_copy(gate[:, :, :], t.gate[:, bass.ds(i * GRP, GRP), :]).then_inc(gate_ready, 1)
                ve.wait_ge(gateT_done, SET + i + 1)
                ve.wait_ge(bias_done, SET + i)
                for q in range(2):
                    w = min(4, GRP - 4 * q)
                    last = v.tensor_copy(gateT[:, 4 * q * P:(4 * q + w) * P], ps[0:EXPERTS, 4 + q, 0:w * P])
                last.then_inc(gateT_ready, 1)
                ve.wait_ge(acc_in, (i + 1) * 16)
                ve.wait_ge(bias_done, SET + i + 1)
                for j in range(GRP):
                    last = v.tensor_tensor(acc[:, j, :], acc[:, j, :], y_ps(j), ALU.add)
                last.then_inc(y_added, 1)
                for e in range(EXPERTS):
                    ve.wait_ge(y_added, SET + i * YG + e + 1)
                    ve.wait_ge(y_done, SET + i * EXPERTS + e + 1)
                    for j in range(GRP):
                        last = v.scalar_tensor_tensor(acc[:, j, :], y_ps(j), gate[:, j, e:e + 1], acc[:, j, :], ALU.mult, ALU.add)
                    last.then_inc(y_added, 1)


def build(nc, a, out):
    t = Tensors()
    t.nc = nc
    dram = lambda n, s: nc.dram_tensor(n, s, F32, kind="Internal").ap()
    gnn_slots = dram("gnn_slots", [M_GNN * P, 1])
    gat_slots = dram("gat_slots", [M_GAT * P, 1])
    gnn_table = dram("gnn_table", [NP, D])
    gat_table = dram("gat_table", [NP, TROW])
    x1 = dram("x1", [NP, D])
    with ExitStack() as c:
        sb = lambda n, s, d=F32: c.enter_context(nc.sbuf_tensor(n, s, d))
        t.iota_f = sb("iota_f", [P, P])
        t.iota_b = sb("iota_b", [P, P], BF16)
        t.ident_f = sb("ident_f", [P, P])
        t.ident_b = sb("ident_b", [P, P], BF16)
        t.neg_ident_b = sb("neg_ident_b", [P, P], BF16)
        t.ones_f = sb("ones_f", [P, P])
        t.ones_b = sb("ones_b", [P, P], BF16)
        t.zero_b = sb("zero_b", [P, P], BF16)
        t.lower_b = sb("lower_b", [P, P], BF16)
        t.valid = sb("valid", [P, 2])
        t.spare = sb("spare", [P, 6])
        t.dinv = sb("dinv", [P, NB])
        t.gnn_idx = sb("gnn_idx", [P, M_GNN + 2 * CH], I32)
        t.gnn_node = sb("gnn_node", [P, M_GNN + CH], BF16)
        t.gnn_block = sb("gnn_block", [1, M_GNN], I32)
        t.gat_idx = sb("gat_idx", [P, M_GAT + 2 * CH], I32)
        t.gat_node = sb("gat_node", [P, M_GAT], BF16)
        t.gat_block = sb("gat_block", [1, M_GAT], I32)
        build_constants(nc, t)

        def load_gnn(sp, key, val, done):
            whole, rest = divmod(E_GNN, T_GNN)
            for tile, arr in ((key, a["src"]), (val, a["dst"])):
                sp.dma_start(tile[0:whole, 0:T_GNN], arr[0:whole * T_GNN].rearrange("(p t) -> p t", t=T_GNN)).then_inc(done, 16)
                sp.dma_start(tile[whole:whole + 1, 0:rest], arr[whole * T_GNN:E_GNN].rearrange("(p t) -> p t", p=1)).then_inc(done, 16)

        def load_gat(sp, key, val, done):
            for tile, row in ((key, 1), (val, 0)):
                sp.dma_start(tile[:, :], a["L0_ffn_edge_index"][row, :].rearrange("(p t) -> p t", p=P)).then_inc(done, 16)

        region = sb("region", [P, REGION])
        first, second = region[:, 0:NB * D], region[:, NB * D:REGION]
        t.msg = first.rearrange("p (a b) -> p a b", b=D)
        t.yT = first.rearrange("p (a b) -> p a b", b=NP)
        t.h = second[:, 0:NB * D].rearrange("p (a b) -> p a b", b=D)
        t.edge_rows = second.rearrange("p (a b) -> p a b", b=ROW)
        t.gat_packed = region[:, REGION - GAT_KEPT:REGION - T_GAT]
        t.gat_pos = region[:, REGION - T_GAT:REGION].bitcast(I32)
        sort_edges(nc, t, region, load_gnn, load_gat, gnn_slots, gat_slots)
        unpack_slots(nc, t, "ugnn_", M_GNN, gnn_slots, t.gnn_idx, t.gnn_node)
        project_input(nc, t, gat_slots, a["x"], a["L0_gnn_W_in"], a["L0_gnn_b_in"])
        gnn_layers(nc, t, gat_slots, a["L0_gnn_Wl"], a["L0_gnn_bl"], a["L0_gnn_Wg"], a["L0_gnn_bg"],
                   a["L0_gnn_gamma"], a["L0_gnn_beta"], gnn_table)
        t.rows = sb("rows", [P, NB, TROW])
        t.adst = sb("adst", [P, NB, HEADS])
        t.top = sb("top", [P, NB, HEADS])
        t.node = sb("node", [P, NB, 2 * HEADS])
        t.sums = sb("sums", [P, NB, ROW])
        t.gate = sb("gate", [P, NB, EXPERTS])
        t.rows_b = t.rows[:, :, :].bitcast(BF16)
        attention_rows(nc, t, gat_slots, a["x"], a["L0_ffn_W_gat"], a["L0_ffn_att_src"], a["L0_ffn_att_dst"], x1, gat_table)
        unpack_slots(nc, t, "ugat_", M_GAT, gat_slots, t.gat_idx, t.gat_node)
        attention_max(nc, t, gat_table)
        attention_sum(nc, t)
        attention_gates(nc, t, second, a["L0_ffn_b_gat"], a["L0_ffn_ln_gamma"], a["L0_ffn_ln_beta"],
                        a["L0_ffn_W1"], a["L0_ffn_W2"])
        experts(nc, t, second, a["L0_ffn_b1"], a["L0_ffn_b2"], x1, out)


def kernel(**inputs):
    import numpy as np
    import concourse.bacc as bacc
    from concourse.bass_utils import run_bass_kernel_spmd

    nc = bacc.Bacc("TRN2", target_bir_lowering=False, num_devices=1)
    arrays, aps = {}, {}
    for name, value in inputs.items():
        value = np.ascontiguousarray(value)
        if name == "x":
            value = np.pad(value, ((0, NP - N), (0, 0)))
        arrays["in_" + name] = value
        aps[name] = nc.dram_tensor("in_" + name, value.shape, mybir.dt.from_np(value.dtype), kind="ExternalInput").ap()
    out = nc.dram_tensor("out", [NP, D], F32, kind="ExternalOutput").ap()
    build(nc, aps, out)
    result = run_bass_kernel_spmd(nc, [arrays], core_ids=[0])
    return result.results[0]["out"][0:N]
```
